# Optimizing a Trainium2 kernel written in Bass

```python
import numpy as np
import jax
import jax.numpy as jnp

def _softmax(x, axis=-1):
    return jax.nn.softmax(x, axis=axis)

def _gelu(x):
    return jax.nn.gelu(x, approximate=True)

def _silu(x):
    return jax.nn.silu(x)

def _sigmoid(x):
    return jax.nn.sigmoid(x)

def _layernorm(x, axis=-1, eps=1e-05):
    m = jnp.mean(x, axis=axis, keepdims=True)
    v = jnp.var(x, axis=axis, keepdims=True)
    return (x - m) / jnp.sqrt(v + eps)

def _scatter_add(tgt, idx, src, axis=0):
    return tgt.at[idx].add(src)

def _segment_sum(src, seg, n):
    return jax.ops.segment_sum(src, seg, n)
kernel_name = 'mk_sandwich_d1_jaxref_r2_cdaef4'

def setup_inputs(seed: int=0):
    np.random.seed(seed)
    _w = jnp.asarray

    def _L0_attn_setup():
        import jax, jax.numpy as jnp
        import numpy as np
        N_LAYERS = 2
        D_MODEL = 512
        EXPAND = 2
        D_INNER = EXPAND * D_MODEL
        D_STATE = 16
        D_CONV = 4
        DT_RANK = (D_MODEL + 15) // 16
        BATCH = 2
        SEQ = 512

        def _mamba_block(x, W_in, w_c, b_c, W_x, W_dt, b_dt, A_log, Dp, W_out):
            xz = jnp.einsum('bld,ed->ble', x, W_in)
            xc, z = jnp.split(xz, 2, axis=-1)
            xc = xc.transpose(0, 2, 1)
            xc = jax.lax.conv_general_dilated(xc, w_c, window_strides=(1,), padding=[(D_CONV - 1, 0)], dimension_numbers=('NCH', 'OIH', 'NCH'), feature_group_count=D_INNER) + b_c[None, :, None]
            u = jax.nn.silu(xc).transpose(0, 2, 1)
            x_dbl = jnp.einsum('bld,ed->ble', u, W_x)
            dt, Bm, Cm = jnp.split(x_dbl, [DT_RANK, DT_RANK + D_STATE], axis=-1)
            delta = jax.nn.softplus(jnp.einsum('blr,dr->bld', dt, W_dt) + b_dt)
            A = -jnp.exp(A_log)
            dA = jnp.exp(jnp.einsum('bld,dn->bldn', delta, A))
            dBu = jnp.einsum('bld,bln,bld->bldn', delta, Bm, u)

            def step(h, inp):
                dA_t, dBu_t, C_t = inp
                h = dA_t * h + dBu_t
                return (h, jnp.einsum('bdn,bn->bd', h, C_t))
            h0 = jnp.zeros((x.shape[0], D_INNER, D_STATE), x.dtype)
            _, ys = jax.lax.scan(step, h0, (dA.transpose(1, 0, 2, 3), dBu.transpose(1, 0, 2, 3), Cm.transpose(1, 0, 2)))
            y = ys.transpose(1, 0, 2) + u * Dp
            y = y * jax.nn.silu(z)
            return jnp.einsum('bld,od->blo', y, W_out)

        def _forward(x, in_proj_w, conv_w, conv_b, x_proj_w, dt_proj_w, dt_proj_b, A_log, D, out_proj_w):
            residual = x
            for i in range(N_LAYERS):
                x = _mamba_block(x, in_proj_w[i], conv_w[i], conv_b[i], x_proj_w[i], dt_proj_w[i], dt_proj_b[i], A_log[i], D[i], out_proj_w[i])
            return x + residual
        key = jax.random.key(seed)
        ks = jax.random.split(key, 8)
        x = jax.random.normal(ks[0], (BATCH, SEQ, D_MODEL), jnp.float32)
        in_proj_w = jax.random.normal(ks[1], (N_LAYERS, 2 * D_INNER, D_MODEL), jnp.float32) * 0.02
        conv_w = jax.random.normal(ks[2], (N_LAYERS, D_INNER, 1, D_CONV), jnp.float32) * 0.2
        conv_b = jnp.zeros((N_LAYERS, D_INNER), jnp.float32)
        x_proj_w = jax.random.normal(ks[3], (N_LAYERS, DT_RANK + 2 * D_STATE, D_INNER), jnp.float32) * 0.02
        dt_proj_w = jax.random.normal(ks[4], (N_LAYERS, D_INNER, DT_RANK), jnp.float32) * 0.1
        dt_proj_b = jnp.full((N_LAYERS, D_INNER), float(np.log(np.expm1(0.01))), jnp.float32)
        A_log = jnp.tile(jnp.log(jnp.arange(1, D_STATE + 1, dtype=jnp.float32))[None, None, :], (N_LAYERS, D_INNER, 1))
        D = jnp.ones((N_LAYERS, D_INNER), jnp.float32)
        out_proj_w = jax.random.normal(ks[5], (N_LAYERS, D_MODEL, D_INNER), jnp.float32) * 0.02
        return {'x': x, 'in_proj_w': in_proj_w, 'conv_w': conv_w, 'conv_b': conv_b, 'x_proj_w': x_proj_w, 'dt_proj_w': dt_proj_w, 'dt_proj_b': dt_proj_b, 'A_log': A_log, 'D': D, 'out_proj_w': out_proj_w}
    _L0_attn_in = _L0_attn_setup()

    def _L0_ffn_setup():
        import jax, jax.numpy as jnp
        import numpy as np
        LN_EPS = 1e-05
        NORM_EPS = 1e-12

        def _layernorm(x, gamma, beta):
            mu = x.mean(axis=-1, keepdims=True)
            var = ((x - mu) ** 2).mean(axis=-1, keepdims=True)
            return (x - mu) * jax.lax.rsqrt(var + LN_EPS) * gamma + beta

        def _l2norm(x, axis):
            n = jnp.sqrt((x ** 2).sum(axis=axis, keepdims=True))
            return x / jnp.maximum(n, NORM_EPS)
        key = jax.random.key(seed)
        ks = jax.random.split(key, 4)
        B, N, D, E, S, H = (64, 128, 512, 16, 16, 128)
        x = jax.random.normal(ks[0], (B, N, D), dtype=jnp.float32)
        mu = jax.random.normal(ks[1], (D, E, S), dtype=jnp.float32) / np.sqrt(D)
        w1 = jax.random.normal(ks[2], (E, D, H), dtype=jnp.float32) * np.sqrt(2.0 / D)
        w2 = jax.random.normal(ks[3], (E, H, D), dtype=jnp.float32) * np.sqrt(2.0 / (H + D))
        return {'x': x, 'ln_gamma': jnp.ones((D,), jnp.float32), 'ln_beta': jnp.zeros((D,), jnp.float32), 'mu': mu, 'scale': jnp.ones((1,), jnp.float32), 'w1': w1, 'b1': jnp.zeros((E, H), jnp.float32), 'w2': w2, 'b2': jnp.zeros((E, D), jnp.float32)}
    _L0_ffn_in = _L0_ffn_setup()
    _d = {'L0_attn_x': _L0_attn_in['x'], 'L0_attn_in_proj_w': _L0_attn_in['in_proj_w'], 'L0_attn_conv_w': _L0_attn_in['conv_w'], 'L0_attn_conv_b': _L0_attn_in['conv_b'], 'L0_attn_x_proj_w': _L0_attn_in['x_proj_w'], 'L0_attn_dt_proj_w': _L0_attn_in['dt_proj_w'], 'L0_attn_dt_proj_b': _L0_attn_in['dt_proj_b'], 'L0_attn_A_log': _L0_attn_in['A_log'], 'L0_attn_D': _L0_attn_in['D'], 'L0_attn_out_proj_w': _L0_attn_in['out_proj_w'], 'L0_ffn_ln_gamma': _L0_ffn_in['ln_gamma'], 'L0_ffn_ln_beta': _L0_ffn_in['ln_beta'], 'L0_ffn_mu': _L0_ffn_in['mu'], 'L0_ffn_scale': _L0_ffn_in['scale'], 'L0_ffn_w1': _L0_ffn_in['w1'], 'L0_ffn_b1': _L0_ffn_in['b1'], 'L0_ffn_w2': _L0_ffn_in['w2'], 'L0_ffn_b2': _L0_ffn_in['b2']}
    _x0 = _d['L0_attn_x']
    _d['L0_attn_x'] = jax.random.normal(jax.random.fold_in(jax.random.key(seed), 1), (1, 8192, 512), dtype=_x0.dtype)
    del _x0
    return _d

def reference(L0_attn_x, L0_attn_in_proj_w, L0_attn_conv_w, L0_attn_conv_b, L0_attn_x_proj_w, L0_attn_dt_proj_w, L0_attn_dt_proj_b, L0_attn_A_log, L0_attn_D, L0_attn_out_proj_w, L0_ffn_ln_gamma, L0_ffn_ln_beta, L0_ffn_mu, L0_ffn_scale, L0_ffn_w1, L0_ffn_b1, L0_ffn_w2, L0_ffn_b2):

    def _L0_attn_ref(x, in_proj_w, conv_w, conv_b, x_proj_w, dt_proj_w, dt_proj_b, A_log, D, out_proj_w):
        import jax, jax.numpy as jnp
        import numpy as np
        N_LAYERS = 2
        D_MODEL = 512
        EXPAND = 2
        D_INNER = EXPAND * D_MODEL
        D_STATE = 16
        D_CONV = 4
        DT_RANK = (D_MODEL + 15) // 16
        BATCH = 2
        SEQ = 512

        def _mamba_block(x, W_in, w_c, b_c, W_x, W_dt, b_dt, A_log, Dp, W_out):
            xz = jnp.einsum('bld,ed->ble', x, W_in)
            xc, z = jnp.split(xz, 2, axis=-1)
            xc = xc.transpose(0, 2, 1)
            xc = jax.lax.conv_general_dilated(xc, w_c, window_strides=(1,), padding=[(D_CONV - 1, 0)], dimension_numbers=('NCH', 'OIH', 'NCH'), feature_group_count=D_INNER) + b_c[None, :, None]
            u = jax.nn.silu(xc).transpose(0, 2, 1)
            x_dbl = jnp.einsum('bld,ed->ble', u, W_x)
            dt, Bm, Cm = jnp.split(x_dbl, [DT_RANK, DT_RANK + D_STATE], axis=-1)
            delta = jax.nn.softplus(jnp.einsum('blr,dr->bld', dt, W_dt) + b_dt)
            A = -jnp.exp(A_log)
            dA = jnp.exp(jnp.einsum('bld,dn->bldn', delta, A))
            dBu = jnp.einsum('bld,bln,bld->bldn', delta, Bm, u)

            def step(h, inp):
                dA_t, dBu_t, C_t = inp
                h = dA_t * h + dBu_t
                return (h, jnp.einsum('bdn,bn->bd', h, C_t))
            h0 = jnp.zeros((x.shape[0], D_INNER, D_STATE), x.dtype)
            _, ys = jax.lax.scan(step, h0, (dA.transpose(1, 0, 2, 3), dBu.transpose(1, 0, 2, 3), Cm.transpose(1, 0, 2)))
            y = ys.transpose(1, 0, 2) + u * Dp
            y = y * jax.nn.silu(z)
            return jnp.einsum('bld,od->blo', y, W_out)

        def _forward(x, in_proj_w, conv_w, conv_b, x_proj_w, dt_proj_w, dt_proj_b, A_log, D, out_proj_w):
            residual = x
            for i in range(N_LAYERS):
                x = _mamba_block(x, in_proj_w[i], conv_w[i], conv_b[i], x_proj_w[i], dt_proj_w[i], dt_proj_b[i], A_log[i], D[i], out_proj_w[i])
            return x + residual
        return _forward(x, in_proj_w, conv_w, conv_b, x_proj_w, dt_proj_w, dt_proj_b, A_log, D, out_proj_w)

    def _L0_ffn_ref(x, ln_gamma, ln_beta, mu, scale, w1, b1, w2, b2):
        import jax, jax.numpy as jnp
        import numpy as np
        LN_EPS = 1e-05
        NORM_EPS = 1e-12

        def _layernorm(x, gamma, beta):
            mu = x.mean(axis=-1, keepdims=True)
            var = ((x - mu) ** 2).mean(axis=-1, keepdims=True)
            return (x - mu) * jax.lax.rsqrt(var + LN_EPS) * gamma + beta

        def _l2norm(x, axis):
            n = jnp.sqrt((x ** 2).sum(axis=axis, keepdims=True))
            return x / jnp.maximum(n, NORM_EPS)
        B, N, D = x.shape
        _, E, S = mu.shape
        xn = _layernorm(x, ln_gamma, ln_beta)
        x_unit = _l2norm(xn, axis=-1)
        mu_unit = _l2norm(mu, axis=0)
        logits = jnp.einsum('bnd,des->bnes', x_unit * scale, mu_unit)
        dispatch = jax.nn.softmax(logits, axis=1)
        combine = jax.nn.softmax(logits.reshape(B, N, E * S), axis=-1).reshape(B, N, E, S)
        slot_in = jnp.einsum('bnd,bnes->besd', xn, dispatch)
        h = jax.nn.gelu(jnp.einsum('besd,edh->besh', slot_in, w1) + b1[None, :, None, :], approximate=False)
        slot_out = jnp.einsum('besh,ehd->besd', h, w2) + b2[None, :, None, :]
        out = jnp.einsum('besd,bnes->bnd', slot_out, combine)
        return out
    x = L0_attn_x
    x = x + _layernorm(_L0_attn_ref(_layernorm(x, axis=-1), L0_attn_in_proj_w, L0_attn_conv_w, L0_attn_conv_b, L0_attn_x_proj_w, L0_attn_dt_proj_w, L0_attn_dt_proj_b, L0_attn_A_log, L0_attn_D, L0_attn_out_proj_w), axis=-1)
    x = x + _layernorm(_L0_ffn_ref(_layernorm(x, axis=-1), L0_ffn_ln_gamma, L0_ffn_ln_beta, L0_ffn_mu, L0_ffn_scale, L0_ffn_w1, L0_ffn_b1, L0_ffn_w2, L0_ffn_b2), axis=-1)
    return x

_drawn_inputs = setup_inputs


def setup_inputs(seed=0):
    import zlib

    import numpy as np

    out = dict(_drawn_inputs(seed))
    spreads = {'L0_attn_conv_b': (0.0, 0.1),
     'L0_attn_dt_proj_b': (-4.600165843963623, 0.2),
     'L0_attn_D': (1.0, 0.2),
     'L0_ffn_ln_gamma': (1.0, 0.2),
     'L0_ffn_ln_beta': (0.0, 0.1),
     'L0_ffn_b1': (0.0, 0.1),
     'L0_ffn_b2': (0.0, 0.1)}
    factors = {}
    for name, (base, spread) in spreads.items():
        noise = np.random.default_rng([zlib.crc32(name.encode()), seed]).standard_normal(out[name].shape)
        drawn = base * np.exp(spread * noise) if base else spread * noise
        out[name] = jnp.asarray(drawn.astype(out[name].dtype))
    for name, factor in factors.items():
        out[name] = (out[name] * factor).astype(out[name].dtype)
    return out
```

```python
from contextlib import ExitStack

import concourse.bass as bass
from concourse import mybir

ALU = mybir.AluOpType
ACT = mybir.ActivationFunctionType
AX_X = mybir.AxisListType.X
F32 = mybir.dt.float32

P = 128
D_MODEL = 512
D_INNER = 1024
STATES = 16
TAPS = 4
RANK = 32
SEQ = 8192
LAYERS = 2
T = 512
J = T // P
NC = SEQ // T
KD = D_MODEL // P
NB = D_INNER // P
HB = NB // 2
GROUPS = 2 * STATES
SCANS = GROUPS * HB
XD = RANK + 2 * STATES
PAR = STATES + TAPS + 3
LN_EPS = 1e-5
NORM_EPS = 1e-12
EXPERTS = 16
SLOTS = 256
HID = 128

PROJ_TILES = 4 * NB + 4 + 2
PROJ_PROLOGUE = 2 * NB + 2 + HB
PROJ_FIRST = PROJ_TILES - 4
TURN_TILES = SCANS + NB
TURN_FIRST = SCANS + HB

C_SCAN, C_BU, C_EXP, C_TURN, C_PROJ, C_HS, C_Y, C_W, C_DP, C_XC = 4, SCANS, SCANS, 4, 8, GROUPS, NB, NB, 2, NB


class Tally:

    def __init__(self, base):
        self.base, self.n = base, 0

    def at(self, extra):
        return self.base + (self.n + extra)


def body_kinds(eng, run):
    run(0, True, False)
    with eng.Fori(1, NC - 1) as c:
        run(c, False, False)
    run(NC - 1, False, True)


def mamba_stack(nc, ctx, d):
    def sb(name, shape):
        return ctx.enter_context(nc.sbuf_tensor(name, shape, F32))

    def ps(name, shape):
        return ctx.enter_context(nc.psum_tensor(name, shape, F32))

    def sem(name):
        return ctx.enter_context(nc.semaphore(name))

    w_in = sb("w_in", [P, KD, 2 * D_INNER])
    w_out = sb("w_out", [P, NB, D_MODEL])
    w_x = sb("w_x", [P, NB, XD])
    w_dt = sb("w_dt", [RANK, D_INNER])
    par = sb("par", [P, NB, PAR])
    neg_a = sb("neg_a", [P, NB, STATES])
    conv_diag = sb("conv_diag", [P, 2, TAPS, P])
    ident = sb("ident_m", [P, P])
    zeros = sb("zeros_m", [P, NB * 3])
    x_conv = sb("x_conv", [P, KD, T])
    x_gate = sb("x_gate", [P, KD, T])
    conv_in = sb("conv_in", [P, 2, 3 + T])
    halo = sb("halo", [P, NB, 3])
    u = sb("u", [P, NB, T])
    delta = sb("delta", [P, NB, T])
    tmp = sb("tmp", [P, 2, T])
    w = sb("w", [P, NB, T])
    ud = sb("ud", [P, NB, T])
    zy = sb("zy", [P, NB, T])
    xdbl = sb("xdbl", [P, T])
    c_next = sb("c_next", [P, J, STATES])
    c_now = sb("c_now", [P, J, STATES])
    b_rep = sb("b_rep", [P, 4, T])
    bu = sb("bu", [P, 4, T])
    h = sb("h", [P, 2, HB, T])
    h_last = sb("h_last", [P, GROUPS * HB])
    acc = sb("acc", [P, 2, J, HB * P])
    stage = sb("stage", [P, 2, T])

    decay = ps("decay", [P, 2, T])
    turn = ps("turn", [P, 4, T])
    proj = ps("proj", [P, 2, T])

    weights_in = sem("weights_in")
    xconv_in = sem("xconv_in")
    xgate_in = sem("xgate_in")
    brep_in = [sem(f"brep_in{r}") for r in range(4)]
    b_stored = sem("b_stored")
    out_stored = [sem(f"out_stored{r}") for r in range(2)]
    ident_set = sem("ident_set")
    zeros_set = sem("zeros_set")
    hz_set = sem("hz_set")
    a_set = sem("a_set")
    halo_set = sem("halo_set")
    proj_full = sem("proj_full")
    proj_done = sem("proj_done")
    convin_set = sem("convin_set")
    abs_set = sem("abs_set")
    softplus_set = sem("softplus_set")
    delta_set = sem("delta_set")
    w_set = sem("w_set")
    ud_set = sem("ud_set")
    decay_set = sem("decay_set")
    bu_set = sem("bu_set")
    scanned = sem("scanned")
    turn_full = sem("turn_full")
    turn_done = sem("turn_done")
    hlast_set = sem("hlast_set")
    c_set = sem("c_set")
    y_set = sem("y_set")

    N_W = 5
    block = ctx.enter_context(nc.Block())

    def proj_base(l, c, first):
        if first:
            return l * (NC * PROJ_TILES) + PROJ_PROLOGUE
        return l * (NC * PROJ_TILES) + c * PROJ_TILES + (PROJ_PROLOGUE + PROJ_FIRST - PROJ_TILES)

    def turn_base(l, c, first):
        if first:
            return l * (NC * TURN_TILES)
        return l * (NC * TURN_TILES) + c * TURN_TILES + (TURN_FIRST - TURN_TILES)

    @block.sync
    def _(sp):
        sp.sem_inc(b_stored, 16)
        with sp.Fori(0, LAYERS) as l:
            for r in range(2):
                sp.wait_ge(out_stored[r], l * (NC * 2 * 16) + 16)
            sp.dma_start(w_in[:], d["w_in"][bass.ds(l, 1)].rearrange("a p k e -> (a p) k e")).then_inc(weights_in, 16)
            sp.dma_start(par[:], d["par"][bass.ds(l, 1)].rearrange("a p b n -> (a p) b n")).then_inc(weights_in, 16)
            sp.dma_start(w_x[:], d["w_x"][bass.ds(l, 1)].rearrange("a p b n -> (a p) b n")).then_inc(weights_in, 16)
            sp.dma_start(w_dt[:], d["w_dt"][bass.ds(l, 1)].rearrange("a p n -> (a p) n")).then_inc(weights_in, 16)
            sp.dma_start(w_out[:], d["w_out"][bass.ds(l, 1)].rearrange("a p b n -> (a p) b n")).then_inc(weights_in, 16)

            def load_x(dst, G, done):
                sp.dma_start(dst[:], d["xt"][bass.ds(G, 1)].rearrange("a p k t -> (a p) k t")).then_inc(done, 16)

            def load_b(G, k):
                sp.wait_ge(bu_set, G * SCANS + (4 * (k - 4) + 4 + C_BU))
                if k == 0:
                    sp.wait_ge(b_stored, G * 16 + 32)
                n = k % STATES
                src = d["b_rows"][bass.ds(G, 1), n, :].rearrange("a t -> (a t)").partition_broadcast(P)
                sp.dma_start(b_rep[:, k % 4, :], src).then_inc(brep_in[k % 4], 16)

            load_x(x_conv, l * NC, xconv_in)

            def body(c, first, last):
                G = l * NC + c
                for k in range(GROUPS):
                    load_b(G, k)
                    if k == 3 and not last:
                        sp.wait_ge(convin_set, G * NB + NB + C_XC)
                        load_x(x_conv, G + 1, xconv_in)
                    if k == 8:
                        sp.wait_ge(decay_set, G * SCANS + C_EXP)
                        load_x(x_gate, G, xgate_in)

            body_kinds(sp, body)
        for r in range(2):
            sp.wait_ge(out_stored[r], 16 + LAYERS * NC * 2 * 16)

    @block.tensor
    def _(pe):
        pe.wait_ge(ident_set, 2)
        with pe.Fori(0, LAYERS) as l:
            pe.wait_ge(weights_in, l * (16 * N_W) + 16 * N_W)

            def bank(pj):
                pe.wait_ge(proj_done, pj.at(C_PROJ - 1))
                return proj[:, pj.n % 2, :]

            def full(pj, mm):
                mm.then_inc(proj_full, 1)
                pj.n += 1

            def conv_half(pj, X, b):
                if b == 0:
                    pe.wait_ge(xconv_in, X * 16 + 16)
                out = bank(pj)
                for k in range(KD):
                    mm = pe.matmul(out, w_in[:, k, b * P:(b + 1) * P], x_conv[:, k, :], start=k == 0, stop=k == KD - 1)
                full(pj, mm)

            def conv(pj, X, b):
                pe.wait_ge(convin_set, X * NB + (b + 1 + C_XC))
                out = bank(pj)
                for k in range(TAPS):
                    mm = pe.matmul(out, conv_diag[:, b % 2, k, :], conv_in[:, b % 2, k:k + T], start=k == 0, stop=k == TAPS - 1)
                full(pj, mm)

            def x_proj(pj):
                pe.wait_ge(proj_done, pj.at(C_PROJ))
                out = bank(pj)
                for b in range(NB):
                    mm = pe.matmul(out[0:XD, :], w_x[:, b, :], u[:, b, :], start=b == 0, stop=b == NB - 1)
                full(pj, mm)

            def turn_c(pj):
                pe.wait_ge(proj_done, pj.at(C_PROJ))
                out = bank(pj)
                for j in range(J):
                    mm = pe.transpose(out[:, j * P:(j + 1) * P], xdbl[:, j * P:(j + 1) * P], ident[:])
                full(pj, mm)

            def delta_proj(pj, b):
                out = bank(pj)
                full(pj, pe.matmul(out, w_dt[:, b * P:(b + 1) * P], xdbl[0:RANK, :], start=True, stop=True))

            def gate(pj, G, b):
                if b == 0:
                    pe.wait_ge(xgate_in, G * 16 + 16)
                out = bank(pj)
                for k in range(KD):
                    mm = pe.matmul(out, w_in[:, k, D_INNER + b * P:D_INNER + (b + 1) * P], x_gate[:, k, :],
                                   start=k == 0, stop=k == KD - 1)
                full(pj, mm)

            def out_proj(pj, G, o):
                if o == 0:
                    pe.wait_ge(y_set, G * NB + (NB + C_Y))
                out = bank(pj)
                for b in range(NB):
                    mm = pe.matmul(out, w_out[:, b, o * P:(o + 1) * P], zy[:, b, :], start=b == 0, stop=b == NB - 1)
                full(pj, mm)

            def turn_states(tn, G, k):
                pe.wait_ge(scanned, G * SCANS + (4 * k + 4 + C_SCAN))
                for j in range(J):
                    pe.wait_ge(turn_done, tn.at(C_TURN - 3))
                    for b in range(HB):
                        mm = pe.transpose(turn[:, tn.n % 4, b * P:(b + 1) * P], h[:, k % 2, b, j * P:(j + 1) * P], ident[:])
                    mm.then_inc(turn_full, 1)
                    tn.n += 1

            def turn_y(tn, hf, sums):
                pe.wait_ge(turn_done, tn.base + (sums + C_TURN))
                for b in range(HB):
                    pe.wait_ge(turn_done, tn.at(C_TURN - 3))
                    for j in range(J):
                        mm = pe.transpose(turn[:, tn.n % 4, j * P:(j + 1) * P], acc[:, hf, j, b * P:(b + 1) * P], ident[:])
                    mm.then_inc(turn_full, 1)
                    tn.n += 1

            pj = Tally(l * (NC * PROJ_TILES))
            X = l * NC
            for b in range(0, NB, 2):
                conv_half(pj, X, b)
                conv_half(pj, X, b + 1)
                conv(pj, X, b)
                conv(pj, X, b + 1)
            x_proj(pj)
            turn_c(pj)
            for b in range(HB):
                delta_proj(pj, b)

            def body(c, first, last):
                G = l * NC + c
                pj = Tally(proj_base(l, c, first))
                tn = Tally(turn_base(l, c, first))
                half0 = 0
                for k in range(GROUPS):
                    turn_states(tn, G, k)
                    if k == STATES - 1:
                        half0 = tn.n
                    if not first and k in (4, 9, 14, 17):
                        out_proj(pj, G - 1, (4, 9, 14, 17).index(k))
                    if not last and k in (0, 1, 5, 6, 10, 11, 15, 16):
                        conv_half(pj, G + 1, (0, 1, 5, 6, 10, 11, 15, 16).index(k))
                    if not last and k in (2, 3, 7, 8, 12, 13, 18, 19):
                        conv(pj, G + 1, (2, 3, 7, 8, 12, 13, 18, 19).index(k))
                    if k in (5, 6, 10, 11):
                        delta_proj(pj, HB + (5, 6, 10, 11).index(k))
                    if k in (20, 21, 23, 24, 27, 28, 29, 30):
                        gate(pj, G, (20, 21, 23, 24, 27, 28, 29, 30).index(k))
                    if not last and k == 22:
                        x_proj(pj)
                    if not last and k == 25:
                        turn_c(pj)
                        delta_proj(pj, 0)
                        delta_proj(pj, 1)
                    if not last and k == 26:
                        delta_proj(pj, 2)
                        delta_proj(pj, 3)
                    if k == 1 and not first:
                        turn_y(tn, 1, 0)
                    if k == 26:
                        turn_y(tn, 0, half0)

            body_kinds(pe, body)

            pj = Tally(l * (NC * PROJ_TILES) + (NC * PROJ_TILES - 4))
            tn = Tally(l * (NC * TURN_TILES) + (NC * TURN_TILES - HB))
            turn_y(tn, 1, 0)
            for o in range(KD):
                out_proj(pj, X + (NC - 1), o)

    @block.scalar
    def _(act):
        act.sem_inc(proj_done, C_PROJ)
        act.sem_inc(decay_set, C_EXP)
        act.sem_inc(convin_set, C_XC)
        act.sem_inc(ud_set, C_W)
        for r in range(2):
            act.sem_inc(out_stored[r], 16)
        act.wait_ge(zeros_set, 1)
        act.wait_ge(ident_set, 2)
        with act.Fori(0, LAYERS) as l:
            act.wait_ge(weights_in, l * (16 * N_W) + 16 * N_W)
            act.activation(neg_a[:], par[:, :, 0:STATES], ACT.Exp).then_inc(a_set, 1)
            act.wait_ge(a_set, 2 * l + 1)
            act.mul(neg_a[:], neg_a[:], -1.0).then_inc(a_set, 1)
            act.copy(halo[:].rearrange("p b t -> p (b t)"), zeros[:]).then_inc(halo_set, 1)
            act.wait_ge(a_set, 2 * l + 2)
            act.wait_ge(halo_set, l + 1)
            conv_bias, dt_bias = STATES + TAPS, STATES + TAPS + 1

            def take(pj):
                act.wait_ge(proj_full, pj.at(1))
                return proj[:, pj.n % 2, :]

            def done(pj, ins):
                ins.then_inc(proj_done, 1)
                pj.n += 1

            def conv_half(pj, X, b):
                src = take(pj)
                act.wait_ge(proj_done, pj.at(C_PROJ - 1))
                act.copy(conv_in[:, b % 2, 0:3], halo[:, b, :])
                for k in range(TAPS):
                    act.activation(conv_diag[:, b % 2, k, :], ident[:], ACT.Copy, scale=par[:, b, STATES + k:STATES + k + 1])
                act.copy(conv_in[:, b % 2, 3:3 + T], src).then_inc(convin_set, 1)
                act.wait_ge(convin_set, X * NB + (b + 1 + C_XC))
                done(pj, act.copy(halo[:, b, :], src[:, T - 3:T]))

            def conv(pj, X, b):
                act.wait_ge(w_set, X * NB + (b + 1))
                act.wait_ge(ud_set, X * NB + (b + 1))
                done(pj, act.activation(u[:, b, :], take(pj), ACT.Silu, bias=par[:, b, conv_bias:conv_bias + 1]))

            def x_proj(pj, X):
                act.wait_ge(b_stored, X * 16 + 16)
                done(pj, act.copy(xdbl[0:XD, :], take(pj)[0:XD, :]))
                act.wait_ge(proj_done, pj.at(C_PROJ))
                act.dma_start(d["b_rows"][bass.ds(X, 1)].rearrange("a n t -> (a n) t"),
                              xdbl[RANK:RANK + STATES, :]).then_inc(b_stored, 16)

            def turn_c(pj, X):
                act.wait_ge(c_set, X + 1)
                src = take(pj).rearrange("p (j r) -> p j r", j=J)
                done(pj, act.copy(c_next[:], src[:, :, RANK + STATES:XD]))

            def delta_proj(pj, X, b):
                src = take(pj)
                bias = par[:, b, dt_bias:dt_bias + 1]
                part = tmp[:, b % 2, :]
                act.wait_ge(delta_set, X * NB + (b + 1))
                act.wait_ge(w_set, X * NB + (b + 1))
                act.wait_ge(decay_set, X * SCANS + (b // HB * (SCANS // 2) - SCANS // 2 + C_EXP))
                act.activation(part, src, ACT.Abs, bias=bias).then_inc(abs_set, 1)
                done(pj, act.activation(delta[:, b, :], src, ACT.Relu, bias=bias))
                act.wait_ge(abs_set, (X * NB + b) * 2 + 1)
                act.activation(part, part, ACT.Exp, scale=-1.0).then_inc(abs_set, 1)
                act.wait_ge(abs_set, (X * NB + b) * 2 + 2)
                act.activation(part, part, ACT.Ln, bias=1.0).then_inc(softplus_set, 1)

            def skip(pj, X, b):
                act.wait_ge(proj_done, pj.at(C_PROJ))
                act.wait_ge(y_set, X * NB + (b + 1))
                act.activation(ud[:, b, :], u[:, b, :], ACT.Copy, scale=par[:, b, PAR - 1:PAR]).then_inc(ud_set, 1)

            def gate(pj, G, b):
                done(pj, act.activation(zy[:, b, :], take(pj), ACT.Silu))

            def out_proj(pj, G, o):
                act.wait_ge(out_stored[o % 2], G * 32 + (o // 2 * 16 + 16))
                done(pj, act.copy(stage[:, o % 2, :], take(pj)))
                act.wait_ge(proj_done, pj.at(C_PROJ))
                act.dma_start(d["xt"][bass.ds(G + NC, 1), :, o, :].rearrange("a p t -> (a p) t"),
                              stage[:, o % 2, :]).then_inc(out_stored[o % 2], 16)

            def decay_of(G, k, b):
                hf, n = divmod(k, STATES)
                blk = hf * HB + b
                act.wait_ge(scanned, G * SCANS + (4 * k + b - 1 + C_SCAN))
                if n == 0:
                    act.wait_ge(delta_set, G * NB + (blk + 1 + C_DP))
                act.activation(decay[:, b % 2, :], delta[:, blk, :], ACT.Exp,
                               scale=neg_a[:, blk, n:n + 1]).then_inc(decay_set, 1)

            pj = Tally(l * (NC * PROJ_TILES))
            X = l * NC
            for b in range(0, NB, 2):
                conv_half(pj, X, b)
                conv_half(pj, X, b + 1)
                conv(pj, X, b)
                conv(pj, X, b + 1)
            x_proj(pj, X)
            turn_c(pj, X)
            for b in range(HB):
                delta_proj(pj, X, b)
            for b in range(HB):
                skip(pj, X, b)

            def body(c, first, last):
                G = l * NC + c
                pj = Tally(proj_base(l, c, first))
                for k in range(GROUPS):
                    decay_of(G, k, 0)
                    decay_of(G, k, 1)
                    if not first and k in (5, 10, 15, 18):
                        out_proj(pj, G - 1, (5, 10, 15, 18).index(k))
                    if not last and k in (1, 2, 6, 7, 11, 12, 16, 17):
                        conv_half(pj, G + 1, (1, 2, 6, 7, 11, 12, 16, 17).index(k))
                    if not last and k in (4, 9, 14, 20):
                        b = 2 * (4, 9, 14, 20).index(k)
                        conv(pj, G + 1, b)
                        conv(pj, G + 1, b + 1)
                    if k in (6, 7, 11, 12):
                        delta_proj(pj, G, HB + (6, 7, 11, 12).index(k))
                    if k in (22, 25, 29, 31):
                        b = 2 * (22, 25, 29, 31).index(k)
                        gate(pj, G, b)
                        gate(pj, G, b + 1)
                    if not last and k == 23:
                        x_proj(pj, G + 1)
                    if not last and k == 26:
                        turn_c(pj, G + 1)
                        delta_proj(pj, G + 1, 0)
                        delta_proj(pj, G + 1, 1)
                    if not last and k == 27:
                        delta_proj(pj, G + 1, 2)
                        delta_proj(pj, G + 1, 3)
                    if k in (4, 5, 8, 10):
                        skip(pj, G, HB + (4, 5, 8, 10).index(k))
                    if not last and k in (30, 31):
                        skip(pj, G + 1, 2 * (k - 30))
                        skip(pj, G + 1, 2 * (k - 30) + 1)
                    decay_of(G, k, 2)
                    decay_of(G, k, 3)

            body_kinds(act, body)
            pj = Tally(l * (NC * PROJ_TILES) + (NC * PROJ_TILES - 4))
            for o in range(KD):
                out_proj(pj, X + (NC - 1), o)

    @block.gpsimd
    def _(pool):
        pool.sem_inc(bu_set, C_BU)
        pool.sem_inc(w_set, C_W)
        pool.sem_inc(delta_set, C_DP)
        pool.memset(zeros[:], 0.0)
        pool.memset(xdbl[:], 0.0).then_inc(zeros_set, 1)
        pool.memset(ident[:], 0.0).then_inc(ident_set, 1)
        pool.wait_ge(ident_set, 1)
        pool.affine_select(out=ident[:], in_=ident[:], compare_op=ALU.not_equal, fill=1.0, base=0,
                           pattern=[[-1, P]], channel_multiplier=1).then_inc(ident_set, 1)
        pool.wait_ge(ident_set, 2)
        with pool.Fori(0, LAYERS) as l:
            pool.wait_ge(weights_in, l * (16 * N_W) + 16 * N_W)

            def delta_w(X, b):
                pool.wait_ge(softplus_set, X * NB + (b + 1))
                pool.tensor_tensor(delta[:, b, :], delta[:, b, :], tmp[:, b % 2, :], ALU.add).then_inc(delta_set, 1)
                pool.wait_ge(delta_set, X * NB + (b + 1 + C_DP))
                pool.wait_ge(bu_set, X * SCANS + (b // HB * (SCANS // 2) - SCANS // 2 + C_BU))
                pool.tensor_tensor(w[:, b, :], delta[:, b, :], u[:, b, :], ALU.mult).then_inc(w_set, 1)

            def input_of(G, k, b):
                hf, n = divmod(k, STATES)
                blk = hf * HB + b
                if b == 0:
                    pool.wait_ge(brep_in[k % 4], G * (GROUPS * 4) + (k // 4 + 1) * 16)
                if n == 0:
                    pool.wait_ge(w_set, G * NB + (blk + 1 + C_W))
                pool.wait_ge(scanned, G * SCANS + (4 * k + b + 1))
                pool.tensor_tensor(bu[:, b, :], w[:, blk, :], b_rep[:, k % 4, :], ALU.mult).then_inc(bu_set, 1)

            X = l * NC
            for b in range(HB):
                delta_w(X, b)

            def body(c, first, last):
                G = l * NC + c
                for k in range(GROUPS):
                    for b in range(HB):
                        input_of(G, k, b)
                    if k in (7, 8, 12, 13):
                        delta_w(G, HB + (7, 8, 12, 13).index(k))
                    if not last and k in (27, 28):
                        for b in range(2 * (k - 27), 2 * (k - 27) + 2):
                            delta_w(G + 1, b)

            body_kinds(pool, body)

    @block.vector
    def _(dve):
        dve.sem_inc(scanned, C_SCAN)
        dve.sem_inc(turn_done, C_TURN)
        dve.sem_inc(hlast_set, C_HS)
        dve.sem_inc(y_set, C_Y)
        dve.sem_inc(c_set, 1)
        with dve.Fori(0, LAYERS) as l:
            dve.wait_ge(hlast_set, l * (NC * GROUPS) + C_HS)
            dve.memset(h_last[:], 0.0).then_inc(hz_set, 1)
            dve.wait_ge(hz_set, l + 1)

            def scan(G, k, b):
                dve.wait_ge(decay_set, G * SCANS + (4 * k + b + 1 + C_EXP))
                dve.wait_ge(bu_set, G * SCANS + (4 * k + b + 1 + C_BU))
                if b == 0:
                    dve.wait_ge(hlast_set, G * GROUPS + (k + 1))
                dve.tensor_tensor_scan(h[:, k % 2, b, :], decay[:, b % 2, :], bu[:, b, :],
                                       h_last[:, 4 * k + b:4 * k + b + 1], ALU.mult, ALU.add).then_inc(scanned, 1)

            def save_last(G, k):
                dve.wait_ge(scanned, G * SCANS + (4 * k + 4 + C_SCAN))
                dve.tensor_copy(h_last[:, 4 * k:4 * k + HB], h[:, k % 2, :, T - 1]).then_inc(hlast_set, 1)

            def add_state(tn, k, j):
                hf, n = divmod(k, STATES)
                dve.wait_ge(turn_full, tn.at(1))
                dve.wait_ge(turn_done, tn.at(C_TURN - 3))
                scalar = c_now[:, j, n:n + 1]
                if n == 0:
                    ins = dve.tensor_scalar(acc[:, hf, j, :], turn[:, tn.n % 4, :], scalar, None, ALU.mult)
                else:
                    ins = dve.scalar_tensor_tensor(acc[:, hf, j, :], turn[:, tn.n % 4, :], scalar, acc[:, hf, j, :],
                                                   ALU.mult, ALU.add)
                ins.then_inc(turn_done, 1)
                tn.n += 1

            def finish_y(tn, G, hf):
                for b in range(hf * HB, hf * HB + HB):
                    dve.wait_ge(turn_full, tn.at(1))
                    dve.wait_ge(ud_set, G * NB + (b + 1 + C_W))
                    dve.tensor_tensor(ud[:, b, :], turn[:, tn.n % 4, :], ud[:, b, :], ALU.add).then_inc(turn_done, 1)
                    tn.n += 1
                    dve.wait_ge(turn_done, tn.at(C_TURN))
                    dve.tensor_tensor(zy[:, b, :], ud[:, b, :], zy[:, b, :], ALU.mult).then_inc(y_set, 1)

            def body(c, first, last):
                G = l * NC + c
                tn = Tally(turn_base(l, c, first))
                if not first:
                    tn.n = -4
                for k in range(GROUPS):
                    if k == 1:
                        dve.wait_ge(turn_done, tn.at(C_TURN))
                        dve.tensor_copy(c_now[:], c_next[:]).then_inc(c_set, 1)
                        dve.wait_ge(c_set, G + 2)
                    for b in range(HB):
                        scan(G, k, b)
                        if b == 0 and k > 0:
                            save_last(G, k - 1)
                        if b == 0 and k == 0 and not first:
                            save_last(G - 1, GROUPS - 1)
                        if k > 0:
                            add_state(tn, k - 1, b)
                        elif not first:
                            add_state(tn, GROUPS - 1, b)
                    if k == 2 and not first:
                        finish_y(tn, G - 1, 1)
                    if k == 27:
                        finish_y(tn, G, 0)

            body_kinds(dve, body)
            G = l * NC + (NC - 1)
            tn = Tally(l * (NC * TURN_TILES) + (NC * TURN_TILES - HB))
            tn.n = -4
            save_last(G, GROUPS - 1)
            for j in range(J):
                add_state(tn, GROUPS - 1, j)
            finish_y(tn, G, 1)


class Chain:

    def __init__(self, eng, sem, base):
        self.eng, self.sem, self.base, self.n = eng, sem, base, 0

    def link(self, ins):
        ins.then_inc(self.sem, 1)
        self.n += 1
        self.eng.wait_ge(self.sem, self.base + self.n)


def makers(nc, ctx, tag):
    def sb(name, shape):
        return ctx.enter_context(nc.sbuf_tensor(name + tag, shape, F32))

    def ps(name, shape):
        return ctx.enter_context(nc.psum_tensor(name + tag, shape, F32))

    def sem(name):
        return ctx.enter_context(nc.semaphore(name + tag))

    return sb, ps, sem


def build_identity(pool, ident, ident_set):
    pool.memset(ident[:], 0.0).then_inc(ident_set, 1)
    pool.wait_ge(ident_set, 1)
    pool.affine_select(out=ident[:], in_=ident[:], compare_op=ALU.not_equal, fill=1.0, base=0,
                       pattern=[[-1, P]], channel_multiplier=1).then_inc(ident_set, 1)


def moments(dve, chain, stats, mv, rows, spare):
    for j in range(J):
        ins = dve.bn_stats(stats[:, j, :], rows[:, j, :])
    chain.link(ins)
    dve.memset(spare[:], 0.0)
    for j in range(J):
        ins = dve.bn_aggr(mv[:, j, :], stats[:, j, :])
    return ins


def norm_input(nc, ctx, d):
    sb, ps, sem = makers(nc, ctx, "_n")
    ident = sb("ident", [P, P])
    eps = sb("eps", [P, 1])
    x = sb("x", [P, 2, J, D_MODEL])
    xn = sb("xn", [P, 2, J, D_MODEL])
    xt = sb("xt", [P, 2, KD, T])
    stats = sb("stats", [P, J, 6])
    spare = sb("spare", [P, 1])
    mv = sb("mv", [P, J, 2])
    sd = sb("sd", [P, J])
    rstd = sb("rstd", [P, J])
    turn = ps("turn", [P, 2, KD, T])

    ident_set, eps_set = sem("ident_set"), sem("eps_set")
    x_in = [sem(f"x_in{s}") for s in range(2)]
    res_stored = [sem(f"res_stored{s}") for s in range(2)]
    xt_stored = [sem(f"xt_stored{s}") for s in range(2)]
    mv_set, sd_set, xn_set = sem("mv_set"), sem("sd_set"), sem("xn_set")
    turned, xt_set = sem("turned"), sem("xt_set")
    dve_step = sem("dve_step")
    block = ctx.enter_context(nc.Block())

    @block.gpsimd
    def _(pool):
        pool.memset(eps[:], LN_EPS).then_inc(eps_set, 1)
        build_identity(pool, ident, ident_set)

    @block.sync
    def _(sp):
        with sp.Fori(0, NC // 2) as pair:
            i = 2 * pair
            for s in range(2):
                sp.wait_ge(xn_set, i + (s + 1))
                sp.dma_start(x[:, s], d["x"][bass.ds(i + s, 1)].rearrange("a j p d -> p (a j) d")).then_inc(x_in[s], 16)

    @block.vector
    def _(dve):
        dve.sem_inc(xn_set, 2)
        with dve.Fori(0, NC // 2) as pair:
            i = 2 * pair
            for s in range(2):
                chain = Chain(dve, dve_step, (i + s) * 2)
                dve.wait_ge(x_in[s], i * 8 + 16)
                moments(dve, chain, stats, mv, x[:, s], spare).then_inc(mv_set, 1)
                dve.wait_ge(sd_set, i + (s + 1))
                chain.link(dve.reciprocal(rstd[:], sd[:]))
                dve.wait_ge(res_stored[s], i * 8 + 16)
                dve.wait_ge(turned, i + (s + 1))
                for j in range(J):
                    ins = dve.tensor_scalar(xn[:, s, j, :], x[:, s, j, :], mv[:, j, 0:1], rstd[:, j:j + 1],
                                            ALU.subtract, ALU.mult)
                ins.then_inc(xn_set, 1)

    @block.scalar
    def _(act):
        act.wait_ge(eps_set, 1)
        act.sem_inc(xt_set, 2)
        for s in range(2):
            act.sem_inc(res_stored[s], 16)
            act.sem_inc(xt_stored[s], 16)
        with act.Fori(0, NC // 2) as pair:
            i = 2 * pair
            for s in range(2):
                act.wait_ge(mv_set, i + (s + 1))
                act.activation(sd[:], mv[:, :, 1], ACT.Sqrt, bias=eps[:]).then_inc(sd_set, 1)
                act.wait_ge(turned, i + (s + 3))
                act.wait_ge(xt_stored[s], i * 8 + 16)
                act.copy(xt[:, s], turn[:, s]).then_inc(xt_set, 1)
                act.dma_start(d["res"][bass.ds(i + s, 1)].rearrange("a p j d -> (a p) j d"), xn[:, s]).then_inc(res_stored[s], 16)
                act.wait_ge(xt_set, i + (s + 3))
                act.dma_start(d["xt"][bass.ds(i + s, 1)].rearrange("a p k t -> (a p) k t"), xt[:, s]).then_inc(xt_stored[s], 16)
        for s in range(2):
            act.wait_ge(res_stored[s], NC * 8 + 16)
            act.wait_ge(xt_stored[s], NC * 8 + 16)

    @block.tensor
    def _(pe):
        pe.sem_inc(turned, 2)
        pe.wait_ge(ident_set, 2)
        with pe.Fori(0, NC // 2) as pair:
            i = 2 * pair
            for s in range(2):
                pe.wait_ge(xn_set, i + (s + 3))
                pe.wait_ge(xt_set, i + (s + 1))
                for j in range(J):
                    for k in range(KD):
                        mm = pe.transpose(turn[:, s, k, j * P:(j + 1) * P], xn[:, s, j, k * P:(k + 1) * P], ident[:])
                mm.then_inc(turned, 1)


def moe_logits(nc, ctx, d, logits):
    sb, ps, sem = makers(nc, ctx, "_l")
    ident = sb("ident", [P, P])
    ones = sb("ones", [P, P])
    eps = sb("eps", [P, 1])
    gamma = sb("gamma", [P, D_MODEL])
    beta = sb("beta", [P, D_MODEL])
    scale = sb("scale", [P, 1])
    mu = sb("mu", [P, KD, SLOTS])
    mu_sq = sb("mu_sq", [P, KD, SLOTS])
    mu_norm = sb("mu_norm", [P, SLOTS])
    x = sb("x", [P, J, D_MODEL])
    res = sb("res", [P, J, D_MODEL])
    mt = sb("mt", [P, KD, T])
    r = sb("r", [P, J, D_MODEL])
    x1 = sb("x1", [P, 2, J, D_MODEL])
    xh = sb("xh", [P, J, D_MODEL])
    xn = sb("xn", [P, 2, J, D_MODEL])
    xnt = sb("xnt", [P, KD, T])
    junk = sb("junk", [P, D_MODEL])
    stats = sb("stats", [P, J, 6])
    spare = sb("spare", [P, 1])
    mv = sb("mv", [P, J, 2])
    mv2 = sb("mv2", [P, J, 2])
    sd, sd2, sd3, sd4 = (sb(f"sd{n}", [P, J]) for n in range(4))
    r1, r2, r3, q, rs, ssq = (sb(n, [P, J]) for n in ("r1", "r2", "r3", "q", "rs", "ssq"))
    ta = ps("ta", [P, J, D_MODEL])
    tb = ps("tb", [P, 2, T])
    tl = ps("tl", [P, J, SLOTS])

    ident_set, const_set, small_in = sem("ident_set"), sem("const_set"), sem("small_in")
    x_in, res_in, mt_in = sem("x_in"), sem("res_in"), sem("mt_in")
    sq_set, munorm_ps, munorm_set, mu_set = sem("sq_set"), sem("munorm_ps"), sem("munorm_set"), sem("mu_set")
    ta_set, r_set, rn_set, mv_set, sd_set = sem("ta_set"), sem("r_set"), sem("rn_set"), sem("mv_set"), sem("sd_set")
    x1_set, mv2_set, sd2_set, q_set, sd3_set, xh_set = (sem(n) for n in ("x1_set", "mv2_set", "sd2_set", "q_set", "sd3_set", "xh_set"))
    g_set, xn_set, sd4_set, rs_set = (sem(n) for n in ("g_set", "xn_set", "sd4_set", "rs_set"))
    tb_set, xnt_set, tl_set, log_set = (sem(n) for n in ("tb_set", "xnt_set", "tl_set", "log_set"))
    x1_stored = [sem(f"x1_stored{s}") for s in range(2)]
    xn_stored = [sem(f"xn_stored{s}") for s in range(2)]
    dve_step, act_step = sem("dve_step"), sem("act_step")
    block = ctx.enter_context(nc.Block())

    @block.gpsimd
    def _(pool):
        pool.memset(eps[:], LN_EPS)
        pool.memset(ones[:], 1.0).then_inc(const_set, 1)
        build_identity(pool, ident, ident_set)
        pool.wait_ge(small_in, 64)
        pool.sem_inc(g_set, 1)
        with pool.Fori(0, NC // 2) as pair:
            i = 2 * pair
            for s in range(2):
                c = i + s
                pool.wait_ge(x_in, c * 16 + 16)
                pool.wait_ge(rn_set, c + 1)
                pool.wait_ge(x1_stored[s], i * 8 + 16)
                pool.tensor_tensor(x1[:, s], r[:], x[:], ALU.add).then_inc(x1_set, 1)
                pool.wait_ge(xh_set, c + 1)
                pool.wait_ge(xn_stored[s], i * 8 + 16)
                pool.wait_ge(log_set, c + 1)
                pool.tensor_tensor(xn[:, s], xh[:], gamma[:].unsqueeze(1).to_broadcast([P, J, D_MODEL]), ALU.mult).then_inc(g_set, 1)
                pool.wait_ge(g_set, c + 2)
                pool.tensor_tensor(xn[:, s], xn[:, s], beta[:].unsqueeze(1).to_broadcast([P, J, D_MODEL]), ALU.add).then_inc(xn_set, 1)

    @block.sync
    def _(sp):
        sp.dma_start(mu[:], d["mu"]).then_inc(small_in, 16)
        sp.dma_start(gamma[:], d["gamma"].partition_broadcast(P)).then_inc(small_in, 16)
        sp.dma_start(beta[:], d["beta"].partition_broadcast(P)).then_inc(small_in, 16)
        sp.dma_start(scale[:], d["scale"].partition_broadcast(P)).then_inc(small_in, 16)
        for s in range(2):
            sp.sem_inc(x1_stored[s], 16)
            sp.sem_inc(xn_stored[s], 16)
        with sp.Fori(0, NC) as c:
            sp.wait_ge(ta_set, c + 1)
            sp.dma_start(mt[:], d["xt"][bass.ds(c + LAYERS * NC, 1)].rearrange("a p k t -> (a p) k t")).then_inc(mt_in, 16)
            sp.wait_ge(r_set, c + 1)
            sp.dma_start(res[:], d["res"][bass.ds(c, 1)].rearrange("a p j d -> (a p) j d")).then_inc(res_in, 16)
            sp.wait_ge(x1_set, c + 1)
            sp.dma_start(x[:], d["x"][bass.ds(c, 1)].rearrange("a j p d -> p (a j) d")).then_inc(x_in, 16)

    @block.vector
    def _(dve):
        dve.sem_inc(r_set, 1)
        dve.sem_inc(log_set, 2)
        dve.sem_inc(x1_set, 1)
        dve.wait_ge(small_in, 64)
        dve.tensor_tensor(mu_sq[:], mu[:], mu[:], ALU.mult).then_inc(sq_set, 1)
        dve.wait_ge(munorm_set, 1)
        chain = Chain(dve, dve_step, 0)
        chain.link(dve.tensor_scalar(mu_norm[:], mu_norm[:], NORM_EPS, None, ALU.max))
        chain.link(dve.reciprocal(mu_norm[:], mu_norm[:]))
        dve.tensor_tensor(mu[:], mu[:], mu_norm[:].unsqueeze(1).to_broadcast([P, KD, SLOTS]), ALU.mult).then_inc(mu_set, 1)
        with dve.Fori(0, NC // 2) as pair:
            i = 2 * pair
            for s in range(2):
                c = i + s
                chain = Chain(dve, dve_step, c * 10 + 2)
                dve.wait_ge(ta_set, c + 2)
                dve.wait_ge(res_in, c * 16 + 16)
                dve.wait_ge(x1_set, c + 1)
                dve.tensor_tensor(r[:], ta[:], res[:], ALU.add).then_inc(r_set, 1)
                dve.wait_ge(r_set, c + 2)
                moments(dve, chain, stats, mv, r, spare).then_inc(mv_set, 1)
                dve.wait_ge(sd_set, c + 1)
                chain.link(dve.reciprocal(r1[:], sd[:]))
                for j in range(J):
                    ins = dve.tensor_scalar(r[:, j, :], r[:, j, :], mv[:, j, 0:1], r1[:, j:j + 1], ALU.subtract, ALU.mult)
                ins.then_inc(rn_set, 1)
                dve.wait_ge(x1_set, c + 2)
                moments(dve, chain, stats, mv2, x1[:, s], spare).then_inc(mv2_set, 1)
                dve.wait_ge(sd2_set, c + 1)
                chain.link(dve.reciprocal(r2[:], sd2[:]))
                chain.link(dve.tensor_tensor(q[:], mv2[:, :, 1], r2[:], ALU.mult))
                dve.tensor_tensor(q[:], q[:], r2[:], ALU.mult).then_inc(q_set, 1)
                dve.wait_ge(sd3_set, c + 1)
                chain.link(dve.reciprocal(r3[:], sd3[:]))
                chain.link(dve.tensor_tensor(r3[:], r3[:], r2[:], ALU.mult))
                dve.wait_ge(g_set, c + 1)
                for j in range(J):
                    ins = dve.tensor_scalar(xh[:, j, :], x1[:, s, j, :], mv2[:, j, 0:1], r3[:, j:j + 1], ALU.subtract, ALU.mult)
                ins.then_inc(xh_set, 1)
                dve.wait_ge(sd4_set, c + 1)
                chain.link(dve.tensor_scalar(rs[:], sd4[:], NORM_EPS, None, ALU.max))
                chain.link(dve.reciprocal(rs[:], rs[:]))
                chain.link(dve.tensor_scalar(rs[:], rs[:], scale[:, 0:1], None, ALU.mult))
                dve.wait_ge(tl_set, c + 2)
                for j in range(J):
                    ins = dve.tensor_scalar(logits[:, bass.ds(c * J + j, 1), :].rearrange("p a s -> p (a s)"), tl[:, j, :],
                                            rs[:, j:j + 1], None, ALU.mult)
                ins.then_inc(log_set, 1)

    @block.scalar
    def _(act):
        act.wait_ge(const_set, 1)
        act.wait_ge(munorm_ps, 1)
        act.activation(mu_norm[:], tl[:, 0, :], ACT.Sqrt).then_inc(munorm_set, 1)
        act.sem_inc(xnt_set, 2)
        act.sem_inc(act_step, 1)
        with act.Fori(0, NC // 2) as pair:
            i = 2 * pair
            for s in range(2):
                c = i + s
                act.wait_ge(mv_set, c + 1)
                act.activation(sd[:], mv[:, :, 1], ACT.Sqrt, bias=eps[:]).then_inc(sd_set, 1)
                act.wait_ge(mv2_set, c + 1)
                act.activation(sd2[:], mv2[:, :, 1], ACT.Sqrt, bias=eps[:]).then_inc(sd2_set, 1)
                act.wait_ge(q_set, c + 1)
                act.activation(sd3[:], q[:], ACT.Sqrt, bias=eps[:]).then_inc(sd3_set, 1)
                act.wait_ge(xn_set, c + 1)
                act.dma_start(d["x1"][bass.ds(c, 1)].rearrange("a p j d -> (a p) j d"), x1[:, s]).then_inc(x1_stored[s], 16)
                act.dma_start(d["xn"][bass.ds(c, 1)].rearrange("a p j d -> (a p) j d"), xn[:, s]).then_inc(xn_stored[s], 16)
                for j in range(J):
                    act.wait_ge(act_step, c * J + (j + 1))
                    act.activation(junk[:], xn[:, s, j, :], ACT.Square, accum_out=ssq[:, j:j + 1]).then_inc(act_step, 1)
                act.wait_ge(act_step, c * J + (J + 1))
                act.activation(sd4[:], ssq[:], ACT.Sqrt).then_inc(sd4_set, 1)
                for k in range(KD):
                    if k == 0:
                        act.wait_ge(tl_set, c + 1)
                    act.wait_ge(tb_set, c * 4 + (k + 3))
                    act.copy(xnt[:, k, :], tb[:, k % 2, :]).then_inc(xnt_set, 1)
        for s in range(2):
            act.wait_ge(x1_stored[s], NC * 8 + 16)
            act.wait_ge(xn_stored[s], NC * 8 + 16)

    @block.tensor
    def _(pe):
        pe.wait_ge(ident_set, 2)
        pe.wait_ge(const_set, 1)
        pe.wait_ge(sq_set, 1)
        for k in range(KD):
            mm = pe.matmul(tl[:, 0, :], ones[:], mu_sq[:, k, :], start=k == 0, stop=k == KD - 1)
        mm.then_inc(munorm_ps, 1)
        pe.wait_ge(mu_set, 1)
        pe.sem_inc(ta_set, 1)
        pe.sem_inc(tb_set, 2)
        pe.sem_inc(tl_set, 1)
        with pe.Fori(0, NC // 2) as pair:
            i = 2 * pair
            for s in range(2):
                c = i + s
                pe.wait_ge(mt_in, c * 16 + 16)
                pe.wait_ge(r_set, c + 1)
                for j in range(J):
                    for k in range(KD):
                        mm = pe.transpose(ta[:, j, k * P:(k + 1) * P], mt[:, k, j * P:(j + 1) * P], ident[:])
                mm.then_inc(ta_set, 1)
                pe.wait_ge(xn_set, c + 1)
                for k in range(KD):
                    pe.wait_ge(xnt_set, c * 4 + (k + 1))
                    for j in range(J):
                        mm = pe.transpose(tb[:, k % 2, j * P:(j + 1) * P], xn[:, s, j, k * P:(k + 1) * P], ident[:])
                    mm.then_inc(tb_set, 1)
                pe.wait_ge(xnt_set, c * 4 + 6)
                pe.wait_ge(log_set, c + 2)
                for j in range(J):
                    for k in range(KD):
                        mm = pe.matmul(tl[:, j, :], xnt[:, k, j * P:(j + 1) * P], mu[:, k, :], start=k == 0, stop=k == KD - 1)
                mm.then_inc(tl_set, 1)


def moe_dispatch(nc, ctx, d, logits, slot_out):
    sb, ps, sem = makers(nc, ctx, "_d")
    ident = sb("ident", [P, P])
    zeros = sb("zeros", [P, P])
    ones = sb("ones", [P, 1])
    top = sb("top", [P, SLOTS])
    top_t = sb("top_t", [P, 2])
    top_b = sb("top_b", [P, 2, P])
    top_rep = sb("top_rep", [P, SLOTS])
    xn = sb("xn", [P, 2, J, D_MODEL])
    diff = sb("diff", [P, 2, J, SLOTS])
    e = sb("e", [P, 2, J, SLOTS])
    rden = sb("rden", [P, 2])
    slot_in = sb("slot_in", [P, 2, D_MODEL])
    slot_t = sb("slot_t", [P, KD, SLOTS])
    hidden = sb("hidden", [P, EXPERTS, P])
    w1 = sb("w1", [P, KD, EXPERTS, HID])
    w2 = sb("w2", [P, EXPERTS, D_MODEL])
    b1 = sb("b1", [P, EXPERTS])
    b2 = sb("b2", [P, 2, D_MODEL])
    sums = ps("sums", [P, 2, D_MODEL])
    den = ps("den", [P, 2, 512])
    turn = ps("turn", [P, 4, 512])
    per = SLOTS // EXPERTS
    half = EXPERTS // 2

    ident_set, const_set = sem("ident_set"), sem("const_set")
    w_in = sem("w_in")
    xn_in = [sem(f"xn_in{s}") for s in range(2)]
    top_set, top_turned, topb_set, top_rep_ps, top_rep_set = (sem(n) for n in ("top_set", "top_turned", "topb_set", "top_rep_ps", "top_rep_set"))
    diff_set, e_set, summed = sem("diff_set"), sem("e_set"), sem("summed")
    slot_set, slot_turned, slot_t_set, hid_ps, hid_set, out_ps, out_set = (
        sem(n) for n in ("slot_set", "slot_turned", "slot_t_set", "hid_ps", "hid_set", "out_ps", "out_set"))
    dve_step = sem("dve_step")
    block = ctx.enter_context(nc.Block())

    @block.gpsimd
    def _(pool):
        pool.memset(ones[:], 1.0)
        pool.memset(zeros[:], 0.0)
        pool.memset(hidden[:], 0.0).then_inc(const_set, 1)
        build_identity(pool, ident, ident_set)

    @block.sync
    def _(sp):
        for s in range(2):
            sp.dma_start(xn[:, s], d["xn"][s]).then_inc(xn_in[s], 16)
        sp.dma_start(w1[:], d["w1"]).then_inc(w_in, 16)
        sp.dma_start(w2[:], d["w2"]).then_inc(w_in, 16)
        sp.dma_start(b1[:], d["b1"]).then_inc(w_in, 16)
        for e8 in range(EXPERTS):
            p0 = (e8 % half) * per
            sp.dma_start(b2[p0:p0 + per, e8 // half, :], d["b2"][e8].partition_broadcast(per)).then_inc(w_in, 16)
        with sp.Fori(1, NC // 2) as pair:
            i = 2 * pair
            for s in range(2):
                sp.wait_ge(summed, i + (s + 1))
                sp.dma_start(xn[:, s], d["xn"][bass.ds(i + s, 1)].rearrange("a p j d -> (a p) j d")).then_inc(xn_in[s], 16)

    @block.vector
    def _(dve):
        chain = Chain(dve, dve_step, 0)
        dve.tensor_reduce(top[:], logits[:].rearrange("p c s -> p s c"), AX_X, ALU.max).then_inc(top_set, 1)
        dve.wait_ge(top_turned, 1)
        for h in range(2):
            ins = dve.tensor_reduce(top_t[:, h:h + 1], turn[:, h, 0:P], AX_X, ALU.max)
        chain.link(ins)
        dve.wait_ge(const_set, 1)
        for h in range(2):
            ins = dve.tensor_scalar(top_b[:, h, :], zeros[:], top_t[:, h:h + 1], None, ALU.add)
        ins.then_inc(topb_set, 1)
        dve.wait_ge(top_rep_ps, 1)
        dve.tensor_copy(top_rep[:].rearrange("p (h s) -> p h s", h=2), turn[:, 2:4, 0:P]).then_inc(top_rep_set, 1)
        dve.wait_ge(top_rep_set, 1)
        dve.sem_inc(diff_set, 2)
        with dve.Fori(0, NC // 2) as pair:
            i = 2 * pair
            for s in range(2):
                c = i + s
                dve.wait_ge(e_set, c + 1)
                dve.tensor_tensor(diff[:, s], logits[:, bass.ds(c * J, J), :],
                                  top_rep[:].unsqueeze(1).to_broadcast([P, J, SLOTS]), ALU.subtract).then_inc(diff_set, 1)
        dve.wait_ge(summed, NC + 2)
        chain.link(dve.reciprocal(rden[:], den[:, :, 0]))
        for h in range(2):
            ins = dve.tensor_scalar(slot_in[:, h, :], sums[:, h, :], rden[:, h:h + 1], None, ALU.mult)
        ins.then_inc(slot_set, 1)
        dve.wait_ge(slot_turned, 1)
        dve.tensor_copy(slot_t[:], turn[:, :, 0:SLOTS]).then_inc(slot_t_set, 1)
        dve.wait_ge(out_ps, 1)
        dve.wait_ge(w_in, 16 * (3 + EXPERTS))
        dve.tensor_tensor(slot_out[:], turn[:, 2:4, :], b2[:], ALU.add).then_inc(out_set, 1)
        dve.wait_ge(out_set, 1)

    @block.scalar
    def _(act):
        act.sem_inc(e_set, 2)
        with act.Fori(0, NC // 2) as pair:
            i = 2 * pair
            for s in range(2):
                c = i + s
                act.wait_ge(diff_set, c + 3)
                act.wait_ge(summed, c + 1)
                act.activation(e[:, s], diff[:, s], ACT.Exp).then_inc(e_set, 1)
        act.wait_ge(hid_ps, 1)
        act.wait_ge(w_in, 16 * (3 + EXPERTS))
        act.wait_ge(const_set, 1)
        for x in range(EXPERTS):
            p0 = (x % half) * per
            ins = act.activation(hidden[:, x, p0:p0 + per], den[:, 1, x * per:(x + 1) * per], ACT.Gelu, bias=b1[:, x:x + 1])
        ins.then_inc(hid_set, 1)

    @block.tensor
    def _(pe):
        pe.wait_ge(ident_set, 2)
        pe.wait_ge(top_set, 1)
        for h in range(2):
            mm = pe.transpose(turn[:, h, 0:P], top[:, h * P:(h + 1) * P], ident[:])
        mm.then_inc(top_turned, 1)
        pe.wait_ge(topb_set, 1)
        for h in range(2):
            mm = pe.transpose(turn[:, 2 + h, 0:P], top_b[:, h, :], ident[:])
        mm.then_inc(top_rep_ps, 1)
        pe.wait_ge(const_set, 1)
        pe.sem_inc(summed, 2)
        for h in range(2):
            pe.matmul(sums[:, h, 0:P], zeros[:], ident[:], start=True, stop=False, skip_group_check=True)
            for k in range(1, KD):
                pe.matmul(sums[:, h, k * P:(k + 1) * P], zeros[:], ident[:], start=False, stop=False, skip_group_check=True)
            pe.matmul(den[:, h, 0:1], zeros[:], ones[:], start=True, stop=False, skip_group_check=True)
        with pe.Fori(0, NC // 2) as pair:
            i = 2 * pair
            for s in range(2):
                c = i + s
                pe.wait_ge(e_set, c + 3)
                pe.wait_ge(xn_in[s], i * 8 + 16)
                for j in range(J):
                    for h in range(2):
                        pe.matmul(sums[:, h, :], e[:, s, j, h * P:(h + 1) * P], xn[:, s, j, :], start=False, stop=False, skip_group_check=True)
                        mm = pe.matmul(den[:, h, 0:1], e[:, s, j, h * P:(h + 1) * P], ones[:], start=False, stop=False, skip_group_check=True)
                mm.then_inc(summed, 1)
        pe.wait_ge(slot_set, 1)
        for k in range(KD):
            for h in range(2):
                mm = pe.transpose(turn[:, k, h * P:(h + 1) * P], slot_in[:, h, k * P:(k + 1) * P], ident[:])
        mm.then_inc(slot_turned, 1)
        pe.wait_ge(slot_t_set, 1)
        pe.wait_ge(w_in, 16 * (3 + EXPERTS))
        for x in range(EXPERTS):
            for k in range(KD):
                mm = pe.matmul(den[:, 1, x * per:(x + 1) * per], w1[:, k, x, :], slot_t[:, k, x * per:(x + 1) * per],
                               start=k == 0, stop=k == KD - 1)
        mm.then_inc(hid_ps, 1)
        pe.wait_ge(hid_set, 1)
        for x in range(EXPERTS):
            mm = pe.matmul(turn[:, 2 + x // half, :], hidden[:, x, :], w2[:, x, :], start=x % half == 0, stop=x % half == half - 1)
        mm.then_inc(out_ps, 1)


def moe_combine(nc, ctx, d, logits, slot_out):
    sb, ps, sem = makers(nc, ctx, "_c")
    ident = sb("ident", [P, P])
    eps = sb("eps", [P, 1])
    x1 = sb("x1", [P, 2, J, D_MODEL])
    neg_top = sb("neg_top", [P, 2, J])
    e = sb("e", [P, 2, J, SLOTS])
    et = sb("et", [P, 2, 2, T])
    den = sb("den", [P, 2, J])
    rden = sb("rden", [P, J])
    stats = sb("stats", [P, J, 6])
    spare = sb("spare", [P, 1])
    mv = sb("mv", [P, J, 2])
    var = sb("var", [P, J])
    sd = sb("sd", [P, J])
    mul, add = sb("mul", [P, J]), sb("add", [P, J])
    y = sb("y", [P, 2, J, D_MODEL])
    turn = ps("turn", [P, 2, T])
    mix = ps("mix", [P, J, D_MODEL])

    ident_set, eps_set = sem("ident_set"), sem("eps_set")
    x1_in = [sem(f"x1_in{s}") for s in range(2)]
    stored = [sem(f"stored{s}") for s in range(2)]
    top_set, e_set, turned, et_set, mixed, var_set, sd_set, coef_set, y_set, sum_set = (
        sem(n) for n in ("top_set", "e_set", "turned", "et_set", "mixed", "var_set", "sd_set", "coef_set", "y_set", "sum_set"))
    dve_step = sem("dve_step")
    block = ctx.enter_context(nc.Block())

    @block.gpsimd
    def _(pool):
        pool.memset(eps[:], LN_EPS).then_inc(eps_set, 1)
        build_identity(pool, ident, ident_set)
        pool.sem_inc(sum_set, 2)
        with pool.Fori(0, NC // 2) as pair:
            i = 2 * pair
            for s in range(2):
                pool.wait_ge(y_set, i + (s + 2))
                pool.wait_ge(x1_in[s], i * 8 + 16)
                pool.tensor_tensor(y[:, s], y[:, s], x1[:, s], ALU.add).then_inc(sum_set, 1)

    @block.sync
    def _(sp):
        for s in range(2):
            sp.sem_inc(stored[s], 16)
            sp.dma_start(x1[:, s], d["x1"][s]).then_inc(x1_in[s], 16)
        with sp.Fori(0, NC // 2 - 1) as pair:
            i = 2 * pair
            for s in range(2):
                sp.wait_ge(sum_set, i + (s + 3))
                sp.dma_start(d["out"][bass.ds(i + s, 1)].rearrange("a j p d -> p (a j) d"), y[:, s]).then_inc(stored[s], 16)
                sp.dma_start(x1[:, s], d["x1"][bass.ds(i + (s + 2), 1)].rearrange("a p j d -> (a p) j d")).then_inc(x1_in[s], 16)
        for s in range(2):
            sp.wait_ge(sum_set, NC + s + 1)
            sp.dma_start(d["out"][NC - 2 + s].rearrange("j p d -> p j d"), y[:, s]).then_inc(stored[s], 16)
        for s in range(2):
            sp.wait_ge(stored[s], 16 + NC * 8)

    @block.vector
    def _(dve):
        dve.sem_inc(coef_set, 1)
        dve.sem_inc(et_set, 2)
        dve.sem_inc(top_set, 2)

        def tops(c, s):
            dve.wait_ge(e_set, c + 1)
            dve.tensor_reduce(neg_top[:, s], logits[:, bass.ds(c * J, J), :], AX_X, ALU.max, negate=True).then_inc(top_set, 1)

        with dve.Fori(0, NC // 2) as pair:
            i = 2 * pair
            for s in range(2):
                c = i + s
                chain = Chain(dve, dve_step, c * 5)
                tops(c, s)
                dve.wait_ge(turned, c + 3)
                dve.wait_ge(mixed, c + 1)
                dve.tensor_copy(et[:, s], turn[:]).then_inc(et_set, 1)
                dve.wait_ge(mixed, c + 2)
                for j in range(J):
                    ins = dve.bn_stats(stats[:, j, :], mix[:, j, :])
                chain.link(ins)
                dve.memset(spare[:], 0.0)
                for j in range(J):
                    ins = dve.bn_aggr(mv[:, j, :], stats[:, j, :])
                chain.link(ins)
                chain.link(dve.reciprocal(rden[:], den[:, s]))
                chain.link(dve.tensor_tensor(var[:], mv[:, :, 1], rden[:], ALU.mult))
                dve.tensor_tensor(var[:], var[:], rden[:], ALU.mult).then_inc(var_set, 1)
                dve.wait_ge(sd_set, c + 1)
                chain.link(dve.reciprocal(mul[:], sd[:]))
                dve.tensor_tensor(mul[:], mul[:], rden[:], ALU.mult).then_inc(coef_set, 1)
                dve.wait_ge(coef_set, c * 2 + 2)
                dve.scalar_tensor_tensor(add[:], mv[:, :, 0], -1.0, mul[:], ALU.mult, ALU.mult).then_inc(coef_set, 1)

    @block.scalar
    def _(act):
        act.wait_ge(eps_set, 1)
        act.sem_inc(e_set, 2)
        act.sem_inc(y_set, 1)
        with act.Fori(0, NC // 2) as pair:
            i = 2 * pair
            for s in range(2):
                c = i + s
                act.wait_ge(top_set, c + 3)
                act.wait_ge(turned, c + 1)
                for j in range(J):
                    ins = act.activation(e[:, s, j, :], logits[:, bass.ds(c * J + j, 1), :].rearrange("p a s -> p (a s)"),
                                         ACT.Exp, bias=neg_top[:, s, j:j + 1], accum_out=den[:, s, j:j + 1])
                ins.then_inc(e_set, 1)
                act.wait_ge(var_set, c + 1)
                act.activation(sd[:], var[:], ACT.Sqrt, bias=eps[:]).then_inc(sd_set, 1)
                act.wait_ge(coef_set, c * 2 + 3)
                act.wait_ge(stored[s], i * 8 + 16)
                for j in range(J):
                    ins = act.activation(y[:, s, j, :], mix[:, j, :], ACT.Identity, scale=mul[:, j:j + 1], bias=add[:, j:j + 1])
                ins.then_inc(y_set, 1)

    @block.tensor
    def _(pe):
        pe.wait_ge(ident_set, 2)
        pe.sem_inc(turned, 2)
        pe.sem_inc(mixed, 1)
        with pe.Fori(0, NC // 2) as pair:
            i = 2 * pair
            for s in range(2):
                c = i + s
                pe.wait_ge(e_set, c + 3)
                pe.wait_ge(et_set, c + 2)
                for j in range(J):
                    for h in range(2):
                        mm = pe.transpose(turn[:, h, j * P:(j + 1) * P], e[:, s, j, h * P:(h + 1) * P], ident[:])
                mm.then_inc(turned, 1)
                pe.wait_ge(et_set, c + 3)
                pe.wait_ge(y_set, c + 1)
                for j in range(J):
                    for h in range(2):
                        mm = pe.matmul(mix[:, j, :], et[:, s, h, j * P:(j + 1) * P], slot_out[:, h, :], start=h == 0, stop=h == 1)
                mm.then_inc(mixed, 1)


def build(nc, x, in_w, par, x_w, dt_w, out_w, mu, gamma, beta, scale, w1, b1, w2, b2, out):
    d = {"x": x.rearrange("(c j p) d -> c j p d", j=J, p=P), "out": out.rearrange("(c j p) d -> c j p d", j=J, p=P),
         "w_in": in_w, "par": par, "w_x": x_w, "w_dt": dt_w, "w_out": out_w,
         "mu": mu, "gamma": gamma, "beta": beta, "scale": scale, "w1": w1, "b1": b1, "w2": w2, "b2": b2}
    for name, shape in (("xt", [(LAYERS + 1) * NC, P, KD, T]), ("b_rows", [LAYERS * NC, STATES, T]),
                        ("res", [NC, P, J, D_MODEL]), ("x1", [NC, P, J, D_MODEL]), ("xn", [NC, P, J, D_MODEL])):
        d[name] = nc.dram_tensor(name, shape, F32, kind="Internal").ap()
    with ExitStack() as ctx:
        norm_input(nc, ctx, d)
    with ExitStack() as ctx:
        mamba_stack(nc, ctx, d)
    with ExitStack() as keep:
        logits = keep.enter_context(nc.sbuf_tensor("logits", [P, NC * J, SLOTS], F32))
        slot_out = keep.enter_context(nc.sbuf_tensor("slot_out", [P, 2, D_MODEL], F32))
        with ExitStack() as ctx:
            moe_logits(nc, ctx, d, logits)
        with ExitStack() as ctx:
            moe_dispatch(nc, ctx, d, logits, slot_out)
        with ExitStack() as ctx:
            moe_combine(nc, ctx, d, logits, slot_out)


def kernel(**inputs):
    import numpy as _np
    import concourse.bacc as _bacc
    from concourse import mybir as _mybir
    from concourse.bass_utils import run_bass_kernel_spmd as _run

    a = {name.split("_", 1)[1]: _np.asarray(v) for name, v in inputs.items()}

    def rows_in(m, blocks):
        return m.transpose(0, 2, 1).reshape(LAYERS, blocks, P, m.shape[1]).transpose(0, 2, 1, 3)

    def per_channel(m):
        return m.reshape(LAYERS, NB, P, -1)

    par = _np.concatenate([per_channel(a["attn_" + n]) for n in ("A_log", "conv_w", "conv_b", "dt_proj_b", "D")], axis=-1)
    arrays = {
        "x": a["attn_x"].reshape(SEQ, D_MODEL),
        "in_w": rows_in(a["attn_in_proj_w"], KD),
        "par": par.transpose(0, 2, 1, 3),
        "x_w": rows_in(a["attn_x_proj_w"], NB),
        "dt_w": a["attn_dt_proj_w"].transpose(0, 2, 1),
        "out_w": rows_in(a["attn_out_proj_w"], NB),
        "mu": a["ffn_mu"].reshape(KD, P, SLOTS).transpose(1, 0, 2),
        "gamma": a["ffn_ln_gamma"],
        "beta": a["ffn_ln_beta"],
        "scale": a["ffn_scale"],
        "w1": a["ffn_w1"].reshape(EXPERTS, KD, P, HID).transpose(2, 1, 0, 3),
        "b1": a["ffn_b1"].transpose(1, 0),
        "w2": a["ffn_w2"].transpose(1, 0, 2),
        "b2": a["ffn_b2"],
    }
    nc = _bacc.Bacc("TRN2", target_bir_lowering=False, num_devices=1, dynamic_dma_scratch_size=256)
    ins, args = {}, []
    for name, v in arrays.items():
        v = _np.ascontiguousarray(v)
        ins[f"in_{name}_dram"] = v
        args.append(nc.dram_tensor(f"in_{name}_dram", v.shape, _mybir.dt.from_np(v.dtype), kind="ExternalInput").ap())
    args.append(nc.dram_tensor("out_0_dram", (SEQ, D_MODEL), F32, kind="ExternalOutput").ap())
    build(nc, *args)
    r = _run(nc, [ins], core_ids=[0])
    return r.results[0]["out_0_dram"].reshape(1, SEQ, D_MODEL)
```

```python
from contextlib import ExitStack

import concourse.bass as bass
from concourse import mybir

ALU = mybir.AluOpType
ACT = mybir.ActivationFunctionType
AX_X = mybir.AxisListType.X
F32 = mybir.dt.float32

P = 128
D_MODEL = 512
D_INNER = 1024
STATES = 16
TAPS = 4
RANK = 32
SEQ = 8192
LAYERS = 2
T = 512
J = T // P
NC = SEQ // T
KD = D_MODEL // P
NB = D_INNER // P
HB = NB // 2
GROUPS = 2 * STATES
SCANS = GROUPS * HB
XD = RANK + 2 * STATES
PAR = STATES + TAPS + 3
LN_EPS = 1e-5
NORM_EPS = 1e-12
EXPERTS = 16
SLOTS = 256
HID = 128

PROJ_TILES = 4 * NB + 4 + 2
PROJ_PROLOGUE = 2 * NB + 2 + HB
PROJ_FIRST = PROJ_TILES - 4
TURN_TILES = SCANS + NB
TURN_FIRST = SCANS + HB

C_SCAN, C_BU, C_EXP, C_TURN, C_PROJ, C_HS, C_Y, C_W, C_XC = 4, SCANS, SCANS, 4, 8, GROUPS, NB, NB, NB


CONV_HALF_AT = (0, 1, 6, 7, 11, 12, 16, 17)
CONV_AT = (2, 3, 8, 9, 13, 14, 18, 19)
OUT_AT = (4, 10, 15, 20)
X_PROJ_AT = 21
GATE_AT = (22, 23, 24, 25, 26, 27, 28, 29)
DELTA_AT = (0, 1, 2, 3)
TURN_C_AT = 23
DELTA_NEXT_AT = (24, 25, 26, 27)
TURN_Y_BEFORE_AT = (1, 2)
TURN_Y_AT = (28, 29)
ITEM_LAG, SMALL_LAG = 3, 2
DELTA_W_AT = (8, 9, 10, 11)
DELTA_W_NEXT_AT = (30, 31)


class Tally:

    def __init__(self, base):
        self.base, self.n = base, 0

    def at(self, extra):
        return self.base + (self.n + extra)


def body_kinds(eng, run):
    run(0, True, False)
    with eng.Fori(1, NC - 1) as c:
        run(c, False, False)
    run(NC - 1, False, True)


def mamba_stack(nc, ctx, d):
    def sb(name, shape):
        return ctx.enter_context(nc.sbuf_tensor(name, shape, F32))

    def ps(name, shape):
        return ctx.enter_context(nc.psum_tensor(name, shape, F32))

    def sem(name):
        return ctx.enter_context(nc.semaphore(name))

    w_in = sb("w_in", [P, KD, 2 * D_INNER])
    w_out = sb("w_out", [P, NB, D_MODEL])
    w_x = sb("w_x", [P, NB, XD])
    w_dt = sb("w_dt", [RANK, D_INNER])
    par = sb("par", [P, NB, PAR])
    neg_a = sb("neg_a", [P, NB, STATES])
    conv_diag = sb("conv_diag", [P, 2, TAPS, P])
    ident = sb("ident_m", [P, P])
    zeros = sb("zeros_m", [P, NB * 3])
    x_conv = sb("x_conv", [P, KD, T])
    x_gate = sb("x_gate", [P, KD, T])
    conv_in = sb("conv_in", [P, 2, 3 + T])
    halo = sb("halo", [P, NB, 3])
    u = sb("u", [P, NB, T])
    delta = sb("delta", [P, NB, T])
    w = sb("w", [P, NB, T])
    ud = sb("ud", [P, NB, T])
    zy = sb("zy", [P, NB, T])
    xdbl = sb("xdbl", [P, T])
    c_next = sb("c_next", [P, J, STATES])
    c_now = sb("c_now", [P, J, STATES])
    b_rep = sb("b_rep", [P, 4, T])
    bu = sb("bu", [P, 4, T])
    h = sb("h", [P, 2, HB, T])
    h_last = sb("h_last", [P, GROUPS * HB])
    acc = sb("acc", [P, 2, J, HB * P])
    stage = sb("stage", [P, 2, T])
    spare = sb("spare_m", [P, 1])

    decay = ps("decay", [P, HB, T])
    turn = ps("turn", [P, 2, T])
    proj = ps("proj", [P, 2, T])

    weights_in = sem("weights_in")
    xconv_in = sem("xconv_in")
    xgate_in = sem("xgate_in")
    brep_in = [sem(f"brep_in{r}") for r in range(4)]
    b_stored = sem("b_stored")
    out_stored = [sem(f"out_stored{r}") for r in range(2)]
    ident_set = sem("ident_set")
    zeros_set = sem("zeros_set")
    hz_set = sem("hz_set")
    a_set = sem("a_set")
    halo_set = sem("halo_set")
    proj_full = sem("proj_full")
    proj_done = sem("proj_done")
    convin_set = sem("convin_set")
    u_set = sem("u_set")
    xdbl_set = sem("xdbl_set")
    exp_set = sem("exp_set")
    z_set = sem("z_set")
    softplus_set = sem("softplus_set")
    delta_set = sem("delta_set")
    w_set = sem("w_set")
    ud_set = sem("ud_set")
    decay_set = sem("decay_set")
    bu_set = sem("bu_set")
    scanned = sem("scanned")
    turn_full = sem("turn_full")
    turn_done = sem("turn_done")
    hlast_set = sem("hlast_set")
    c_set = sem("c_set")
    y_set = sem("y_set")

    N_W = 5
    block = ctx.enter_context(nc.Block())

    def proj_base(l, c, first):
        if first:
            return l * (NC * PROJ_TILES) + PROJ_PROLOGUE
        return l * (NC * PROJ_TILES) + c * PROJ_TILES + (PROJ_PROLOGUE + PROJ_FIRST - PROJ_TILES)

    def turn_base(l, c, first):
        if first:
            return l * (NC * TURN_TILES)
        return l * (NC * TURN_TILES) + c * TURN_TILES + (TURN_FIRST - TURN_TILES)

    @block.sync
    def _(sp):
        sp.sem_inc(b_stored, 16)
        with sp.Fori(0, LAYERS) as l:
            for r in range(2):
                sp.wait_ge(out_stored[r], l * (NC * 2 * 16) + 16)
            sp.dma_start(w_in[:], d["w_in"][bass.ds(l, 1)].rearrange("a p k e -> (a p) k e")).then_inc(weights_in, 16)
            sp.dma_start(par[:], d["par"][bass.ds(l, 1)].rearrange("a p b n -> (a p) b n")).then_inc(weights_in, 16)
            sp.dma_start(w_x[:], d["w_x"][bass.ds(l, 1)].rearrange("a p b n -> (a p) b n")).then_inc(weights_in, 16)
            sp.dma_start(w_dt[:], d["w_dt"][bass.ds(l, 1)].rearrange("a p n -> (a p) n")).then_inc(weights_in, 16)
            sp.dma_start(w_out[:], d["w_out"][bass.ds(l, 1)].rearrange("a p b n -> (a p) b n")).then_inc(weights_in, 16)

            def load_x(dst, G, done):
                sp.dma_start(dst[:], d["xt"][bass.ds(G, 1)].rearrange("a p k t -> (a p) k t")).then_inc(done, 16)

            def load_b(G, k):
                sp.wait_ge(bu_set, G * SCANS + (4 * (k - 4) + 4 + C_BU))
                if k == 0:
                    sp.wait_ge(b_stored, G * 16 + 32)
                n = k % STATES
                src = d["b_rows"][bass.ds(G, 1), n, :].rearrange("a t -> (a t)").partition_broadcast(P)
                sp.dma_start(b_rep[:, k % 4, :], src).then_inc(brep_in[k % 4], 16)

            load_x(x_conv, l * NC, xconv_in)

            def body(c, first, last):
                G = l * NC + c
                for k in range(GROUPS):
                    load_b(G, k)
                    if k == 3 and not last:
                        sp.wait_ge(convin_set, G * NB + NB + C_XC)
                        load_x(x_conv, G + 1, xconv_in)
                    if k == 8:
                        sp.wait_ge(decay_set, G * SCANS + C_EXP)
                        load_x(x_gate, G, xgate_in)

            body_kinds(sp, body)
        for r in range(2):
            sp.wait_ge(out_stored[r], 16 + LAYERS * NC * 2 * 16)

    @block.tensor
    def _(pe):
        pe.wait_ge(ident_set, 2)
        with pe.Fori(0, LAYERS) as l:
            pe.wait_ge(weights_in, l * (16 * N_W) + 16 * N_W)

            def bank(pj):
                pe.wait_ge(proj_done, pj.at(C_PROJ - 1))
                return proj[:, pj.n % 2, :]

            def full(pj, mm):
                mm.then_inc(proj_full, 1)
                pj.n += 1

            def parts(pj, operands, part, count):
                lo, hi = part
                out = proj[:, pj.n % 2, :] if lo else bank(pj)
                for n in range(lo, hi):
                    lhs, rhs = operands(n)
                    mm = pe.matmul(out[0:lhs.shape[1], :], lhs, rhs, start=n == 0, stop=n == count - 1)
                if hi == count:
                    full(pj, mm)

            def conv_half(pj, X, b, part=(0, KD)):
                if b == 0 and part[0] == 0:
                    pe.wait_ge(xconv_in, X * 16 + 16)
                parts(pj, lambda k: (w_in[:, k, b * P:(b + 1) * P], x_conv[:, k, :]), part, KD)

            def conv(pj, X, b, part=(0, TAPS)):
                if part[0] == 0:
                    pe.wait_ge(convin_set, X * NB + (b + 1 + C_XC))
                parts(pj, lambda k: (conv_diag[:, b % 2, k, :], conv_in[:, b % 2, k:k + T]), part, TAPS)

            def x_proj(pj, X, part=(0, NB)):
                if part[0] == 0:
                    pe.wait_ge(u_set, X * 2 + 2)
                parts(pj, lambda b: (w_x[:, b, :], u[:, b, :]), part, NB)

            def gate(pj, G, b, part):
                if b == 0 and part[0] == 0:
                    pe.wait_ge(xgate_in, G * 16 + 16)
                parts(pj, lambda k: (w_in[:, k, D_INNER + b * P:D_INNER + (b + 1) * P], x_gate[:, k, :]), part, KD)

            def out_proj(pj, G, o, part=(0, NB)):
                if o == 0 and part[0] == 0:
                    pe.wait_ge(y_set, G * NB + (NB + C_Y))
                parts(pj, lambda b: (w_out[:, b, o * P:(o + 1) * P], zy[:, b, :]), part, NB)

            def turn_c(pj, X):
                pe.wait_ge(xdbl_set, X + 1)
                out = bank(pj)
                for j in range(J):
                    mm = pe.transpose(out[:, j * P:(j + 1) * P], xdbl[:, j * P:(j + 1) * P], ident[:])
                full(pj, mm)

            def delta_proj(pj, b):
                out = bank(pj)
                full(pj, pe.matmul(out, w_dt[:, b * P:(b + 1) * P], xdbl[0:RANK, :], start=True, stop=True))

            def turn_states(tn, G, k, j):
                if j == 0:
                    pe.wait_ge(scanned, G * SCANS + (4 * k + 4 + C_SCAN))
                pe.wait_ge(turn_done, tn.at(C_TURN - 1))
                for b in range(HB):
                    mm = pe.transpose(turn[:, tn.n % 2, b * P:(b + 1) * P], h[:, k % 2, b, j * P:(j + 1) * P], ident[:])
                mm.then_inc(turn_full, 1)
                tn.n += 1

            def turn_y(tn, hf, sums, blocks):
                pe.wait_ge(turn_done, tn.base + (sums + C_TURN))
                for b in blocks:
                    pe.wait_ge(turn_done, tn.at(C_TURN - 1))
                    for j in range(J):
                        mm = pe.transpose(turn[:, tn.n % 2, j * P:(j + 1) * P], acc[:, hf, j, b * P:(b + 1) * P], ident[:])
                    mm.then_inc(turn_full, 1)
                    tn.n += 1

            pj = Tally(l * (NC * PROJ_TILES))
            X = l * NC
            for b in range(0, NB, 2):
                conv_half(pj, X, b)
                conv_half(pj, X, b + 1)
                conv(pj, X, b)
                conv(pj, X, b + 1)
            x_proj(pj, X)
            turn_c(pj, X)
            for b in range(HB):
                delta_proj(pj, b)

            def body(c, first, last):
                G = l * NC + c
                pj = Tally(proj_base(l, c, first))
                tn = Tally(turn_base(l, c, first))
                half0 = 0
                for k in range(GROUPS):
                    small = True
                    for j in range(J):
                        turn_states(tn, G, k, j)
                        if j == 0:
                            if k in DELTA_AT:
                                delta_proj(pj, HB + DELTA_AT.index(k))
                            elif k == TURN_C_AT and not last:
                                turn_c(pj, G + 1)
                            elif k in DELTA_NEXT_AT and not last:
                                delta_proj(pj, DELTA_NEXT_AT.index(k))
                            else:
                                small = False
                        lo, hi = ((0, 0, 1, 2)[j], (0, 1, 2, 4)[j]) if small else (j, j + 1)
                        if lo == hi:
                            continue
                        if not last and k in CONV_HALF_AT:
                            conv_half(pj, G + 1, CONV_HALF_AT.index(k), (lo, hi))
                        if not last and k in CONV_AT:
                            conv(pj, G + 1, CONV_AT.index(k), (lo, hi))
                        if not first and k in OUT_AT:
                            out_proj(pj, G - 1, OUT_AT.index(k), (2 * lo, 2 * hi))
                        if not last and k == X_PROJ_AT:
                            x_proj(pj, G + 1, (2 * lo, 2 * hi))
                        if k in GATE_AT:
                            gate(pj, G, GATE_AT.index(k), (lo, hi))
                    if k == STATES - 1:
                        half0 = tn.n
                    if k in TURN_Y_BEFORE_AT and not first:
                        b = 2 * TURN_Y_BEFORE_AT.index(k)
                        turn_y(tn, 1, 0, (b, b + 1))
                    if k in TURN_Y_AT:
                        b = 2 * TURN_Y_AT.index(k)
                        turn_y(tn, 0, half0, (b, b + 1))

            body_kinds(pe, body)

            pj = Tally(l * (NC * PROJ_TILES) + (NC * PROJ_TILES - 4))
            tn = Tally(l * (NC * TURN_TILES) + (NC * TURN_TILES - HB))
            turn_y(tn, 1, 0, range(HB))
            for o in range(KD):
                out_proj(pj, X + (NC - 1), o)

    @block.scalar
    def _(act):
        act.sem_inc(proj_done, C_PROJ)
        act.sem_inc(decay_set, C_EXP)
        act.sem_inc(convin_set, C_XC)
        act.sem_inc(ud_set, C_W)
        for r in range(2):
            act.sem_inc(out_stored[r], 16)
        act.wait_ge(zeros_set, 1)
        act.wait_ge(ident_set, 2)
        with act.Fori(0, LAYERS) as l:
            act.wait_ge(weights_in, l * (16 * N_W) + 16 * N_W)
            act.activation(neg_a[:], par[:, :, 0:STATES], ACT.Exp).then_inc(a_set, 1)
            act.wait_ge(a_set, 2 * l + 1)
            act.mul(neg_a[:], neg_a[:], -1.0).then_inc(a_set, 1)
            act.copy(halo[:].rearrange("p b t -> p (b t)"), zeros[:]).then_inc(halo_set, 1)
            act.wait_ge(a_set, 2 * l + 2)
            act.wait_ge(halo_set, l + 1)
            conv_bias, dt_bias = STATES + TAPS, STATES + TAPS + 1

            def take(pj):
                act.wait_ge(proj_full, pj.at(1))
                return proj[:, pj.n % 2, :]

            def done(pj, ins):
                ins.then_inc(proj_done, 1)
                pj.n += 1

            def conv_half(pj, X, b):
                src = take(pj)
                act.wait_ge(proj_done, pj.at(C_PROJ - 1))
                act.copy(conv_in[:, b % 2, 0:3], halo[:, b, :])
                for k in range(TAPS):
                    act.activation(conv_diag[:, b % 2, k, :], ident[:], ACT.Copy, scale=par[:, b, STATES + k:STATES + k + 1])
                act.copy(conv_in[:, b % 2, 3:3 + T], src).then_inc(convin_set, 1)
                act.wait_ge(convin_set, X * NB + (b + 1 + C_XC))
                done(pj, act.copy(halo[:, b, :], src[:, T - 3:T]))

            def conv(pj, X, b):
                act.wait_ge(w_set, X * NB + (b + 1))
                act.wait_ge(ud_set, X * NB + (b + 1))
                done(pj, act.activation(u[:, b, :], take(pj), ACT.Identity, bias=par[:, b, conv_bias:conv_bias + 1]))

            def silu_u(pj, hf):
                act.wait_ge(proj_done, pj.at(C_PROJ))
                act.activation(u[:, hf * HB:hf * HB + HB, :], u[:, hf * HB:hf * HB + HB, :], ACT.Silu).then_inc(u_set, 1)

            def x_proj(pj, X):
                act.wait_ge(b_stored, X * 16 + 16)
                out = take(pj)
                act.copy(xdbl[0:XD, :], out[0:XD, :]).then_inc(xdbl_set, 1)
                act.wait_ge(xdbl_set, X + 1)
                act.dma_start(d["b_rows"][bass.ds(X, 1)].rearrange("a n t -> (a n) t"),
                              xdbl[RANK:RANK + STATES, :]).then_inc(b_stored, 16)
                done(pj, act.copy(spare[:], out[:, 0:1]))

            def turn_c(pj, X):
                act.wait_ge(c_set, X + 1)
                src = take(pj).rearrange("p (j r) -> p j r", j=J)
                done(pj, act.copy(c_next[:], src[:, :, RANK + STATES:XD]))

            def delta_proj(pj, X, b):
                src = take(pj)
                bias = par[:, b, dt_bias:dt_bias + 1]
                if b % HB == 0:
                    act.wait_ge(w_set, X * NB + (b + HB))
                    act.wait_ge(decay_set, X * SCANS + (b // HB * (SCANS // 2) - SCANS // 2 + C_EXP))
                    act.wait_ge(bu_set, X * SCANS + (b // HB * (SCANS // 2) - SCANS // 2 + C_BU))
                act.activation(w[:, b, :], src, ACT.Abs, bias=bias)
                done(pj, act.activation(delta[:, b, :], src, ACT.Relu, bias=bias))

            def softplus_exp(pj, X, hf):
                act.wait_ge(proj_done, pj.at(C_PROJ))
                act.activation(w[:, hf * HB:hf * HB + HB, :], w[:, hf * HB:hf * HB + HB, :], ACT.Exp, scale=-1.0).then_inc(exp_set, 1)

            def softplus_ln(X, hf):
                act.wait_ge(exp_set, X * 2 + (hf + 1))
                act.activation(w[:, hf * HB:hf * HB + HB, :], w[:, hf * HB:hf * HB + HB, :], ACT.Ln, bias=1.0).then_inc(softplus_set, 1)

            def skip(X, b):
                act.wait_ge(y_set, X * NB + (b + 1))
                act.activation(ud[:, b, :], u[:, b, :], ACT.Copy, scale=par[:, b, PAR - 1:PAR]).then_inc(ud_set, 1)

            def gate(pj, G, b):
                done(pj, act.copy(zy[:, b, :], take(pj)))

            def silu_z(pj, hf):
                act.wait_ge(proj_done, pj.at(C_PROJ))
                act.activation(zy[:, hf * HB:hf * HB + HB, :], zy[:, hf * HB:hf * HB + HB, :], ACT.Silu).then_inc(z_set, 1)

            def out_proj(pj, G, o):
                act.wait_ge(out_stored[o % 2], G * 32 + (o // 2 * 16 + 16))
                done(pj, act.copy(stage[:, o % 2, :], take(pj)))
                act.wait_ge(proj_done, pj.at(C_PROJ))
                act.dma_start(d["xt"][bass.ds(G + NC, 1), :, o, :].rearrange("a p t -> (a p) t"),
                              stage[:, o % 2, :]).then_inc(out_stored[o % 2], 16)

            def decay_of(G, k, b):
                hf, n = divmod(k, STATES)
                blk = hf * HB + b
                act.wait_ge(scanned, G * SCANS + (4 * k + b + 1))
                if n == 0:
                    act.wait_ge(delta_set, G * NB + (blk + 1))
                act.activation(decay[:, b, :], delta[:, blk, :], ACT.Exp,
                               scale=neg_a[:, blk, n:n + 1]).then_inc(decay_set, 1)

            pj = Tally(l * (NC * PROJ_TILES))
            X = l * NC
            for b in range(0, NB, 2):
                conv_half(pj, X, b)
                conv_half(pj, X, b + 1)
                conv(pj, X, b)
                conv(pj, X, b + 1)
            silu_u(pj, 0)
            silu_u(pj, 1)
            x_proj(pj, X)
            turn_c(pj, X)
            for b in range(HB):
                delta_proj(pj, X, b)
            softplus_exp(pj, X, 0)
            softplus_ln(X, 0)

            def body(c, first, last):
                G = l * NC + c
                pj = Tally(proj_base(l, c, first))
                for k in range(GROUPS):
                    decay_of(G, k, 0)
                    item, small = k - ITEM_LAG, k - SMALL_LAG
                    if not last and item in CONV_HALF_AT:
                        conv_half(pj, G + 1, CONV_HALF_AT.index(item))
                    if not last and item in CONV_AT:
                        b = CONV_AT.index(item)
                        conv(pj, G + 1, b)
                        if b % HB == HB - 1:
                            silu_u(pj, b // HB)
                    if not first and item in OUT_AT:
                        out_proj(pj, G - 1, OUT_AT.index(item))
                    if not last and item == X_PROJ_AT:
                        x_proj(pj, G + 1)
                    if item in GATE_AT:
                        b = GATE_AT.index(item)
                        gate(pj, G, b)
                        if b == HB - 1:
                            silu_z(pj, 0)
                    if small == DELTA_AT[-1] + 1:
                        softplus_ln(G, 1)
                    if not last and small == DELTA_NEXT_AT[-1] + 1:
                        softplus_ln(G + 1, 0)
                    for b in range(1, HB):
                        decay_of(G, k, b)
                    if small in DELTA_AT:
                        delta_proj(pj, G, HB + DELTA_AT.index(small))
                    if small == DELTA_AT[-1]:
                        softplus_exp(pj, G, 1)
                    if not last and small == TURN_C_AT:
                        turn_c(pj, G + 1)
                    if not last and small in DELTA_NEXT_AT:
                        delta_proj(pj, G + 1, DELTA_NEXT_AT.index(small))
                    if not last and small == DELTA_NEXT_AT[-1]:
                        softplus_exp(pj, G + 1, 0)
                    if 1 <= k <= NB:
                        skip(G, k - 1)
                    if k == GROUPS - 1:
                        gate(pj, G, NB - 1)
                        silu_z(pj, 1)

            body_kinds(act, body)
            pj = Tally(l * (NC * PROJ_TILES) + (NC * PROJ_TILES - 4))
            for o in range(KD):
                out_proj(pj, X + (NC - 1), o)

    @block.gpsimd
    def _(pool):
        pool.sem_inc(bu_set, C_BU)
        pool.sem_inc(w_set, C_W)
        pool.memset(zeros[:], 0.0)
        pool.memset(xdbl[:], 0.0).then_inc(zeros_set, 1)
        pool.memset(ident[:], 0.0).then_inc(ident_set, 1)
        pool.wait_ge(ident_set, 1)
        pool.affine_select(out=ident[:], in_=ident[:], compare_op=ALU.not_equal, fill=1.0, base=0,
                           pattern=[[-1, P]], channel_multiplier=1).then_inc(ident_set, 1)
        pool.wait_ge(ident_set, 2)
        with pool.Fori(0, LAYERS) as l:
            pool.wait_ge(weights_in, l * (16 * N_W) + 16 * N_W)

            def delta_w(X, b):
                pool.wait_ge(softplus_set, X * 2 + (b // HB + 1))
                pool.tensor_tensor(delta[:, b, :], delta[:, b, :], w[:, b, :], ALU.add).then_inc(delta_set, 1)
                pool.wait_ge(delta_set, X * NB + (b + 1))
                pool.tensor_tensor(w[:, b, :], delta[:, b, :], u[:, b, :], ALU.mult).then_inc(w_set, 1)

            def input_of(G, k, b):
                hf, n = divmod(k, STATES)
                blk = hf * HB + b
                if b == 0:
                    pool.wait_ge(brep_in[k % 4], G * (GROUPS * 4) + (k // 4 + 1) * 16)
                if n == 0:
                    pool.wait_ge(w_set, G * NB + (blk + 1 + C_W))
                pool.wait_ge(scanned, G * SCANS + (4 * k + b + 1))
                pool.tensor_tensor(bu[:, b, :], w[:, blk, :], b_rep[:, k % 4, :], ALU.mult).then_inc(bu_set, 1)

            X = l * NC
            for b in range(HB):
                delta_w(X, b)

            def body(c, first, last):
                G = l * NC + c
                for k in range(GROUPS):
                    for b in range(HB):
                        input_of(G, k, b)
                    if k in DELTA_W_AT:
                        delta_w(G, HB + DELTA_W_AT.index(k))
                    if not last and k in DELTA_W_NEXT_AT:
                        b = 2 * DELTA_W_NEXT_AT.index(k)
                        delta_w(G + 1, b)
                        delta_w(G + 1, b + 1)

            body_kinds(pool, body)

    @block.vector
    def _(dve):
        dve.sem_inc(scanned, C_SCAN)
        dve.sem_inc(turn_done, C_TURN)
        dve.sem_inc(hlast_set, C_HS)
        dve.sem_inc(y_set, C_Y)
        dve.sem_inc(c_set, 1)
        with dve.Fori(0, LAYERS) as l:
            dve.wait_ge(hlast_set, l * (NC * GROUPS) + C_HS)
            dve.memset(h_last[:], 0.0).then_inc(hz_set, 1)
            dve.wait_ge(hz_set, l + 1)

            def scan(G, k, b):
                dve.wait_ge(decay_set, G * SCANS + (4 * k + b + 1 + C_EXP))
                dve.wait_ge(bu_set, G * SCANS + (4 * k + b + 1 + C_BU))
                if b == 0:
                    dve.wait_ge(hlast_set, G * GROUPS + (k + 1))
                dve.tensor_tensor_scan(h[:, k % 2, b, :], decay[:, b, :], bu[:, b, :],
                                       h_last[:, 4 * k + b:4 * k + b + 1], ALU.mult, ALU.add).then_inc(scanned, 1)

            def save_last(G, k):
                dve.wait_ge(scanned, G * SCANS + (4 * k + 4 + C_SCAN))
                dve.tensor_copy(h_last[:, 4 * k:4 * k + HB], h[:, k % 2, :, T - 1]).then_inc(hlast_set, 1)

            def add_state(tn, k, j):
                hf, n = divmod(k, STATES)
                dve.wait_ge(turn_full, tn.at(1))
                dve.wait_ge(turn_done, tn.at(C_TURN - 3))
                scalar = c_now[:, j, n:n + 1]
                if n == 0:
                    ins = dve.tensor_scalar(acc[:, hf, j, :], turn[:, tn.n % 2, :], scalar, None, ALU.mult)
                else:
                    ins = dve.scalar_tensor_tensor(acc[:, hf, j, :], turn[:, tn.n % 2, :], scalar, acc[:, hf, j, :],
                                                   ALU.mult, ALU.add)
                ins.then_inc(turn_done, 1)
                tn.n += 1

            def finish_y(tn, G, blocks):
                for b in blocks:
                    dve.wait_ge(z_set, G * 2 + (b // HB + 1))
                    dve.wait_ge(turn_full, tn.at(1))
                    dve.wait_ge(ud_set, G * NB + (b + 1 + C_W))
                    dve.tensor_tensor(ud[:, b, :], turn[:, tn.n % 2, :], ud[:, b, :], ALU.add).then_inc(turn_done, 1)
                    tn.n += 1
                    dve.wait_ge(turn_done, tn.at(C_TURN))
                    dve.tensor_tensor(zy[:, b, :], ud[:, b, :], zy[:, b, :], ALU.mult).then_inc(y_set, 1)

            def body(c, first, last):
                G = l * NC + c
                tn = Tally(turn_base(l, c, first))
                if not first:
                    tn.n = -4
                for k in range(GROUPS):
                    if k == 1:
                        dve.wait_ge(turn_done, tn.at(C_TURN))
                        dve.tensor_copy(c_now[:], c_next[:]).then_inc(c_set, 1)
                        dve.wait_ge(c_set, G + 2)
                    for b in range(HB):
                        scan(G, k, b)
                        if b == 0 and k > 0:
                            save_last(G, k - 1)
                        if b == 0 and k == 0 and not first:
                            save_last(G - 1, GROUPS - 1)
                        if k > 0:
                            add_state(tn, k - 1, b)
                        elif not first:
                            add_state(tn, GROUPS - 1, b)
                    if k - 1 in TURN_Y_BEFORE_AT and not first:
                        b = HB + 2 * TURN_Y_BEFORE_AT.index(k - 1)
                        finish_y(tn, G - 1, (b, b + 1))
                    if k - 1 in TURN_Y_AT:
                        b = 2 * TURN_Y_AT.index(k - 1)
                        finish_y(tn, G, (b, b + 1))

            body_kinds(dve, body)
            G = l * NC + (NC - 1)
            tn = Tally(l * (NC * TURN_TILES) + (NC * TURN_TILES - HB))
            tn.n = -4
            save_last(G, GROUPS - 1)
            for j in range(J):
                add_state(tn, GROUPS - 1, j)
            finish_y(tn, G, range(HB, NB))


class Chain:

    def __init__(self, eng, sem, base):
        self.eng, self.sem, self.base, self.n = eng, sem, base, 0

    def link(self, ins):
        ins.then_inc(self.sem, 1)
        self.n += 1
        self.eng.wait_ge(self.sem, self.base + self.n)


def makers(nc, ctx, tag):
    def sb(name, shape):
        return ctx.enter_context(nc.sbuf_tensor(name + tag, shape, F32))

    def ps(name, shape):
        return ctx.enter_context(nc.psum_tensor(name + tag, shape, F32))

    def sem(name):
        return ctx.enter_context(nc.semaphore(name + tag))

    return sb, ps, sem


def build_identity(pool, ident, ident_set):
    pool.memset(ident[:], 0.0).then_inc(ident_set, 1)
    pool.wait_ge(ident_set, 1)
    pool.affine_select(out=ident[:], in_=ident[:], compare_op=ALU.not_equal, fill=1.0, base=0,
                       pattern=[[-1, P]], channel_multiplier=1).then_inc(ident_set, 1)


def moments(dve, chain, stats, mv, rows, spare):
    for j in range(J):
        ins = dve.bn_stats(stats[:, j, :], rows[:, j, :])
    chain.link(ins)
    dve.memset(spare[:], 0.0)
    for j in range(J):
        ins = dve.bn_aggr(mv[:, j, :], stats[:, j, :])
    return ins


def norm_input(nc, ctx, d):
    sb, ps, sem = makers(nc, ctx, "_n")
    ident = sb("ident", [P, P])
    eps = sb("eps", [P, 1])
    x = sb("x", [P, 2, J, D_MODEL])
    xn = sb("xn", [P, 2, J, D_MODEL])
    xt = sb("xt", [P, 2, KD, T])
    stats = sb("stats", [P, J, 6])
    spare = sb("spare", [P, 1])
    mv = sb("mv", [P, J, 2])
    sd = sb("sd", [P, J])
    rstd = sb("rstd", [P, J])
    turn = ps("turn", [P, 2, KD, T])

    ident_set, eps_set = sem("ident_set"), sem("eps_set")
    x_in = [sem(f"x_in{s}") for s in range(2)]
    res_stored = [sem(f"res_stored{s}") for s in range(2)]
    xt_stored = [sem(f"xt_stored{s}") for s in range(2)]
    mv_set, sd_set, xn_set = sem("mv_set"), sem("sd_set"), sem("xn_set")
    turned, xt_set = sem("turned"), sem("xt_set")
    dve_step = sem("dve_step")
    block = ctx.enter_context(nc.Block())

    @block.gpsimd
    def _(pool):
        pool.memset(eps[:], LN_EPS).then_inc(eps_set, 1)
        build_identity(pool, ident, ident_set)

    @block.sync
    def _(sp):
        with sp.Fori(0, NC // 2) as pair:
            i = 2 * pair
            for s in range(2):
                sp.wait_ge(xn_set, i + (s + 1))
                sp.dma_start(x[:, s], d["x"][bass.ds(i + s, 1)].rearrange("a j p d -> p (a j) d")).then_inc(x_in[s], 16)

    @block.vector
    def _(dve):
        dve.sem_inc(xn_set, 2)
        with dve.Fori(0, NC // 2) as pair:
            i = 2 * pair
            for s in range(2):
                chain = Chain(dve, dve_step, (i + s) * 2)
                dve.wait_ge(x_in[s], i * 8 + 16)
                moments(dve, chain, stats, mv, x[:, s], spare).then_inc(mv_set, 1)
                dve.wait_ge(sd_set, i + (s + 1))
                chain.link(dve.reciprocal(rstd[:], sd[:]))
                dve.wait_ge(res_stored[s], i * 8 + 16)
                dve.wait_ge(turned, i + (s + 1))
                for j in range(J):
                    ins = dve.tensor_scalar(xn[:, s, j, :], x[:, s, j, :], mv[:, j, 0:1], rstd[:, j:j + 1],
                                            ALU.subtract, ALU.mult)
                ins.then_inc(xn_set, 1)

    @block.scalar
    def _(act):
        act.wait_ge(eps_set, 1)
        act.sem_inc(xt_set, 2)
        for s in range(2):
            act.sem_inc(res_stored[s], 16)
            act.sem_inc(xt_stored[s], 16)
        with act.Fori(0, NC // 2) as pair:
            i = 2 * pair
            for s in range(2):
                act.wait_ge(mv_set, i + (s + 1))
                act.activation(sd[:], mv[:, :, 1], ACT.Sqrt, bias=eps[:]).then_inc(sd_set, 1)
                act.wait_ge(turned, i + (s + 3))
                act.wait_ge(xt_stored[s], i * 8 + 16)
                act.copy(xt[:, s], turn[:, s]).then_inc(xt_set, 1)
                act.dma_start(d["res"][bass.ds(i + s, 1)].rearrange("a p j d -> (a p) j d"), xn[:, s]).then_inc(res_stored[s], 16)
                act.wait_ge(xt_set, i + (s + 3))
                act.dma_start(d["xt"][bass.ds(i + s, 1)].rearrange("a p k t -> (a p) k t"), xt[:, s]).then_inc(xt_stored[s], 16)
        for s in range(2):
            act.wait_ge(res_stored[s], NC * 8 + 16)
            act.wait_ge(xt_stored[s], NC * 8 + 16)

    @block.tensor
    def _(pe):
        pe.sem_inc(turned, 2)
        pe.wait_ge(ident_set, 2)
        with pe.Fori(0, NC // 2) as pair:
            i = 2 * pair
            for s in range(2):
                pe.wait_ge(xn_set, i + (s + 3))
                pe.wait_ge(xt_set, i + (s + 1))
                for j in range(J):
                    for k in range(KD):
                        mm = pe.transpose(turn[:, s, k, j * P:(j + 1) * P], xn[:, s, j, k * P:(k + 1) * P], ident[:])
                mm.then_inc(turned, 1)


def moe_logits(nc, ctx, d, logits):
    sb, ps, sem = makers(nc, ctx, "_l")
    ident = sb("ident", [P, P])
    ones = sb("ones", [P, P])
    eps = sb("eps", [P, 1])
    gamma = sb("gamma", [P, D_MODEL])
    beta = sb("beta", [P, D_MODEL])
    scale = sb("scale", [P, 1])
    mu = sb("mu", [P, KD, SLOTS])
    mu_sq = sb("mu_sq", [P, KD, SLOTS])
    mu_norm = sb("mu_norm", [P, SLOTS])
    x = sb("x", [P, J, D_MODEL])
    res = sb("res", [P, J, D_MODEL])
    mt = sb("mt", [P, KD, T])
    r = sb("r", [P, J, D_MODEL])
    x1 = sb("x1", [P, 2, J, D_MODEL])
    xh = sb("xh", [P, J, D_MODEL])
    xn = sb("xn", [P, 2, J, D_MODEL])
    xnt = sb("xnt", [P, KD, T])
    junk = sb("junk", [P, D_MODEL])
    stats = sb("stats", [P, J, 6])
    spare = sb("spare", [P, 1])
    mv = sb("mv", [P, J, 2])
    mv2 = sb("mv2", [P, J, 2])
    sd, sd2, sd3, sd4 = (sb(f"sd{n}", [P, J]) for n in range(4))
    r1, r2, r3, q, rs, ssq = (sb(n, [P, J]) for n in ("r1", "r2", "r3", "q", "rs", "ssq"))
    ta = ps("ta", [P, J, D_MODEL])
    tb = ps("tb", [P, 2, T])
    tl = ps("tl", [P, J, SLOTS])

    ident_set, const_set, small_in = sem("ident_set"), sem("const_set"), sem("small_in")
    x_in, res_in, mt_in = sem("x_in"), sem("res_in"), sem("mt_in")
    sq_set, munorm_ps, munorm_set, mu_set = sem("sq_set"), sem("munorm_ps"), sem("munorm_set"), sem("mu_set")
    ta_set, r_set, rn_set, mv_set, sd_set = sem("ta_set"), sem("r_set"), sem("rn_set"), sem("mv_set"), sem("sd_set")
    x1_set, mv2_set, sd2_set, q_set, sd3_set, xh_set = (sem(n) for n in ("x1_set", "mv2_set", "sd2_set", "q_set", "sd3_set", "xh_set"))
    g_set, xn_set, sd4_set, rs_set = (sem(n) for n in ("g_set", "xn_set", "sd4_set", "rs_set"))
    tb_set, xnt_set, tl_set, log_set = (sem(n) for n in ("tb_set", "xnt_set", "tl_set", "log_set"))
    x1_stored = [sem(f"x1_stored{s}") for s in range(2)]
    xn_stored = [sem(f"xn_stored{s}") for s in range(2)]
    dve_step, act_step = sem("dve_step"), sem("act_step")
    block = ctx.enter_context(nc.Block())

    @block.gpsimd
    def _(pool):
        pool.memset(eps[:], LN_EPS)
        pool.memset(ones[:], 1.0).then_inc(const_set, 1)
        build_identity(pool, ident, ident_set)
        pool.wait_ge(small_in, 64)
        pool.sem_inc(g_set, 1)
        with pool.Fori(0, NC // 2) as pair:
            i = 2 * pair
            for s in range(2):
                c = i + s
                pool.wait_ge(x_in, c * 16 + 16)
                pool.wait_ge(rn_set, c + 1)
                pool.wait_ge(x1_stored[s], i * 8 + 16)
                pool.tensor_tensor(x1[:, s], r[:], x[:], ALU.add).then_inc(x1_set, 1)
                pool.wait_ge(xh_set, c + 1)
                pool.wait_ge(xn_stored[s], i * 8 + 16)
                pool.wait_ge(log_set, c + 1)
                pool.tensor_tensor(xn[:, s], xh[:], gamma[:].unsqueeze(1).to_broadcast([P, J, D_MODEL]), ALU.mult).then_inc(g_set, 1)
                pool.wait_ge(g_set, c + 2)
                pool.tensor_tensor(xn[:, s], xn[:, s], beta[:].unsqueeze(1).to_broadcast([P, J, D_MODEL]), ALU.add).then_inc(xn_set, 1)

    @block.sync
    def _(sp):
        sp.dma_start(mu[:], d["mu"]).then_inc(small_in, 16)
        sp.dma_start(gamma[:], d["gamma"].partition_broadcast(P)).then_inc(small_in, 16)
        sp.dma_start(beta[:], d["beta"].partition_broadcast(P)).then_inc(small_in, 16)
        sp.dma_start(scale[:], d["scale"].partition_broadcast(P)).then_inc(small_in, 16)
        for s in range(2):
            sp.sem_inc(x1_stored[s], 16)
            sp.sem_inc(xn_stored[s], 16)
        with sp.Fori(0, NC) as c:
            sp.wait_ge(ta_set, c + 1)
            sp.dma_start(mt[:], d["xt"][bass.ds(c + LAYERS * NC, 1)].rearrange("a p k t -> (a p) k t")).then_inc(mt_in, 16)
            sp.wait_ge(r_set, c + 1)
            sp.dma_start(res[:], d["res"][bass.ds(c, 1)].rearrange("a p j d -> (a p) j d")).then_inc(res_in, 16)
            sp.wait_ge(x1_set, c + 1)
            sp.dma_start(x[:], d["x"][bass.ds(c, 1)].rearrange("a j p d -> p (a j) d")).then_inc(x_in, 16)

    @block.vector
    def _(dve):
        dve.sem_inc(r_set, 1)
        dve.sem_inc(log_set, 2)
        dve.sem_inc(x1_set, 1)
        dve.wait_ge(small_in, 64)
        dve.tensor_tensor(mu_sq[:], mu[:], mu[:], ALU.mult).then_inc(sq_set, 1)
        dve.wait_ge(munorm_set, 1)
        chain = Chain(dve, dve_step, 0)
        chain.link(dve.tensor_scalar(mu_norm[:], mu_norm[:], NORM_EPS, None, ALU.max))
        chain.link(dve.reciprocal(mu_norm[:], mu_norm[:]))
        dve.tensor_tensor(mu[:], mu[:], mu_norm[:].unsqueeze(1).to_broadcast([P, KD, SLOTS]), ALU.mult).then_inc(mu_set, 1)
        with dve.Fori(0, NC // 2) as pair:
            i = 2 * pair
            for s in range(2):
                c = i + s
                chain = Chain(dve, dve_step, c * 10 + 2)
                dve.wait_ge(ta_set, c + 2)
                dve.wait_ge(res_in, c * 16 + 16)
                dve.wait_ge(x1_set, c + 1)
                dve.tensor_tensor(r[:], ta[:], res[:], ALU.add).then_inc(r_set, 1)
                dve.wait_ge(r_set, c + 2)
                moments(dve, chain, stats, mv, r, spare).then_inc(mv_set, 1)
                dve.wait_ge(sd_set, c + 1)
                chain.link(dve.reciprocal(r1[:], sd[:]))
                for j in range(J):
                    ins = dve.tensor_scalar(r[:, j, :], r[:, j, :], mv[:, j, 0:1], r1[:, j:j + 1], ALU.subtract, ALU.mult)
                ins.then_inc(rn_set, 1)
                dve.wait_ge(x1_set, c + 2)
                moments(dve, chain, stats, mv2, x1[:, s], spare).then_inc(mv2_set, 1)
                dve.wait_ge(sd2_set, c + 1)
                chain.link(dve.reciprocal(r2[:], sd2[:]))
                chain.link(dve.tensor_tensor(q[:], mv2[:, :, 1], r2[:], ALU.mult))
                dve.tensor_tensor(q[:], q[:], r2[:], ALU.mult).then_inc(q_set, 1)
                dve.wait_ge(sd3_set, c + 1)
                chain.link(dve.reciprocal(r3[:], sd3[:]))
                chain.link(dve.tensor_tensor(r3[:], r3[:], r2[:], ALU.mult))
                dve.wait_ge(g_set, c + 1)
                for j in range(J):
                    ins = dve.tensor_scalar(xh[:, j, :], x1[:, s, j, :], mv2[:, j, 0:1], r3[:, j:j + 1], ALU.subtract, ALU.mult)
                ins.then_inc(xh_set, 1)
                dve.wait_ge(sd4_set, c + 1)
                chain.link(dve.tensor_scalar(rs[:], sd4[:], NORM_EPS, None, ALU.max))
                chain.link(dve.reciprocal(rs[:], rs[:]))
                chain.link(dve.tensor_scalar(rs[:], rs[:], scale[:, 0:1], None, ALU.mult))
                dve.wait_ge(tl_set, c + 2)
                for j in range(J):
                    ins = dve.tensor_scalar(logits[:, bass.ds(c * J + j, 1), :].rearrange("p a s -> p (a s)"), tl[:, j, :],
                                            rs[:, j:j + 1], None, ALU.mult)
                ins.then_inc(log_set, 1)

    @block.scalar
    def _(act):
        act.wait_ge(const_set, 1)
        act.wait_ge(munorm_ps, 1)
        act.activation(mu_norm[:], tl[:, 0, :], ACT.Sqrt).then_inc(munorm_set, 1)
        act.sem_inc(xnt_set, 2)
        act.sem_inc(act_step, 1)
        with act.Fori(0, NC // 2) as pair:
            i = 2 * pair
            for s in range(2):
                c = i + s
                act.wait_ge(mv_set, c + 1)
                act.activation(sd[:], mv[:, :, 1], ACT.Sqrt, bias=eps[:]).then_inc(sd_set, 1)
                act.wait_ge(mv2_set, c + 1)
                act.activation(sd2[:], mv2[:, :, 1], ACT.Sqrt, bias=eps[:]).then_inc(sd2_set, 1)
                act.wait_ge(q_set, c + 1)
                act.activation(sd3[:], q[:], ACT.Sqrt, bias=eps[:]).then_inc(sd3_set, 1)
                act.wait_ge(xn_set, c + 1)
                act.dma_start(d["x1"][bass.ds(c, 1)].rearrange("a p j d -> (a p) j d"), x1[:, s]).then_inc(x1_stored[s], 16)
                act.dma_start(d["xn"][bass.ds(c, 1)].rearrange("a p j d -> (a p) j d"), xn[:, s]).then_inc(xn_stored[s], 16)
                for j in range(J):
                    act.wait_ge(act_step, c * J + (j + 1))
                    act.activation(junk[:], xn[:, s, j, :], ACT.Square, accum_out=ssq[:, j:j + 1]).then_inc(act_step, 1)
                act.wait_ge(act_step, c * J + (J + 1))
                act.activation(sd4[:], ssq[:], ACT.Sqrt).then_inc(sd4_set, 1)
                for k in range(KD):
                    if k == 0:
                        act.wait_ge(tl_set, c + 1)
                    act.wait_ge(tb_set, c * 4 + (k + 3))
                    act.copy(xnt[:, k, :], tb[:, k % 2, :]).then_inc(xnt_set, 1)
        for s in range(2):
            act.wait_ge(x1_stored[s], NC * 8 + 16)
            act.wait_ge(xn_stored[s], NC * 8 + 16)

    @block.tensor
    def _(pe):
        pe.wait_ge(ident_set, 2)
        pe.wait_ge(const_set, 1)
        pe.wait_ge(sq_set, 1)
        for k in range(KD):
            mm = pe.matmul(tl[:, 0, :], ones[:], mu_sq[:, k, :], start=k == 0, stop=k == KD - 1)
        mm.then_inc(munorm_ps, 1)
        pe.wait_ge(mu_set, 1)
        pe.sem_inc(ta_set, 1)
        pe.sem_inc(tb_set, 2)
        pe.sem_inc(tl_set, 1)
        with pe.Fori(0, NC // 2) as pair:
            i = 2 * pair
            for s in range(2):
                c = i + s
                pe.wait_ge(mt_in, c * 16 + 16)
                pe.wait_ge(r_set, c + 1)
                for j in range(J):
                    for k in range(KD):
                        mm = pe.transpose(ta[:, j, k * P:(k + 1) * P], mt[:, k, j * P:(j + 1) * P], ident[:])
                mm.then_inc(ta_set, 1)
                pe.wait_ge(xn_set, c + 1)
                for k in range(KD):
                    pe.wait_ge(xnt_set, c * 4 + (k + 1))
                    for j in range(J):
                        mm = pe.transpose(tb[:, k % 2, j * P:(j + 1) * P], xn[:, s, j, k * P:(k + 1) * P], ident[:])
                    mm.then_inc(tb_set, 1)
                pe.wait_ge(xnt_set, c * 4 + 6)
                pe.wait_ge(log_set, c + 2)
                for j in range(J):
                    for k in range(KD):
                        mm = pe.matmul(tl[:, j, :], xnt[:, k, j * P:(j + 1) * P], mu[:, k, :], start=k == 0, stop=k == KD - 1)
                mm.then_inc(tl_set, 1)


def moe_dispatch(nc, ctx, d, logits, slot_out):
    sb, ps, sem = makers(nc, ctx, "_d")
    ident = sb("ident", [P, P])
    zeros = sb("zeros", [P, P])
    ones = sb("ones", [P, 1])
    top = sb("top", [P, SLOTS])
    top_t = sb("top_t", [P, 2])
    top_b = sb("top_b", [P, 2, P])
    top_rep = sb("top_rep", [P, SLOTS])
    xn = sb("xn", [P, 2, J, D_MODEL])
    diff = sb("diff", [P, 2, J, SLOTS])
    e = sb("e", [P, 2, J, SLOTS])
    rden = sb("rden", [P, 2])
    slot_in = sb("slot_in", [P, 2, D_MODEL])
    slot_t = sb("slot_t", [P, KD, SLOTS])
    hidden = sb("hidden", [P, EXPERTS, P])
    w1 = sb("w1", [P, KD, EXPERTS, HID])
    w2 = sb("w2", [P, EXPERTS, D_MODEL])
    b1 = sb("b1", [P, EXPERTS])
    b2 = sb("b2", [P, 2, D_MODEL])
    sums = ps("sums", [P, 2, D_MODEL])
    den = ps("den", [P, 2, 512])
    turn = ps("turn", [P, 4, 512])
    per = SLOTS // EXPERTS
    half = EXPERTS // 2

    ident_set, const_set = sem("ident_set"), sem("const_set")
    w_in = sem("w_in")
    xn_in = [sem(f"xn_in{s}") for s in range(2)]
    top_set, top_turned, topb_set, top_rep_ps, top_rep_set = (sem(n) for n in ("top_set", "top_turned", "topb_set", "top_rep_ps", "top_rep_set"))
    diff_set, e_set, summed = sem("diff_set"), sem("e_set"), sem("summed")
    slot_set, slot_turned, slot_t_set, hid_ps, hid_set, out_ps, out_set = (
        sem(n) for n in ("slot_set", "slot_turned", "slot_t_set", "hid_ps", "hid_set", "out_ps", "out_set"))
    dve_step = sem("dve_step")
    block = ctx.enter_context(nc.Block())

    @block.gpsimd
    def _(pool):
        pool.memset(ones[:], 1.0)
        pool.memset(zeros[:], 0.0)
        pool.memset(hidden[:], 0.0).then_inc(const_set, 1)
        build_identity(pool, ident, ident_set)

    @block.sync
    def _(sp):
        for s in range(2):
            sp.dma_start(xn[:, s], d["xn"][s]).then_inc(xn_in[s], 16)
        sp.dma_start(w1[:], d["w1"]).then_inc(w_in, 16)
        sp.dma_start(w2[:], d["w2"]).then_inc(w_in, 16)
        sp.dma_start(b1[:], d["b1"]).then_inc(w_in, 16)
        for e8 in range(EXPERTS):
            p0 = (e8 % half) * per
            sp.dma_start(b2[p0:p0 + per, e8 // half, :], d["b2"][e8].partition_broadcast(per)).then_inc(w_in, 16)
        with sp.Fori(1, NC // 2) as pair:
            i = 2 * pair
            for s in range(2):
                sp.wait_ge(summed, i + (s + 1))
                sp.dma_start(xn[:, s], d["xn"][bass.ds(i + s, 1)].rearrange("a p j d -> (a p) j d")).then_inc(xn_in[s], 16)

    @block.vector
    def _(dve):
        chain = Chain(dve, dve_step, 0)
        dve.tensor_reduce(top[:], logits[:].rearrange("p c s -> p s c"), AX_X, ALU.max).then_inc(top_set, 1)
        dve.wait_ge(top_turned, 1)
        for h in range(2):
            ins = dve.tensor_reduce(top_t[:, h:h + 1], turn[:, h, 0:P], AX_X, ALU.max)
        chain.link(ins)
        dve.wait_ge(const_set, 1)
        for h in range(2):
            ins = dve.tensor_scalar(top_b[:, h, :], zeros[:], top_t[:, h:h + 1], None, ALU.add)
        ins.then_inc(topb_set, 1)
        dve.wait_ge(top_rep_ps, 1)
        dve.tensor_copy(top_rep[:].rearrange("p (h s) -> p h s", h=2), turn[:, 2:4, 0:P]).then_inc(top_rep_set, 1)
        dve.wait_ge(top_rep_set, 1)
        dve.sem_inc(diff_set, 2)
        with dve.Fori(0, NC // 2) as pair:
            i = 2 * pair
            for s in range(2):
                c = i + s
                dve.wait_ge(e_set, c + 1)
                dve.tensor_tensor(diff[:, s], logits[:, bass.ds(c * J, J), :],
                                  top_rep[:].unsqueeze(1).to_broadcast([P, J, SLOTS]), ALU.subtract).then_inc(diff_set, 1)
        dve.wait_ge(summed, NC + 2)
        chain.link(dve.reciprocal(rden[:], den[:, :, 0]))
        for h in range(2):
            ins = dve.tensor_scalar(slot_in[:, h, :], sums[:, h, :], rden[:, h:h + 1], None, ALU.mult)
        ins.then_inc(slot_set, 1)
        dve.wait_ge(slot_turned, 1)
        dve.tensor_copy(slot_t[:], turn[:, :, 0:SLOTS]).then_inc(slot_t_set, 1)
        dve.wait_ge(out_ps, 1)
        dve.wait_ge(w_in, 16 * (3 + EXPERTS))
        dve.tensor_tensor(slot_out[:], turn[:, 2:4, :], b2[:], ALU.add).then_inc(out_set, 1)
        dve.wait_ge(out_set, 1)

    @block.scalar
    def _(act):
        act.sem_inc(e_set, 2)
        with act.Fori(0, NC // 2) as pair:
            i = 2 * pair
            for s in range(2):
                c = i + s
                act.wait_ge(diff_set, c + 3)
                act.wait_ge(summed, c + 1)
                act.activation(e[:, s], diff[:, s], ACT.Exp).then_inc(e_set, 1)
        act.wait_ge(hid_ps, 1)
        act.wait_ge(w_in, 16 * (3 + EXPERTS))
        act.wait_ge(const_set, 1)
        for x in range(EXPERTS):
            p0 = (x % half) * per
            ins = act.activation(hidden[:, x, p0:p0 + per], den[:, 1, x * per:(x + 1) * per], ACT.Gelu, bias=b1[:, x:x + 1])
        ins.then_inc(hid_set, 1)

    @block.tensor
    def _(pe):
        pe.wait_ge(ident_set, 2)
        pe.wait_ge(top_set, 1)
        for h in range(2):
            mm = pe.transpose(turn[:, h, 0:P], top[:, h * P:(h + 1) * P], ident[:])
        mm.then_inc(top_turned, 1)
        pe.wait_ge(topb_set, 1)
        for h in range(2):
            mm = pe.transpose(turn[:, 2 + h, 0:P], top_b[:, h, :], ident[:])
        mm.then_inc(top_rep_ps, 1)
        pe.wait_ge(const_set, 1)
        pe.sem_inc(summed, 2)
        for h in range(2):
            pe.matmul(sums[:, h, 0:P], zeros[:], ident[:], start=True, stop=False, skip_group_check=True)
            for k in range(1, KD):
                pe.matmul(sums[:, h, k * P:(k + 1) * P], zeros[:], ident[:], start=False, stop=False, skip_group_check=True)
            pe.matmul(den[:, h, 0:1], zeros[:], ones[:], start=True, stop=False, skip_group_check=True)
        with pe.Fori(0, NC // 2) as pair:
            i = 2 * pair
            for s in range(2):
                c = i + s
                pe.wait_ge(e_set, c + 3)
                pe.wait_ge(xn_in[s], i * 8 + 16)
                for j in range(J):
                    for h in range(2):
                        pe.matmul(sums[:, h, :], e[:, s, j, h * P:(h + 1) * P], xn[:, s, j, :], start=False, stop=False, skip_group_check=True)
                        mm = pe.matmul(den[:, h, 0:1], e[:, s, j, h * P:(h + 1) * P], ones[:], start=False, stop=False, skip_group_check=True)
                mm.then_inc(summed, 1)
        pe.wait_ge(slot_set, 1)
        for k in range(KD):
            for h in range(2):
                mm = pe.transpose(turn[:, k, h * P:(h + 1) * P], slot_in[:, h, k * P:(k + 1) * P], ident[:])
        mm.then_inc(slot_turned, 1)
        pe.wait_ge(slot_t_set, 1)
        pe.wait_ge(w_in, 16 * (3 + EXPERTS))
        for x in range(EXPERTS):
            for k in range(KD):
                mm = pe.matmul(den[:, 1, x * per:(x + 1) * per], w1[:, k, x, :], slot_t[:, k, x * per:(x + 1) * per],
                               start=k == 0, stop=k == KD - 1)
        mm.then_inc(hid_ps, 1)
        pe.wait_ge(hid_set, 1)
        for x in range(EXPERTS):
            mm = pe.matmul(turn[:, 2 + x // half, :], hidden[:, x, :], w2[:, x, :], start=x % half == 0, stop=x % half == half - 1)
        mm.then_inc(out_ps, 1)


def moe_combine(nc, ctx, d, logits, slot_out):
    sb, ps, sem = makers(nc, ctx, "_c")
    ident = sb("ident", [P, P])
    eps = sb("eps", [P, 1])
    x1 = sb("x1", [P, 2, J, D_MODEL])
    neg_top = sb("neg_top", [P, 2, J])
    e = sb("e", [P, 2, J, SLOTS])
    et = sb("et", [P, 2, 2, T])
    den = sb("den", [P, 2, J])
    rden = sb("rden", [P, J])
    stats = sb("stats", [P, J, 6])
    spare = sb("spare", [P, 1])
    mv = sb("mv", [P, J, 2])
    var = sb("var", [P, J])
    sd = sb("sd", [P, J])
    mul, add = sb("mul", [P, J]), sb("add", [P, J])
    y = sb("y", [P, 2, J, D_MODEL])
    turn = ps("turn", [P, 2, T])
    mix = ps("mix", [P, J, D_MODEL])

    ident_set, eps_set = sem("ident_set"), sem("eps_set")
    x1_in = [sem(f"x1_in{s}") for s in range(2)]
    stored = [sem(f"stored{s}") for s in range(2)]
    top_set, e_set, turned, et_set, mixed, var_set, sd_set, coef_set, y_set, sum_set = (
        sem(n) for n in ("top_set", "e_set", "turned", "et_set", "mixed", "var_set", "sd_set", "coef_set", "y_set", "sum_set"))
    dve_step = sem("dve_step")
    block = ctx.enter_context(nc.Block())

    @block.gpsimd
    def _(pool):
        pool.memset(eps[:], LN_EPS).then_inc(eps_set, 1)
        build_identity(pool, ident, ident_set)
        pool.sem_inc(sum_set, 2)
        with pool.Fori(0, NC // 2) as pair:
            i = 2 * pair
            for s in range(2):
                pool.wait_ge(y_set, i + (s + 2))
                pool.wait_ge(x1_in[s], i * 8 + 16)
                pool.tensor_tensor(y[:, s], y[:, s], x1[:, s], ALU.add).then_inc(sum_set, 1)

    @block.sync
    def _(sp):
        for s in range(2):
            sp.sem_inc(stored[s], 16)
            sp.dma_start(x1[:, s], d["x1"][s]).then_inc(x1_in[s], 16)
        with sp.Fori(0, NC // 2 - 1) as pair:
            i = 2 * pair
            for s in range(2):
                sp.wait_ge(sum_set, i + (s + 3))
                sp.dma_start(d["out"][bass.ds(i + s, 1)].rearrange("a j p d -> p (a j) d"), y[:, s]).then_inc(stored[s], 16)
                sp.dma_start(x1[:, s], d["x1"][bass.ds(i + (s + 2), 1)].rearrange("a p j d -> (a p) j d")).then_inc(x1_in[s], 16)
        for s in range(2):
            sp.wait_ge(sum_set, NC + s + 1)
            sp.dma_start(d["out"][NC - 2 + s].rearrange("j p d -> p j d"), y[:, s]).then_inc(stored[s], 16)
        for s in range(2):
            sp.wait_ge(stored[s], 16 + NC * 8)

    @block.vector
    def _(dve):
        dve.sem_inc(coef_set, 1)
        dve.sem_inc(et_set, 2)
        dve.sem_inc(top_set, 2)

        def tops(c, s):
            dve.wait_ge(e_set, c + 1)
            dve.tensor_reduce(neg_top[:, s], logits[:, bass.ds(c * J, J), :], AX_X, ALU.max, negate=True).then_inc(top_set, 1)

        with dve.Fori(0, NC // 2) as pair:
            i = 2 * pair
            for s in range(2):
                c = i + s
                chain = Chain(dve, dve_step, c * 5)
                tops(c, s)
                dve.wait_ge(turned, c + 3)
                dve.wait_ge(mixed, c + 1)
                dve.tensor_copy(et[:, s], turn[:]).then_inc(et_set, 1)
                dve.wait_ge(mixed, c + 2)
                for j in range(J):
                    ins = dve.bn_stats(stats[:, j, :], mix[:, j, :])
                chain.link(ins)
                dve.memset(spare[:], 0.0)
                for j in range(J):
                    ins = dve.bn_aggr(mv[:, j, :], stats[:, j, :])
                chain.link(ins)
                chain.link(dve.reciprocal(rden[:], den[:, s]))
                chain.link(dve.tensor_tensor(var[:], mv[:, :, 1], rden[:], ALU.mult))
                dve.tensor_tensor(var[:], var[:], rden[:], ALU.mult).then_inc(var_set, 1)
                dve.wait_ge(sd_set, c + 1)
                chain.link(dve.reciprocal(mul[:], sd[:]))
                dve.tensor_tensor(mul[:], mul[:], rden[:], ALU.mult).then_inc(coef_set, 1)
                dve.wait_ge(coef_set, c * 2 + 2)
                dve.scalar_tensor_tensor(add[:], mv[:, :, 0], -1.0, mul[:], ALU.mult, ALU.mult).then_inc(coef_set, 1)

    @block.scalar
    def _(act):
        act.wait_ge(eps_set, 1)
        act.sem_inc(e_set, 2)
        act.sem_inc(y_set, 1)
        with act.Fori(0, NC // 2) as pair:
            i = 2 * pair
            for s in range(2):
                c = i + s
                act.wait_ge(top_set, c + 3)
                act.wait_ge(turned, c + 1)
                for j in range(J):
                    ins = act.activation(e[:, s, j, :], logits[:, bass.ds(c * J + j, 1), :].rearrange("p a s -> p (a s)"),
                                         ACT.Exp, bias=neg_top[:, s, j:j + 1], accum_out=den[:, s, j:j + 1])
                ins.then_inc(e_set, 1)
                act.wait_ge(var_set, c + 1)
                act.activation(sd[:], var[:], ACT.Sqrt, bias=eps[:]).then_inc(sd_set, 1)
                act.wait_ge(coef_set, c * 2 + 3)
                act.wait_ge(stored[s], i * 8 + 16)
                for j in range(J):
                    ins = act.activation(y[:, s, j, :], mix[:, j, :], ACT.Identity, scale=mul[:, j:j + 1], bias=add[:, j:j + 1])
                ins.then_inc(y_set, 1)

    @block.tensor
    def _(pe):
        pe.wait_ge(ident_set, 2)
        pe.sem_inc(turned, 2)
        pe.sem_inc(mixed, 1)
        with pe.Fori(0, NC // 2) as pair:
            i = 2 * pair
            for s in range(2):
                c = i + s
                pe.wait_ge(e_set, c + 3)
                pe.wait_ge(et_set, c + 2)
                for j in range(J):
                    for h in range(2):
                        mm = pe.transpose(turn[:, h, j * P:(j + 1) * P], e[:, s, j, h * P:(h + 1) * P], ident[:])
                mm.then_inc(turned, 1)
                pe.wait_ge(et_set, c + 3)
                pe.wait_ge(y_set, c + 1)
                for j in range(J):
                    for h in range(2):
                        mm = pe.matmul(mix[:, j, :], et[:, s, h, j * P:(j + 1) * P], slot_out[:, h, :], start=h == 0, stop=h == 1)
                mm.then_inc(mixed, 1)


def build(nc, x, in_w, par, x_w, dt_w, out_w, mu, gamma, beta, scale, w1, b1, w2, b2, out):
    d = {"x": x.rearrange("(c j p) d -> c j p d", j=J, p=P), "out": out.rearrange("(c j p) d -> c j p d", j=J, p=P),
         "w_in": in_w, "par": par, "w_x": x_w, "w_dt": dt_w, "w_out": out_w,
         "mu": mu, "gamma": gamma, "beta": beta, "scale": scale, "w1": w1, "b1": b1, "w2": w2, "b2": b2}
    for name, shape in (("xt", [(LAYERS + 1) * NC, P, KD, T]), ("b_rows", [LAYERS * NC, STATES, T]),
                        ("res", [NC, P, J, D_MODEL]), ("x1", [NC, P, J, D_MODEL]), ("xn", [NC, P, J, D_MODEL])):
        d[name] = nc.dram_tensor(name, shape, F32, kind="Internal").ap()
    with ExitStack() as ctx:
        norm_input(nc, ctx, d)
    with ExitStack() as ctx:
        mamba_stack(nc, ctx, d)
    with ExitStack() as keep:
        logits = keep.enter_context(nc.sbuf_tensor("logits", [P, NC * J, SLOTS], F32))
        slot_out = keep.enter_context(nc.sbuf_tensor("slot_out", [P, 2, D_MODEL], F32))
        with ExitStack() as ctx:
            moe_logits(nc, ctx, d, logits)
        with ExitStack() as ctx:
            moe_dispatch(nc, ctx, d, logits, slot_out)
        with ExitStack() as ctx:
            moe_combine(nc, ctx, d, logits, slot_out)


def kernel(**inputs):
    import numpy as _np
    import concourse.bacc as _bacc
    from concourse import mybir as _mybir
    from concourse.bass_utils import run_bass_kernel_spmd as _run

    a = {name.split("_", 1)[1]: _np.asarray(v) for name, v in inputs.items()}

    def rows_in(m, blocks):
        return m.transpose(0, 2, 1).reshape(LAYERS, blocks, P, m.shape[1]).transpose(0, 2, 1, 3)

    def per_channel(m):
        return m.reshape(LAYERS, NB, P, -1)

    par = _np.concatenate([per_channel(a["attn_" + n]) for n in ("A_log", "conv_w", "conv_b", "dt_proj_b", "D")], axis=-1)
    arrays = {
        "x": a["attn_x"].reshape(SEQ, D_MODEL),
        "in_w": rows_in(a["attn_in_proj_w"], KD),
        "par": par.transpose(0, 2, 1, 3),
        "x_w": rows_in(a["attn_x_proj_w"], NB),
        "dt_w": a["attn_dt_proj_w"].transpose(0, 2, 1),
        "out_w": rows_in(a["attn_out_proj_w"], NB),
        "mu": a["ffn_mu"].reshape(KD, P, SLOTS).transpose(1, 0, 2),
        "gamma": a["ffn_ln_gamma"],
        "beta": a["ffn_ln_beta"],
        "scale": a["ffn_scale"],
        "w1": a["ffn_w1"].reshape(EXPERTS, KD, P, HID).transpose(2, 1, 0, 3),
        "b1": a["ffn_b1"].transpose(1, 0),
        "w2": a["ffn_w2"].transpose(1, 0, 2),
        "b2": a["ffn_b2"],
    }
    nc = _bacc.Bacc("TRN2", target_bir_lowering=False, num_devices=1, dynamic_dma_scratch_size=256)
    ins, args = {}, []
    for name, v in arrays.items():
        v = _np.ascontiguousarray(v)
        ins[f"in_{name}_dram"] = v
        args.append(nc.dram_tensor(f"in_{name}_dram", v.shape, _mybir.dt.from_np(v.dtype), kind="ExternalInput").ap())
    args.append(nc.dram_tensor("out_0_dram", (SEQ, D_MODEL), F32, kind="ExternalOutput").ap())
    build(nc, *args)
    r = _run(nc, [ins], core_ids=[0])
    return r.results[0]["out_0_dram"].reshape(1, SEQ, D_MODEL)
```

```python
from contextlib import ExitStack

import concourse.bass as bass
from concourse import mybir

ALU = mybir.AluOpType
ACT = mybir.ActivationFunctionType
AX_X = mybir.AxisListType.X
F32 = mybir.dt.float32

P = 128
D_MODEL = 512
D_INNER = 1024
STATES = 16
TAPS = 4
RANK = 32
SEQ = 8192
LAYERS = 2
T = 512
J = T // P
NC = SEQ // T
KD = D_MODEL // P
NB = D_INNER // P
HB = NB // 2
GROUPS = 2 * STATES
SCANS = GROUPS * HB
XD = RANK + 2 * STATES
PAR = STATES + TAPS + 3
LN_EPS = 1e-5
NORM_EPS = 1e-12
EXPERTS = 16
SLOTS = 256
HID = 128

RING = 2
PROJ_TILES = 4 * NB + 4 + 1 + 1
PROJ_PROLOGUE = 2 * NB + 1 + 1 + HB
PROJ_FIRST = PROJ_TILES - 4
TURN_TILES = SCANS + NB
TURN_FIRST = SCANS + HB

C_SCAN, C_BU, C_EXP, C_TURN, C_PROJ, C_HS, C_Y, C_W, C_XC, C_Z = 4, SCANS, SCANS, 4, 8, GROUPS, NB, NB, NB, 2


ORDER = ([("conv_half", 0), ("delta", HB), ("conv_half", 1), ("delta", HB + 1), ("conv", 0), ("delta", HB + 2),
          ("conv_half", 2), ("delta", HB + 3), ("conv", 1)] +
         [item for b in range(3, NB) for item in (("conv_half", b), ("conv", b - 1))] + [("conv", NB - 1)] +
         [("out", 0), ("x_proj", 0), ("out", 1)] + [("delta_next", b) for b in range(HB)] + [("turn_c", 0)] +
         [("out", 2), ("out", 3)] + [("gate", b) for b in range(NB)])
PRODUCTS = {"delta": 1, "conv_half": KD, "conv": TAPS, "out": NB, "x_proj": NB, "delta_next": 1, "turn_c": 1, "gate": KD}
SLOTS_BODY = GROUPS * J
TAKE_LAG = 8
TAPS_LEAD = 2
LN_LAG = 2
ROOM = {k: -0.3 for k in range(NB)}
PAUSE = {"delta_next": 1}
NOT_FIRST = ("out",)
NOT_LAST = ("conv_half", "conv", "x_proj", "delta_next", "turn_c")


def timetable():
    total = sum(PRODUCTS[kind] + PAUSE.get(kind, 0) for kind, _ in ORDER)
    room = [1 + ROOM.get(slot // J, 0) / J for slot in range(SLOTS_BODY)]
    slot_of, reached = [], 0
    for slot in range(SLOTS_BODY):
        reached += room[slot] * total / sum(room)
        while len(slot_of) < min(total, round(reached, 6)):
            slot_of.append(slot)
    work = [[] for _ in range(SLOTS_BODY)]
    take = [[] for _ in range(2 * SLOTS_BODY)]
    p = 0
    for kind, x in ORDER:
        slots = [slot_of[p + q] for q in range(PRODUCTS[kind])]
        for slot in sorted(set(slots)):
            lo = slots.index(slot)
            work[slot].append((kind, x, lo, lo + slots.count(slot)))
        p += PRODUCTS[kind] + PAUSE.get(kind, 0)
        at = slots[-1] + TAKE_LAG
        if kind == "conv_half":
            take[at - TAPS_LEAD].append(("taps", x))
        take[at].append((kind, x))
        if kind == "conv" and x % HB == HB - 1:
            take[at].append(("silu_u", x // HB))
        if kind == "delta" and x == NB - 1:
            take[at].append(("softplus_exp", 1))
            take[at + LN_LAG].append(("softplus_ln", 1))
        if kind == "delta_next" and x == HB - 1:
            take[at].append(("softplus_exp_next", 0))
            take[at + LN_LAG].append(("softplus_ln_next", 0))
        if kind == "gate" and x % HB == HB - 1:
            take[at].append(("silu_z", x // HB))
    return work, take


WORK, TAKE = timetable()
CARRIED = sum(len(tiles) for tiles in TAKE[SLOTS_BODY:]) - 1
TURN_Y_BEFORE_AT = (4, 5, 6, 7)
TURN_Y_AT = (24, 25, 26, 27)
GATE_Y_AT = (1, 2, 3, 4)
SKIP_AT = tuple(range(3, 3 + NB))
DELTA_W_AT = tuple(range(8, 16))
DELTA_W_NEXT_AT = tuple(range(24, GROUPS))


class Tally:

    def __init__(self, base):
        self.base, self.n = base, 0

    def at(self, extra):
        return self.base + (self.n + extra)


class Kind:

    def __init__(self, layer, at_start=False, at_end=False):
        self.layer = layer
        self.first, self.last = at_start and layer == 0, at_end and layer == LAYERS - 1
        self.enters, self.leaves = at_start and layer > 0, at_end and layer < LAYERS - 1
        self.layer_before = layer - self.enters
        self.layer_next = layer + self.leaves


def all_chunks(eng, run):
    for layer in range(LAYERS):
        start, end = layer * NC, layer * NC + NC - 1
        run(start, Kind(layer, at_start=True))
        with eng.Fori(start + 1, end) as G:
            run(G, Kind(layer))
        run(end, Kind(layer, at_end=True))


def mamba_stack(nc, ctx, d):
    def sb(name, shape):
        return ctx.enter_context(nc.sbuf_tensor(name, shape, F32))

    def ps(name, shape):
        return ctx.enter_context(nc.psum_tensor(name, shape, F32))

    def sem(name):
        return ctx.enter_context(nc.semaphore(name))

    w_in = sb("w_in", [P, KD, 2 * D_INNER])
    w_out = sb("w_out", [P, NB, D_MODEL])
    w_x = sb("w_x", [P, NB, XD])
    w_dt = sb("w_dt", [RANK, D_INNER])
    par = sb("par", [P, PAR, NB])
    neg_a = sb("neg_a", [P, STATES, NB])
    conv_diag = sb("conv_diag", [P, 2, TAPS, P])
    ident = sb("ident_m", [P, P])
    zeros = sb("zeros_m", [P, NB * 3])
    x_conv = sb("x_conv", [P, KD, T])
    x_gate = sb("x_gate", [P, KD, T])
    conv_in = sb("conv_in", [P, 2, 3 + T])
    halo = sb("halo", [P, NB, 3])
    u = sb("u", [P, NB, T])
    delta = sb("delta", [P, NB, T])
    w = sb("w", [P, NB, T])
    ud = sb("ud", [P, NB, T])
    zy = sb("zy", [P, NB, T])
    xdbl = sb("xdbl", [P, T])
    c_next = sb("c_next", [P, J, STATES])
    c_now = sb("c_now", [P, J, STATES])
    b_rep = sb("b_rep", [P, 4, T])
    bu = sb("bu", [P, 4, T])
    h = sb("h", [P, 2, HB, T])
    h_last = sb("h_last", [P, GROUPS * HB])
    acc = sb("acc", [P, 2, J, HB * P])
    stage = sb("stage", [P, 2, T])
    spare = sb("spare_m", [P, 1])

    decay = ps("decay", [P, HB, T])
    turn = ps("turn", [P, RING, T])
    proj = ps("proj", [P, RING, T])

    conv_weights_in = sem("conv_weights_in")
    xproj_weights_in = sem("xproj_weights_in")
    delta_weights_in = sem("delta_weights_in")
    a_weights_in = sem("a_weights_in")
    skip_weights_in = sem("skip_weights_in")
    gate_weights_in = sem("gate_weights_in")
    out_weights_in = sem("out_weights_in")
    xconv_in = sem("xconv_in")
    xgate_in = sem("xgate_in")
    brep_in = [sem(f"brep_in{r}") for r in range(4)]
    b_stored = sem("b_stored")
    out_stored = [sem(f"out_stored{r}") for r in range(2)]
    ident_set = sem("ident_set")
    zeros_set = sem("zeros_set")
    a_set = sem("a_set")
    halo_set = sem("halo_set")
    proj_full = sem("proj_full")
    proj_done = sem("proj_done")
    convin_set = sem("convin_set")
    u_set = sem("u_set")
    xdbl_set = sem("xdbl_set")
    exp_set = sem("exp_set")
    z_set = sem("z_set")
    softplus_set = sem("softplus_set")
    delta_set = sem("delta_set")
    w_set = sem("w_set")
    ud_set = sem("ud_set")
    decay_set = sem("decay_set")
    bu_set = sem("bu_set")
    scanned = sem("scanned")
    turn_full = sem("turn_full")
    turn_done = sem("turn_done")
    hlast_set = sem("hlast_set")
    c_set = sem("c_set")
    y_set = sem("y_set")

    block = ctx.enter_context(nc.Block())

    def proj_base(G, kind):
        return PROJ_PROLOGUE if kind.first else G * PROJ_TILES + (PROJ_PROLOGUE + PROJ_FIRST - PROJ_TILES)

    def turn_base(G, kind):
        return 0 if kind.first else G * TURN_TILES + (TURN_FIRST - TURN_TILES)

    G_END = LAYERS * NC

    @block.sync
    def _(sp):
        sp.sem_inc(b_stored, 16)
        conv_par, dt_par, d_par = slice(STATES, STATES + TAPS + 1), slice(PAR - 2, PAR - 1), slice(PAR - 1, PAR)

        def load_conv_weights(l):
            sp.dma_start(w_in[:, :, 0:D_INNER], d["w_in"][l, :, :, 0:D_INNER]).then_inc(conv_weights_in, 16)
            sp.dma_start(par[:, conv_par, :], d["par"][l, :, conv_par, :]).then_inc(conv_weights_in, 16)

        def load_xproj_weights(l):
            sp.dma_start(w_x[:], d["w_x"][l]).then_inc(xproj_weights_in, 16)

        def load_a(l):
            sp.dma_start(par[:, 0:STATES, :], d["par"][l, :, 0:STATES, :]).then_inc(a_weights_in, 16)

        def load_delta_weights(l):
            sp.dma_start(w_dt[:], d["w_dt"][l]).then_inc(delta_weights_in, 16)
            sp.dma_start(par[:, dt_par, :], d["par"][l, :, dt_par, :]).then_inc(delta_weights_in, 16)

        def load_skip_weights(l):
            sp.dma_start(par[:, d_par, :], d["par"][l, :, d_par, :]).then_inc(skip_weights_in, 16)

        def load_gate_weights(l):
            sp.dma_start(w_in[:, :, D_INNER:], d["w_in"][l, :, :, D_INNER:]).then_inc(gate_weights_in, 16)

        def load_out_weights(l):
            sp.dma_start(w_out[:], d["w_out"][l]).then_inc(out_weights_in, 16)

        def load_x(dst, G, layer, done):
            if layer > 0:
                for r in range(2):
                    sp.wait_ge(out_stored[r], (G - NC + 1) * 32 + 16)
            sp.dma_start(dst[:], d["xt"][bass.ds(G, 1)].rearrange("a p k t -> (a p) k t")).then_inc(done, 16)

        def load_conv(X, layer):
            sp.wait_ge(convin_set, X * NB + C_XC)
            load_x(x_conv, X, layer, xconv_in)

        def load_b(G, k):
            sp.wait_ge(bu_set, G * SCANS + (4 * (k - 4) + 4 + C_BU))
            if k == 0:
                sp.wait_ge(b_stored, G * 16 + 32)
            n = k % STATES
            src = d["b_rows"][bass.ds(G, 1), n, :].rearrange("a t -> (a t)").partition_broadcast(P)
            sp.dma_start(b_rep[:, k % 4, :], src).then_inc(brep_in[k % 4], 16)

        def body(G, kind, before_last=False):
            new = kind.layer + 1
            next_but_one = kind.layer_next if not before_last else new
            for k in range(GROUPS):
                load_b(G, k)
                if k == 8:
                    sp.wait_ge(z_set, G * 2 + C_Z)
                    load_x(x_gate, G, kind.layer, xgate_in)
                    if kind.enters:
                        load_gate_weights(kind.layer)
                if k == 12 and kind.leaves:
                    sp.wait_ge(softplus_set, G * 2 + 2)
                    load_delta_weights(new)
                if k == 16 and kind.leaves:
                    sp.wait_ge(ud_set, G * NB + (NB + C_W))
                    load_skip_weights(new)
                if k == 20 and next_but_one < LAYERS and not kind.last:
                    load_conv(G + 2, next_but_one)
                if k == 24 and before_last and new < LAYERS:
                    sp.wait_ge(u_set, G * 2 + 4)
                    load_conv_weights(new)
                    sp.wait_ge(xdbl_set, G + 2)
                    load_xproj_weights(new)
                    load_a(new)
                if k == GROUPS - 1 and kind.enters:
                    for r in range(2):
                        sp.wait_ge(out_stored[r], G * 32 + 16)
                    load_out_weights(kind.layer)

        load_conv_weights(0)
        load_conv(0, 0)
        load_xproj_weights(0)
        load_delta_weights(0)
        load_a(0)
        load_conv(1, 0)
        load_skip_weights(0)
        load_gate_weights(0)
        load_out_weights(0)
        for layer in range(LAYERS):
            start, end = layer * NC, layer * NC + NC - 1
            body(start, Kind(layer, at_start=True))
            with sp.Fori(start + 1, end - 1) as G:
                body(G, Kind(layer))
            body(end - 1, Kind(layer), before_last=True)
            body(end, Kind(layer, at_end=True))
        for r in range(2):
            sp.wait_ge(out_stored[r], 16 + LAYERS * NC * 2 * 16)

    @block.tensor
    def _(pe):
        pe.wait_ge(ident_set, 2)

        def bank(pj):
            pe.wait_ge(proj_done, pj.at(C_PROJ + 1 - RING))
            return proj[:, pj.n % RING, :]

        def full(pj, mm):
            mm.then_inc(proj_full, 1)
            pj.n += 1

        def parts(pj, operands, part, count):
            lo, hi = part
            out = proj[:, pj.n % RING, :] if lo else bank(pj)
            for n in range(lo, hi):
                lhs, rhs = operands(n)
                mm = pe.matmul(out[0:lhs.shape[1], :], lhs, rhs, start=n == 0, stop=n == count - 1)
            if hi == count:
                full(pj, mm)

        def conv_half(pj, X, layer, b, part=(0, KD)):
            if b == 0 and part[0] == 0:
                pe.wait_ge(conv_weights_in, layer * 32 + 32)
                pe.wait_ge(xconv_in, X * 16 + 16)
            parts(pj, lambda k: (w_in[:, k, b * P:(b + 1) * P], x_conv[:, k, :]), part, KD)

        def conv(pj, X, b, part=(0, TAPS)):
            if part[0] == 0:
                pe.wait_ge(convin_set, X * NB + (b + 1 + C_XC))
            parts(pj, lambda k: (conv_diag[:, b % 2, k, :], conv_in[:, b % 2, k:k + T]), part, TAPS)

        def x_proj(pj, X, layer, part=(0, NB)):
            if part[0] == 0:
                pe.wait_ge(xproj_weights_in, layer * 16 + 16)
                pe.wait_ge(u_set, X * 2 + 2)
            parts(pj, lambda b: (w_x[:, b, :], u[:, b, :]), part, NB)

        def gate(pj, G, layer, b, part):
            if b == 0 and part[0] == 0:
                pe.wait_ge(gate_weights_in, layer * 16 + 16)
                pe.wait_ge(xgate_in, G * 16 + 16)
            parts(pj, lambda k: (w_in[:, k, D_INNER + b * P:D_INNER + (b + 1) * P], x_gate[:, k, :]), part, KD)

        def out_proj(pj, G, layer, o, part=(0, NB)):
            if o == 0 and part[0] == 0:
                pe.wait_ge(out_weights_in, layer * 16 + 16)
                pe.wait_ge(y_set, G * NB + (NB + C_Y))
            parts(pj, lambda b: (w_out[:, b, o * P:(o + 1) * P], zy[:, b, :]), part, NB)

        def turn_c(pj, X):
            pe.wait_ge(xdbl_set, X + 1)
            out = bank(pj)
            for j in range(J):
                mm = pe.transpose(out[:, j * P:(j + 1) * P], xdbl[:, j * P:(j + 1) * P], ident[:])
            full(pj, mm)

        def delta_proj(pj, X, layer, b):
            pe.wait_ge(delta_weights_in, layer * 32 + 32)
            pe.wait_ge(xdbl_set, X + 1)
            out = bank(pj)
            full(pj, pe.matmul(out, w_dt[:, b * P:(b + 1) * P], xdbl[0:RANK, :], start=True, stop=True))

        def turn_states(tn, G, k, j):
            if j == 0:
                pe.wait_ge(scanned, G * SCANS + (4 * k + 4 + C_SCAN))
            pe.wait_ge(turn_done, tn.at(C_TURN + 1 - RING))
            for b in range(HB):
                mm = pe.transpose(turn[:, tn.n % RING, b * P:(b + 1) * P], h[:, k % 2, b, j * P:(j + 1) * P], ident[:])
            mm.then_inc(turn_full, 1)
            tn.n += 1

        def turn_y(tn, hf, sums, blocks):
            pe.wait_ge(turn_done, tn.base + (sums + C_TURN))
            for b in blocks:
                pe.wait_ge(turn_done, tn.at(C_TURN + 1 - RING))
                for j in range(J):
                    mm = pe.transpose(turn[:, tn.n % RING, j * P:(j + 1) * P], acc[:, hf, j, b * P:(b + 1) * P], ident[:])
                mm.then_inc(turn_full, 1)
                tn.n += 1

        pj = Tally(0)
        X = 0
        for b in range(0, NB, 2):
            conv_half(pj, X, 0, b)
            conv_half(pj, X, 0, b + 1)
            conv(pj, X, b)
            conv(pj, X, b + 1)
        x_proj(pj, X, 0)
        turn_c(pj, X)
        for b in range(HB):
            delta_proj(pj, X, 0, b)

        def body(G, kind):
            pj = Tally(proj_base(G, kind))
            tn = Tally(turn_base(G, kind))
            half0 = 0
            for k in range(GROUPS):
                for j in range(J):
                    turn_states(tn, G, k, j)
                    for what, x, lo, hi in WORK[J * k + j]:
                        if kind.first and what in NOT_FIRST or kind.last and what in NOT_LAST:
                            continue
                        if what == "delta":
                            delta_proj(pj, G, kind.layer, x)
                        if what == "conv_half":
                            conv_half(pj, G + 1, kind.layer_next, x, (lo, hi))
                        if what == "conv":
                            conv(pj, G + 1, x, (lo, hi))
                        if what == "out":
                            out_proj(pj, G - 1, kind.layer_before, x, (lo, hi))
                        if what == "x_proj":
                            x_proj(pj, G + 1, kind.layer_next, (lo, hi))
                        if what == "delta_next":
                            delta_proj(pj, G + 1, kind.layer_next, x)
                        if what == "turn_c":
                            turn_c(pj, G + 1)
                        if what == "gate":
                            gate(pj, G, kind.layer, x, (lo, hi))
                if k == STATES - 1:
                    half0 = tn.n
                if k in TURN_Y_BEFORE_AT and not kind.first:
                    turn_y(tn, 1, 0, (TURN_Y_BEFORE_AT.index(k),))
                if k in TURN_Y_AT:
                    turn_y(tn, 0, half0, (TURN_Y_AT.index(k),))

        all_chunks(pe, body)

        pj = Tally(G_END * PROJ_TILES - KD)
        tn = Tally(G_END * TURN_TILES - HB)
        turn_y(tn, 1, 0, range(HB))
        for o in range(KD):
            out_proj(pj, G_END - 1, LAYERS - 1, o)

    @block.scalar
    def _(act):
        act.sem_inc(proj_done, C_PROJ)
        act.sem_inc(decay_set, C_EXP)
        act.sem_inc(convin_set, C_XC)
        act.sem_inc(ud_set, C_W)
        act.sem_inc(z_set, C_Z)
        act.sem_inc(hlast_set, C_HS)
        for r in range(2):
            act.sem_inc(out_stored[r], 16)
        act.wait_ge(zeros_set, 1)
        act.wait_ge(ident_set, 2)
        def set_a(G, layer):
            act.wait_ge(a_weights_in, layer * 16 + 16)
            act.wait_ge(decay_set, G * SCANS + C_EXP)
            act.activation(neg_a[:], par[:, 0:STATES, :], ACT.Exp).then_inc(a_set, 1)
            act.wait_ge(a_set, 2 * layer + 1)
            act.mul(neg_a[:], neg_a[:], -1.0).then_inc(a_set, 1)
            act.wait_ge(a_set, 2 * layer + 2)

        def clear_halo(pj, layer):
            act.wait_ge(proj_done, pj.at(C_PROJ))
            act.copy(halo[:].rearrange("p b t -> p (b t)"), zeros[:]).then_inc(halo_set, 1)
            act.wait_ge(halo_set, layer + 1)

        conv_bias, dt_bias = STATES + TAPS, STATES + TAPS + 1

        def take(pj):
            act.wait_ge(proj_full, pj.at(1))
            return proj[:, pj.n % RING, :]

        def done(pj, ins):
            ins.then_inc(proj_done, 1)
            pj.n += 1

        def taps(layer, b):
            if b == 0:
                act.wait_ge(conv_weights_in, layer * 32 + 32)
            for k in range(TAPS):
                act.activation(conv_diag[:, b % 2, k, :], ident[:], ACT.Copy, scale=par[:, STATES + k, b:b + 1])

        def conv_half(pj, X, b):
            src = take(pj)
            act.wait_ge(proj_done, pj.at(C_PROJ - 1))
            act.copy(conv_in[:, b % 2, 0:3], halo[:, b, :])
            act.copy(conv_in[:, b % 2, 3:3 + T], src).then_inc(convin_set, 1)
            act.wait_ge(convin_set, X * NB + (b + 1 + C_XC))
            done(pj, act.copy(halo[:, b, :], src[:, T - 3:T]))

        def conv(pj, X, b):
            act.wait_ge(w_set, X * NB + (b + 1))
            act.wait_ge(ud_set, X * NB + (b + 1))
            done(pj, act.activation(u[:, b, :], take(pj), ACT.Identity, bias=par[:, conv_bias, b:b + 1]))

        def silu_u(pj, hf):
            act.wait_ge(proj_done, pj.at(C_PROJ))
            act.activation(u[:, hf * HB:hf * HB + HB, :], u[:, hf * HB:hf * HB + HB, :], ACT.Silu).then_inc(u_set, 1)

        def x_proj(pj, X):
            act.wait_ge(b_stored, X * 16 + 16)
            out = take(pj)
            act.copy(xdbl[0:XD, :], out[0:XD, :]).then_inc(xdbl_set, 1)
            act.wait_ge(xdbl_set, X + 1)
            act.dma_start(d["b_rows"][bass.ds(X, 1)].rearrange("a n t -> (a n) t"),
                          xdbl[RANK:RANK + STATES, :]).then_inc(b_stored, 16)
            done(pj, act.copy(spare[:], out[:, 0:1]))

        def turn_c(pj, X):
            act.wait_ge(c_set, X + 1)
            src = take(pj).rearrange("p (j r) -> p j r", j=J)
            done(pj, act.copy(c_next[:], src[:, :, RANK + STATES:XD]))

        def delta_proj(pj, X, layer, b):
            if b % HB == 0:
                act.wait_ge(delta_weights_in, layer * 32 + 32)
            src = take(pj)
            bias = par[:, dt_bias, b:b + 1]
            if b % HB == 0:
                act.wait_ge(w_set, X * NB + (b + HB))
                act.wait_ge(decay_set, X * SCANS + (b // HB * (SCANS // 2) - SCANS // 2 + C_EXP))
                act.wait_ge(bu_set, X * SCANS + (b // HB * (SCANS // 2) - SCANS // 2 + C_BU))
            act.activation(w[:, b, :], src, ACT.Abs, bias=bias)
            done(pj, act.activation(delta[:, b, :], src, ACT.Relu, bias=bias))

        def softplus_exp(pj, X, hf):
            act.wait_ge(proj_done, pj.at(C_PROJ))
            act.activation(w[:, hf * HB:hf * HB + HB, :], w[:, hf * HB:hf * HB + HB, :], ACT.Exp, scale=-1.0).then_inc(exp_set, 1)

        def softplus_ln(X, hf):
            act.wait_ge(exp_set, X * 2 + (hf + 1))
            act.activation(w[:, hf * HB:hf * HB + HB, :], w[:, hf * HB:hf * HB + HB, :], ACT.Ln, bias=1.0).then_inc(softplus_set, 1)

        def skip(X, layer, b):
            if b == 0:
                act.wait_ge(skip_weights_in, layer * 16 + 16)
            act.wait_ge(y_set, X * NB + (b + 1))
            act.activation(ud[:, b, :], u[:, b, :], ACT.Copy, scale=par[:, PAR - 1, b:b + 1]).then_inc(ud_set, 1)

        def gate(pj, G, b):
            done(pj, act.copy(zy[:, b, :], take(pj)))

        def silu_z(pj, hf):
            act.wait_ge(proj_done, pj.at(C_PROJ))
            act.activation(zy[:, hf * HB:hf * HB + HB, :], zy[:, hf * HB:hf * HB + HB, :], ACT.Silu).then_inc(z_set, 1)

        def out_proj(pj, G, o):
            act.wait_ge(out_stored[o % 2], G * 32 + (o // 2 * 16 + 16))
            done(pj, act.copy(stage[:, o % 2, :], take(pj)))
            act.wait_ge(proj_done, pj.at(C_PROJ))
            act.dma_start(d["xt"][bass.ds(G + NC, 1), :, o, :].rearrange("a p t -> (a p) t"),
                          stage[:, o % 2, :]).then_inc(out_stored[o % 2], 16)

        def decay_of(G, k, b):
            hf, n = divmod(k, STATES)
            blk = hf * HB + b
            act.wait_ge(scanned, G * SCANS + (4 * k + b + 1))
            if n == 0:
                act.wait_ge(delta_set, G * NB + (blk + 1))
            act.activation(decay[:, b, :], delta[:, blk, :], ACT.Exp,
                           scale=neg_a[:, n, blk:blk + 1]).then_inc(decay_set, 1)

        pj = Tally(0)
        X = 0
        clear_halo(pj, 0)
        for b in range(0, NB, 2):
            taps(0, b)
            taps(0, b + 1)
            conv_half(pj, X, b)
            conv_half(pj, X, b + 1)
            conv(pj, X, b)
            conv(pj, X, b + 1)
        silu_u(pj, 0)
        silu_u(pj, 1)
        x_proj(pj, X)
        turn_c(pj, X)
        for b in range(HB):
            delta_proj(pj, X, 0, b)
        softplus_exp(pj, X, 0)
        softplus_ln(X, 0)

        set_a(0, 0)

        def save_last(G, k):
            act.copy(h_last[:, HB * k:HB * k + HB], h[:, k % 2, :, T - 1]).then_inc(hlast_set, 1)

        def take_tiles(pj, G, position, kind):
            for what, x in TAKE[position]:
                if kind.first and what in NOT_FIRST or kind.last and what in NOT_LAST:
                    continue
                if what == "delta":
                    delta_proj(pj, G, kind.layer, x)
                if what == "taps" and not kind.last:
                    taps(kind.layer_next, x)
                if what == "conv_half":
                    conv_half(pj, G + 1, x)
                if what == "conv":
                    conv(pj, G + 1, x)
                if what == "silu_u" and not kind.last:
                    silu_u(pj, x)
                if what == "out":
                    out_proj(pj, G - 1, x)
                if what == "x_proj":
                    x_proj(pj, G + 1)
                if what == "delta_next":
                    delta_proj(pj, G + 1, kind.layer_next, x)
                if what == "turn_c":
                    turn_c(pj, G + 1)
                if what == "gate":
                    gate(pj, G, x)
                if what == "silu_z":
                    silu_z(pj, x)
                if what == "softplus_exp":
                    softplus_exp(pj, G, x)
                if what == "softplus_ln":
                    softplus_ln(G, x)
                if what == "softplus_exp_next" and not kind.last:
                    softplus_exp(pj, G + 1, x)
                if what == "softplus_ln_next" and not kind.last:
                    softplus_ln(G + 1, x)

        def body(G, kind):
            pj = Tally(proj_base(G, kind))
            if not kind.first:
                pj.n = -CARRIED
            if kind.enters:
                set_a(G, kind.layer)
            if kind.leaves:
                clear_halo(pj, kind.layer + 1)
            for k in range(GROUPS):
                for b in range(HB):
                    decay_of(G, k, b)
                    if b == 0 and k > 1:
                        save_last(G, k - 2)
                    if b == 0 and k < 2 and not kind.first:
                        save_last(G - 1, GROUPS + k - 2)
                    if not kind.first:
                        take_tiles(pj, G - 1, SLOTS_BODY + HB * k + b, kind)
                    take_tiles(pj, G, HB * k + b, kind)
                if k in SKIP_AT:
                    skip(G, kind.layer, SKIP_AT.index(k))

        all_chunks(act, body)
        pj = Tally(G_END * PROJ_TILES - KD)
        pj.n = -CARRIED
        for position in range(SLOTS_BODY, 2 * SLOTS_BODY):
            take_tiles(pj, G_END - 1, position, Kind(LAYERS - 1, at_end=True))
        for o in range(KD):
            out_proj(pj, G_END - 1, o)

    @block.gpsimd
    def _(pool):
        pool.sem_inc(bu_set, C_BU)
        pool.sem_inc(w_set, C_W)
        pool.memset(zeros[:], 0.0)
        pool.memset(xdbl[:], 0.0).then_inc(zeros_set, 1)
        pool.memset(ident[:], 0.0).then_inc(ident_set, 1)
        pool.wait_ge(ident_set, 1)
        pool.affine_select(out=ident[:], in_=ident[:], compare_op=ALU.not_equal, fill=1.0, base=0,
                           pattern=[[-1, P]], channel_multiplier=1).then_inc(ident_set, 1)
        pool.wait_ge(ident_set, 2)

        def delta_w(X, step):
            b, second = divmod(step, 2)
            if not second:
                pool.wait_ge(softplus_set, X * 2 + (b // HB + 1))
                pool.tensor_tensor(delta[:, b, :], delta[:, b, :], w[:, b, :], ALU.add).then_inc(delta_set, 1)
            else:
                pool.wait_ge(delta_set, X * NB + (b + 1))
                pool.tensor_tensor(w[:, b, :], delta[:, b, :], u[:, b, :], ALU.mult).then_inc(w_set, 1)

        def input_of(G, k, b):
            hf, n = divmod(k, STATES)
            blk = hf * HB + b
            if b == 0:
                pool.wait_ge(brep_in[k % 4], G * (GROUPS * 4) + (k // 4 + 1) * 16)
            if n == 0:
                pool.wait_ge(w_set, G * NB + (blk + 1 + C_W))
            pool.wait_ge(scanned, G * SCANS + (4 * k + b + 1))
            pool.tensor_tensor(bu[:, b, :], w[:, blk, :], b_rep[:, k % 4, :], ALU.mult).then_inc(bu_set, 1)

        X = 0
        for step in range(2 * HB):
            delta_w(X, step)

        def body(G, kind):
            for k in range(GROUPS):
                for b in range(HB):
                    input_of(G, k, b)
                for step in range(2 * HB):
                    if k == DELTA_W_AT[step]:
                        delta_w(G, 2 * HB + step)
                    if k == DELTA_W_NEXT_AT[step] and not kind.last:
                        delta_w(G + 1, step)

        all_chunks(pool, body)

    @block.vector
    def _(dve):
        dve.sem_inc(scanned, C_SCAN)
        dve.sem_inc(turn_done, C_TURN)
        dve.sem_inc(y_set, C_Y)
        dve.sem_inc(c_set, 1)
        dve.wait_ge(zeros_set, 1)

        def scan(G, kind, k, b):
            dve.wait_ge(decay_set, G * SCANS + (4 * k + b + 1 + C_EXP))
            dve.wait_ge(bu_set, G * SCANS + (4 * k + b + 1 + C_BU))
            if b == 0:
                dve.wait_ge(hlast_set, G * GROUPS + (k - 1 + C_HS))
            start = zeros[:, 0:1] if kind.first or kind.enters else h_last[:, 4 * k + b:4 * k + b + 1]
            dve.tensor_tensor_scan(h[:, k % 2, b, :], decay[:, b, :], bu[:, b, :], start, ALU.mult, ALU.add).then_inc(scanned, 1)

        def add_state(tn, k, j):
            hf, n = divmod(k, STATES)
            dve.wait_ge(turn_full, tn.at(1))
            dve.wait_ge(turn_done, tn.at(C_TURN - 3))
            scalar = c_now[:, j, n:n + 1]
            if n == 0:
                ins = dve.tensor_scalar(acc[:, hf, j, :], turn[:, tn.n % RING, :], scalar, None, ALU.mult)
            else:
                ins = dve.scalar_tensor_tensor(acc[:, hf, j, :], turn[:, tn.n % RING, :], scalar, acc[:, hf, j, :],
                                               ALU.mult, ALU.add)
            ins.then_inc(turn_done, 1)
            tn.n += 1

        def sum_y(tn, G, b):
            dve.wait_ge(turn_full, tn.at(1))
            dve.wait_ge(ud_set, G * NB + (b + 1 + C_W))
            dve.tensor_tensor(ud[:, b, :], turn[:, tn.n % RING, :], ud[:, b, :], ALU.add).then_inc(turn_done, 1)
            tn.n += 1

        def gate_y(G, b, summed):
            dve.wait_ge(z_set, G * 2 + (b // HB + 1 + C_Z))
            dve.wait_ge(turn_done, summed)
            dve.tensor_tensor(zy[:, b, :], ud[:, b, :], zy[:, b, :], ALU.mult).then_inc(y_set, 1)

        def body(G, kind):
            tn = Tally(turn_base(G, kind))
            if not kind.first:
                tn.n = -4
            for k in range(GROUPS):
                if k == 1:
                    dve.wait_ge(turn_done, tn.at(C_TURN))
                    dve.tensor_copy(c_now[:], c_next[:]).then_inc(c_set, 1)
                    dve.wait_ge(c_set, G + 2)
                for b in range(HB):
                    scan(G, kind, k, b)
                    if k > 0:
                        add_state(tn, k - 1, b)
                    elif not kind.first:
                        add_state(tn, GROUPS - 1, b)
                if k in GATE_Y_AT and not kind.first:
                    gate_y(G - 1, GATE_Y_AT.index(k), tn.base + (C_TURN - J))
                if k - 1 in TURN_Y_BEFORE_AT and not kind.first:
                    b = HB + TURN_Y_BEFORE_AT.index(k - 1)
                    sum_y(tn, G - 1, b)
                    gate_y(G - 1, b, tn.at(C_TURN))
                if k - 1 in TURN_Y_AT:
                    sum_y(tn, G, TURN_Y_AT.index(k - 1))

        all_chunks(dve, body)
        G = G_END - 1
        tn = Tally(G_END * TURN_TILES - HB)
        tn.n = -4
        for j in range(J):
            add_state(tn, GROUPS - 1, j)
        for b in range(HB):
            gate_y(G, b, tn.at(C_TURN))
        for b in range(HB, NB):
            sum_y(tn, G, b)
            gate_y(G, b, tn.at(C_TURN))


LOWEST = -3.4e38


class Chain:

    def __init__(self, eng, sem, base):
        self.eng, self.sem, self.base, self.n = eng, sem, base, 0

    def link(self, ins):
        ins.then_inc(self.sem, 1)
        self.n += 1
        self.eng.wait_ge(self.sem, self.base + self.n)


def makers(nc, ctx, tag):
    def sb(name, shape):
        return ctx.enter_context(nc.sbuf_tensor(name + tag, shape, F32))

    def ps(name, shape):
        return ctx.enter_context(nc.psum_tensor(name + tag, shape, F32))

    def sem(name):
        return ctx.enter_context(nc.semaphore(name + tag))

    return sb, ps, sem


def build_identity(pool, ident, ident_set):
    pool.memset(ident[:], 0.0).then_inc(ident_set, 1)
    pool.wait_ge(ident_set, 1)
    pool.affine_select(out=ident[:], in_=ident[:], compare_op=ALU.not_equal, fill=1.0, base=0,
                       pattern=[[-1, P]], channel_multiplier=1).then_inc(ident_set, 1)


def moments(dve, chain, stats, mv, rows, spare, js=range(J)):
    for j in js:
        ins = dve.bn_stats(stats[:, j, :], rows[:, j, :])
    chain.link(ins)
    dve.memset(spare[:], 0.0)
    for j in js:
        ins = dve.bn_aggr(mv[:, j, :], stats[:, j, :])
    return ins


def pipelined(eng, depth, step, ahead=0):
    for i in range(depth):
        step(i, i % 2, [n <= i for n in range(depth + 1)])
    rest = (NC - depth - ahead) // 2 * 2
    with eng.Fori(0, rest // 2) as pair:
        for s in range(2):
            step(2 * pair + (depth + s), (depth + s) % 2, [True] * (depth + 1))
    for i in range(depth + rest, NC + depth):
        step(i, i % 2, [i - n < NC for n in range(depth + 1)])


def norm_input(nc, ctx, d, rstd, nmr):
    sb, ps, sem = makers(nc, ctx, "_n")
    ident = sb("ident", [P, P])
    x = sb("x", [P, 2, J, D_MODEL])
    xn = sb("xn", [P, 2, J, D_MODEL])
    xt = sb("xt", [P, 2, KD, T])
    stats = sb("stats", [P, 2, J, 6])
    spare = sb("spare", [P, 1])
    mv = sb("mv", [P, 2, J, 2])
    sd = sb("sd", [P, 2, J])
    eps = sb("eps", [P, 1])
    turn = ps("turn", [P, 2, KD, T])

    ident_set, eps_set, mv_set, sd_set = sem("ident_set"), sem("eps_set"), sem("mv_set"), sem("sd_set")
    x_in = [sem(f"x_in{s}") for s in range(2)]
    xt_stored = [sem(f"xt_stored{s}") for s in range(2)]
    coef_set, xn_set, turned, xt_set = sem("coef_set"), sem("xn_set"), sem("turned"), sem("xt_set")
    dve_step, rstd_step = sem("dve_step"), sem("rstd_step")
    block = ctx.enter_context(nc.Block())

    @block.gpsimd
    def _(pool):
        pool.memset(eps[:], LN_EPS).then_inc(eps_set, 1)
        build_identity(pool, ident, ident_set)

    @block.sync
    def _(sp):
        with sp.Fori(0, NC // 2) as pair:
            i = 2 * pair
            for s in range(2):
                sp.wait_ge(xn_set, i + (s + 1))
                sp.dma_start(x[:, s], d["x"][bass.ds(i + s, 1)].rearrange("a j p d -> p (a j) d")).then_inc(x_in[s], 16)

    @block.vector
    def _(dve):
        dve.sem_inc(coef_set, 2)

        def step(i, s, live):
            if live[1]:
                c, s1 = i - 1, 1 - s
                chain = Chain(dve, rstd_step, c)
                dve.wait_ge(sd_set, c + 3)
                now = rstd[:, bass.ds(c * J, J)]
                chain.link(dve.reciprocal(now, sd[:, s1]))
                dve.scalar_tensor_tensor(nmr[:, bass.ds(c * J, J)], mv[:, s1, :, 0], -1.0, now, ALU.mult, ALU.mult).then_inc(coef_set, 1)
            if live[0]:
                chain = Chain(dve, dve_step, i)
                dve.wait_ge(x_in[s], (i - s) * 8 + 16)
                dve.wait_ge(sd_set, i + 1)
                moments(dve, chain, stats[:, s], mv[:, s], x[:, s], spare).then_inc(mv_set, 1)

        pipelined(dve, 1, step)

    @block.scalar
    def _(act):
        act.sem_inc(xn_set, 2)
        act.sem_inc(xt_set, 2)
        for s in range(2):
            act.sem_inc(xt_stored[s], 16)

        act.sem_inc(sd_set, 2)
        act.wait_ge(eps_set, 1)

        def step(i, s, live):
            if live[1]:
                c, s1 = i - 1, 1 - s
                act.wait_ge(coef_set, c + 3)
                act.wait_ge(turned, c + 1)
                for j in range(J):
                    ins = act.activation(xn[:, s1, j, :], x[:, s1, j, :], ACT.Identity, scale=rstd[:, bass.ds(c * J + j, 1)],
                                         bias=nmr[:, bass.ds(c * J + j, 1)])
                ins.then_inc(xn_set, 1)
            if live[0]:
                act.wait_ge(mv_set, i + 1)
                act.wait_ge(coef_set, i + 1)
                act.activation(sd[:, s], mv[:, s, :, 1], ACT.Sqrt, bias=eps[:]).then_inc(sd_set, 1)
            if live[2]:
                c = i - 2
                act.wait_ge(turned, c + 3)
                act.wait_ge(xt_stored[s], (c - s) * 8 + 16)
                act.copy(xt[:, s], turn[:, s]).then_inc(xt_set, 1)
                act.wait_ge(xt_set, c + 3)
                act.dma_start(d["xt"][bass.ds(c, 1)].rearrange("a p k t -> (a p) k t"), xt[:, s]).then_inc(xt_stored[s], 16)

        pipelined(act, 2, step)
        for s in range(2):
            act.wait_ge(xt_stored[s], NC * 8 + 16)

    @block.tensor
    def _(pe):
        pe.sem_inc(turned, 2)
        pe.wait_ge(ident_set, 2)
        with pe.Fori(0, NC // 2) as pair:
            i = 2 * pair
            for s in range(2):
                pe.wait_ge(xn_set, i + (s + 3))
                pe.wait_ge(xt_set, i + (s + 1))
                for j in range(J):
                    for k in range(KD):
                        mm = pe.transpose(turn[:, s, k, j * P:(j + 1) * P], xn[:, s, j, k * P:(k + 1) * P], ident[:])
                mm.then_inc(turned, 1)


def moe_logits(nc, ctx, d, rstd, nmr, logits, run_top):
    sb, ps, sem = makers(nc, ctx, "_l")
    ident = sb("ident", [P, P])
    ones = sb("ones", [P, P])
    gamma_t = sb("gamma_t", [P, KD])
    beta_t = sb("beta_t", [P, KD])
    scale = sb("scale", [P, 1])
    mu = sb("mu", [P, KD, SLOTS])
    mu_sq = sb("mu_sq", [P, KD, SLOTS])
    mu_norm = sb("mu_norm", [P, SLOTS])
    x = sb("x", [P, 2, J, D_MODEL])
    res = sb("res", [P, J, D_MODEL])
    mt = sb("mt", [P, KD, T])
    r = sb("r", [P, 2, J, D_MODEL])
    x1 = sb("x1", [P, 2, J, D_MODEL])
    xh = sb("xh", [P, 2, J, D_MODEL])
    xnt = sb("xnt", [P, 2, KD, T])
    xsq = sb("xsq", [P, KD, T])
    stats, stats2 = sb("stats", [P, J, 6]), sb("stats2", [P, J, 6])
    spare = sb("spare", [P, 1])
    mv, mv2 = sb("mv", [P, J, 2]), sb("mv2", [P, J, 2])
    eps = sb("eps", [P, 1])
    sd, sd2, sd3, sd4 = (sb(n, [P, J]) for n in ("sd", "sd2", "sd3", "sd4"))
    r1, nb1, q, r2, r3, rs = (sb(n, [P, J]) for n in ("r1", "nb1", "q", "r2", "r3", "rs"))
    ta = ps("ta", [P, 2, D_MODEL])
    tb = ps("tb", [P, 2, T])
    tl = ps("tl", [P, J, SLOTS])
    ssq = ps("ssq", [P, 512])

    ident_set, const_set, small_in = sem("ident_set"), sem("const_set"), sem("small_in")
    x_in = [sem(f"x_in{s}") for s in range(2)]
    mt_in = sem("mt_in")
    x1_stored = [sem(f"x1_stored{s}") for s in range(2)]
    xh_stored = [sem(f"xh_stored{s}") for s in range(2)]
    sq_set, munorm_ps, munorm_set, mu_set = sem("sq_set"), sem("munorm_ps"), sem("munorm_set"), sem("mu_set")
    ta_set, r_set, coef_set, res_set, rn_set = (sem(n) for n in ("ta_set", "r_set", "coef_set", "res_set", "rn_set"))
    x1_set, xh_set, tb_set, xnt_set, xsq_set = (sem(n) for n in ("x1_set", "xh_set", "tb_set", "xnt_set", "xsq_set"))
    tl_set, log_set, top_set = sem("tl_set"), sem("log_set"), sem("top_set")
    mv_set, mv2_set, q_set, ssq_set = (sem(n) for n in ("mv_set", "mv2_set", "q_set", "ssq_set"))
    sd_set, sd2_set, sd3_set, sd4_set = (sem(n) for n in ("sd_set", "sd2_set", "sd3_set", "sd4_set"))
    r_step, coef_step, x1_step, r2_step, r3_step, rs_step = (
        sem(n) for n in ("r_step", "coef_step", "x1_step", "r2_step", "r3_step", "rs_step"))
    block = ctx.enter_context(nc.Block())

    @block.gpsimd
    def _(pool):
        pool.memset(eps[:], LN_EPS)
        pool.memset(ones[:], 1.0).then_inc(const_set, 1)
        pool.memset(run_top[:], LOWEST).then_inc(top_set, 1)
        build_identity(pool, ident, ident_set)

        def step(i, s, live):
            if live[0]:
                pool.wait_ge(rn_set, i + 2)
                pool.wait_ge(xh_set, i + 1)
                pool.wait_ge(x1_stored[s], (i - s) * 8 + 16)
                pool.tensor_tensor(x1[:, s], r[:, s], x[:, s], ALU.add).then_inc(x1_set, 1)

        pipelined(pool, 2, step)

    @block.sync
    def _(sp):
        sp.dma_start(mu[:], d["mu"]).then_inc(small_in, 16)
        sp.dma_start(gamma_t[:], d["gamma_t"]).then_inc(small_in, 16)
        sp.dma_start(beta_t[:], d["beta_t"]).then_inc(small_in, 16)
        sp.dma_start(scale[:], d["scale"].partition_broadcast(P)).then_inc(small_in, 16)
        with sp.Fori(0, NC // 2) as pair:
            for s in range(2):
                c = 2 * pair + s
                sp.wait_ge(x1_set, c + 1)
                sp.dma_start(x[:, s], d["x"][bass.ds(c, 1)].rearrange("a j p d -> p (a j) d")).then_inc(x_in[s], 16)
                sp.wait_ge(ta_set, c * J + 1)
                sp.dma_start(mt[:], d["xt"][bass.ds(c + LAYERS * NC, 1)].rearrange("a p k t -> (a p) k t")).then_inc(mt_in, 16)

    @block.vector
    def _(dve):
        dve.sem_inc(r_set, 2)
        dve.sem_inc(coef_set, 1)
        dve.sem_inc(log_set, 2)
        dve.sem_inc(x1_set, 2)
        dve.sem_inc(xh_set, 2)
        dve.wait_ge(small_in, 64)
        dve.tensor_tensor(mu_sq[:], mu[:], mu[:], ALU.mult).then_inc(sq_set, 1)
        dve.wait_ge(munorm_set, 1)
        chain = Chain(dve, r_step, 0)
        chain.link(dve.tensor_scalar(mu_norm[:], mu_norm[:], NORM_EPS, None, ALU.max))
        chain.link(dve.reciprocal(mu_norm[:], mu_norm[:]))
        dve.tensor_tensor(mu[:], mu[:], mu_norm[:].unsqueeze(1).to_broadcast([P, KD, SLOTS]), ALU.mult).then_inc(mu_set, 1)

        def step(i, s, live):
            if live[0]:
                dve.wait_ge(res_set, i + 1)
                dve.wait_ge(x1_set, i + 1)
                for j in range(J):
                    dve.wait_ge(ta_set, i * J + (j + 2))
                    dve.tensor_tensor(r[:, s, j, :], ta[:, j % 2, :], res[:, j, :], ALU.add).then_inc(r_set, 1)
                dve.wait_ge(r_set, i * J + (J + 2))
                dve.wait_ge(coef_set, i + 1)
                chain = Chain(dve, r_step, i + 2)
                moments(dve, chain, stats, mv, r[:, s], spare).then_inc(mv_set, 1)
            if live[1]:
                c, s1 = i - 1, 1 - s
                dve.wait_ge(x1_set, c + 3)
                dve.wait_ge(xh_set, c + 2)
                chain = Chain(dve, x1_step, c)
                moments(dve, chain, stats2, mv2, x1[:, s1], spare).then_inc(mv2_set, 1)
            if live[0]:
                dve.wait_ge(sd_set, i + 1)
                dve.wait_ge(rn_set, i + 1)
                chain = Chain(dve, coef_step, i)
                chain.link(dve.reciprocal(r1[:], sd[:]))
                dve.scalar_tensor_tensor(nb1[:], mv[:, :, 0], -1.0, r1[:], ALU.mult, ALU.mult).then_inc(coef_set, 1)
            if live[1]:
                dve.wait_ge(sd2_set, c + 1)
                chain = Chain(dve, r2_step, c * 2)
                chain.link(dve.reciprocal(r2[:], sd2[:]))
                chain.link(dve.tensor_tensor(q[:], mv2[:, :, 1], r2[:], ALU.mult))
                dve.tensor_tensor(q[:], q[:], r2[:], ALU.mult).then_inc(q_set, 1)
            if live[1]:
                dve.wait_ge(sd3_set, c + 1)
                chain = Chain(dve, r3_step, c * 2)
                chain.link(dve.reciprocal(r3[:], sd3[:]))
                chain.link(dve.tensor_tensor(r3[:], r3[:], r2[:], ALU.mult))
                dve.wait_ge(tb_set, c * KD + 2)
                dve.wait_ge(xh_stored[s1], (c - s1) * 8 + 16)
                for j in range(J):
                    ins = dve.tensor_scalar(xh[:, s1, j, :], x1[:, s1, j, :], mv2[:, j, 0:1], r3[:, j:j + 1], ALU.subtract, ALU.mult)
                ins.then_inc(xh_set, 1)
            if live[2]:
                c2 = i - 2
                dve.wait_ge(sd4_set, c2 + 1)
                dve.wait_ge(log_set, c2 + 2)
                chain = Chain(dve, rs_step, c2 * 3)
                chain.link(dve.tensor_scalar(rs[:], sd4[:], NORM_EPS, None, ALU.max))
                chain.link(dve.reciprocal(rs[:], rs[:]))
                chain.link(dve.tensor_scalar(rs[:], rs[:], scale[:, 0:1], None, ALU.mult))
                dve.wait_ge(tl_set, c2 + 2)
                for j in range(J):
                    ins = dve.tensor_scalar(logits[:, bass.ds(c2 * J + j, 1), :].rearrange("p a s -> p (a s)"), tl[:, j, :],
                                            rs[:, j:j + 1], None, ALU.mult)
                ins.then_inc(log_set, 1)
                dve.wait_ge(log_set, c2 + 3)
                dve.wait_ge(top_set, c2 + 1)
                dve.tensor_tensor(run_top[:], run_top[:], logits[:, bass.ds(c2 * J, J), :], ALU.max).then_inc(top_set, 1)

        pipelined(dve, 2, step)

    @block.scalar
    def _(act):
        act.wait_ge(munorm_ps, 1)
        act.activation(mu_norm[:], tl[:, 0, :], ACT.Sqrt).then_inc(munorm_set, 1)
        act.sem_inc(xnt_set, 2)
        act.sem_inc(rn_set, 1)
        for s in range(2):
            act.sem_inc(x1_stored[s], 16)
            act.sem_inc(xh_stored[s], 16)

        def norm_of_x(c, s):
            act.wait_ge(x_in[s], (c - s) * 8 + 16)
            act.wait_ge(r_set, c * J + 2)
            for j in range(J):
                ins = act.activation(res[:, j, :], x[:, s, j, :], ACT.Identity, scale=rstd[:, bass.ds(c * J + j, 1)],
                                     bias=nmr[:, bass.ds(c * J + j, 1)])
            ins.then_inc(res_set, 1)

        norm_of_x(0, 0)

        def step(i, s, live):
            if live[1]:
                c, s1 = i - 1, 1 - s
                act.wait_ge(x1_set, c + 3)
                act.dma_start(d["x1"][bass.ds(c, 1)].rearrange("a p j d -> (a p) j d"), x1[:, s1]).then_inc(x1_stored[s1], 16)
            if live[0]:
                act.wait_ge(mv_set, i + 1)
                act.activation(sd[:], mv[:, :, 1], ACT.Sqrt, bias=eps[:]).then_inc(sd_set, 1)
            if live[1]:
                act.wait_ge(mv2_set, c + 1)
                act.activation(sd2[:], mv2[:, :, 1], ACT.Sqrt, bias=eps[:]).then_inc(sd2_set, 1)
            if live[1]:
                act.wait_ge(q_set, c + 1)
                act.activation(sd3[:], q[:], ACT.Sqrt, bias=eps[:]).then_inc(sd3_set, 1)
            if live[0]:
                act.wait_ge(coef_set, i + 2)
                for j in range(J):
                    ins = act.activation(r[:, s, j, :], r[:, s, j, :], ACT.Identity, scale=r1[:, j:j + 1], bias=nb1[:, j:j + 1])
                ins.then_inc(rn_set, 1)
            if live[0] and not (isinstance(i, int) and i == NC - 1):
                norm_of_x(i + 1, 1 - s)
            if live[2]:
                act.wait_ge(ssq_set, i)
                act.activation(sd4[:], ssq[:, 0:J], ACT.Sqrt).then_inc(sd4_set, 1)
            if live[1]:
                act.wait_ge(xh_set, c + 3)
                act.dma_start(d["xh"][bass.ds(c, 1)].rearrange("a p j d -> (a p) j d"), xh[:, s1]).then_inc(xh_stored[s1], 16)
                for k in range(KD):
                    act.wait_ge(tb_set, c * KD + (k + 3))
                    act.activation(xnt[:, s1, k, :], tb[:, k % 2, :], ACT.Identity, scale=gamma_t[:, k:k + 1],
                                   bias=beta_t[:, k:k + 1]).then_inc(xnt_set, 1)
                act.wait_ge(xnt_set, c * KD + (KD + 2))
                act.wait_ge(ssq_set, c + 1)
                act.activation(xsq[:], xnt[:, s1], ACT.Square).then_inc(xsq_set, 1)

        pipelined(act, 2, step, ahead=1)
        for s in range(2):
            act.wait_ge(x1_stored[s], NC * 8 + 16)
            act.wait_ge(xh_stored[s], NC * 8 + 16)

    @block.tensor
    def _(pe):
        pe.wait_ge(ident_set, 2)
        pe.wait_ge(const_set, 1)
        pe.wait_ge(sq_set, 1)
        for k in range(KD):
            mm = pe.matmul(tl[:, 0, :], ones[:], mu_sq[:, k, :], start=k == 0, stop=k == KD - 1)
        mm.then_inc(munorm_ps, 1)
        pe.wait_ge(mu_set, 1)
        pe.sem_inc(ta_set, 1)
        pe.sem_inc(tb_set, 2)
        pe.sem_inc(tl_set, 1)
        pe.sem_inc(ssq_set, 1)

        def step(i, s, live):
            if live[0]:
                pe.wait_ge(mt_in, i * 16 + 16)
                for j in range(J):
                    pe.wait_ge(r_set, i * J + (j + 1))
                    for k in range(KD):
                        mm = pe.transpose(ta[:, j % 2, k * P:(k + 1) * P], mt[:, k, j * P:(j + 1) * P], ident[:])
                    mm.then_inc(ta_set, 1)
            if live[2]:
                c = i - 2
                pe.wait_ge(xnt_set, c * KD + (KD + 2))
                pe.wait_ge(log_set, c + 2)
                for j in range(J):
                    for k in range(KD):
                        mm = pe.matmul(tl[:, j, :], xnt[:, s, k, j * P:(j + 1) * P], mu[:, k, :], start=k == 0, stop=k == KD - 1)
                mm.then_inc(tl_set, 1)
                pe.wait_ge(xsq_set, c + 1)
                for j in range(J):
                    for k in range(KD):
                        mm = pe.matmul(ssq[:, j:j + 1], xsq[:, k, j * P:(j + 1) * P], ones[:, 0:1], start=k == 0, stop=k == KD - 1)
                mm.then_inc(ssq_set, 1)
            if live[1]:
                c, s1 = i - 1, 1 - s
                pe.wait_ge(xh_set, c + 3)
                for k in range(KD):
                    pe.wait_ge(xnt_set, c * KD + (k + 1))
                    for j in range(J):
                        mm = pe.transpose(tb[:, k % 2, j * P:(j + 1) * P], xh[:, s1, j, k * P:(k + 1) * P], ident[:])
                    mm.then_inc(tb_set, 1)

        pipelined(pe, 2, step)


def moe_dispatch(nc, ctx, d, logits, run_top, slot_out):
    sb, ps, sem = makers(nc, ctx, "_d")
    ident = sb("ident", [P, P])
    zeros = sb("zeros", [P, P])
    ones = sb("ones", [P, 1])
    top = sb("top", [P, SLOTS])
    top_t = sb("top_t", [P, 2])
    top_b = sb("top_b", [P, 2, P])
    top_rep = sb("top_rep", [P, SLOTS])
    xh = sb("xh", [P, 2, J, D_MODEL])
    diff = sb("diff", [P, 2, J, SLOTS])
    e = sb("e", [P, 2, J, SLOTS])
    rden = sb("rden", [P, 2])
    slot_in = sb("slot_in", [P, 2, D_MODEL])
    slot_t = sb("slot_t", [P, KD, SLOTS])
    hidden = sb("hidden", [P, EXPERTS, P])
    gamma_t = sb("gamma_t", [P, KD])
    beta_t = sb("beta_t", [P, KD])
    w1 = sb("w1", [P, KD, EXPERTS, HID])
    w2 = sb("w2", [P, EXPERTS, D_MODEL])
    b1 = sb("b1", [P, EXPERTS])
    b2 = sb("b2", [P, 2, D_MODEL])
    sums = ps("sums", [P, 2, D_MODEL])
    den = ps("den", [P, 2, 512])
    turn = ps("turn", [P, 4, 512])
    per = SLOTS // EXPERTS
    half = EXPERTS // 2

    ident_set, const_set = sem("ident_set"), sem("const_set")
    w_in = sem("w_in")
    xh_in = [sem(f"xh_in{s}") for s in range(2)]
    top_set, top_turned, topb_set, top_rep_ps, top_rep_set = (sem(n) for n in ("top_set", "top_turned", "topb_set", "top_rep_ps", "top_rep_set"))
    diff_set, e_set, summed = sem("diff_set"), sem("e_set"), sem("summed")
    slot_set, slot_turned, slot_t_set, hid_ps, hid_set, out_ps, out_set = (
        sem(n) for n in ("slot_set", "slot_turned", "slot_t_set", "hid_ps", "hid_set", "out_ps", "out_set"))
    dve_step = sem("dve_step")
    block = ctx.enter_context(nc.Block())

    @block.gpsimd
    def _(pool):
        pool.memset(ones[:], 1.0)
        pool.memset(zeros[:], 0.0)
        pool.memset(hidden[:], 0.0).then_inc(const_set, 1)
        build_identity(pool, ident, ident_set)

    @block.sync
    def _(sp):
        for s in range(2):
            sp.dma_start(xh[:, s], d["xh"][s]).then_inc(xh_in[s], 16)
        sp.dma_start(w1[:], d["w1"]).then_inc(w_in, 16)
        sp.dma_start(w2[:], d["w2"]).then_inc(w_in, 16)
        sp.dma_start(b1[:], d["b1"]).then_inc(w_in, 16)
        sp.dma_start(gamma_t[:], d["gamma_t"]).then_inc(w_in, 16)
        sp.dma_start(beta_t[:], d["beta_t"]).then_inc(w_in, 16)
        for e8 in range(EXPERTS):
            p0 = (e8 % half) * per
            sp.dma_start(b2[p0:p0 + per, e8 // half, :], d["b2"][e8].partition_broadcast(per)).then_inc(w_in, 16)
        with sp.Fori(1, NC // 2) as pair:
            i = 2 * pair
            for s in range(2):
                sp.wait_ge(summed, i + (s + 1))
                sp.dma_start(xh[:, s], d["xh"][bass.ds(i + s, 1)].rearrange("a p j d -> (a p) j d")).then_inc(xh_in[s], 16)

    @block.vector
    def _(dve):
        chain = Chain(dve, dve_step, 0)
        dve.tensor_reduce(top[:], run_top[:].rearrange("p j s -> p s j"), AX_X, ALU.max).then_inc(top_set, 1)
        dve.wait_ge(top_turned, 1)
        for h in range(2):
            ins = dve.tensor_reduce(top_t[:, h:h + 1], turn[:, h, 0:P], AX_X, ALU.max)
        chain.link(ins)
        dve.wait_ge(const_set, 1)
        for h in range(2):
            ins = dve.tensor_scalar(top_b[:, h, :], zeros[:], top_t[:, h:h + 1], None, ALU.add)
        ins.then_inc(topb_set, 1)
        dve.wait_ge(top_rep_ps, 1)
        dve.tensor_copy(top_rep[:].rearrange("p (h s) -> p h s", h=2), turn[:, 2:4, 0:P]).then_inc(top_rep_set, 1)
        dve.wait_ge(top_rep_set, 1)
        dve.sem_inc(diff_set, 2)
        with dve.Fori(0, NC // 2) as pair:
            i = 2 * pair
            for s in range(2):
                c = i + s
                dve.wait_ge(e_set, c + 1)
                dve.tensor_tensor(diff[:, s], logits[:, bass.ds(c * J, J), :],
                                  top_rep[:].unsqueeze(1).to_broadcast([P, J, SLOTS]), ALU.subtract).then_inc(diff_set, 1)
        dve.wait_ge(summed, NC + 2)
        chain.link(dve.reciprocal(rden[:], den[:, :, 0]))
        for h in range(2):
            ins = dve.tensor_scalar(slot_in[:, h, :], sums[:, h, :], rden[:, h:h + 1], None, ALU.mult)
        ins.then_inc(slot_set, 1)
        dve.wait_ge(slot_turned, 1)
        dve.wait_ge(w_in, 16 * (5 + EXPERTS))
        for k in range(KD):
            ins = dve.tensor_scalar(slot_t[:, k, :], turn[:, k, 0:SLOTS], gamma_t[:, k:k + 1], beta_t[:, k:k + 1], ALU.mult, ALU.add)
        ins.then_inc(slot_t_set, 1)
        dve.wait_ge(out_ps, 1)
        dve.wait_ge(w_in, 16 * (5 + EXPERTS))
        dve.tensor_tensor(slot_out[:], turn[:, 2:4, :], b2[:], ALU.add).then_inc(out_set, 1)
        dve.wait_ge(out_set, 1)

    @block.scalar
    def _(act):
        act.sem_inc(e_set, 2)
        with act.Fori(0, NC // 2) as pair:
            i = 2 * pair
            for s in range(2):
                c = i + s
                act.wait_ge(diff_set, c + 3)
                act.wait_ge(summed, c + 1)
                act.activation(e[:, s], diff[:, s], ACT.Exp).then_inc(e_set, 1)
        act.wait_ge(hid_ps, 1)
        act.wait_ge(w_in, 16 * (5 + EXPERTS))
        act.wait_ge(const_set, 1)
        for x in range(EXPERTS):
            p0 = (x % half) * per
            ins = act.activation(hidden[:, x, p0:p0 + per], den[:, 1, x * per:(x + 1) * per], ACT.Gelu, bias=b1[:, x:x + 1])
        ins.then_inc(hid_set, 1)

    @block.tensor
    def _(pe):
        pe.wait_ge(ident_set, 2)
        pe.wait_ge(top_set, 1)
        for h in range(2):
            mm = pe.transpose(turn[:, h, 0:P], top[:, h * P:(h + 1) * P], ident[:])
        mm.then_inc(top_turned, 1)
        pe.wait_ge(topb_set, 1)
        for h in range(2):
            mm = pe.transpose(turn[:, 2 + h, 0:P], top_b[:, h, :], ident[:])
        mm.then_inc(top_rep_ps, 1)
        pe.wait_ge(const_set, 1)
        pe.sem_inc(summed, 2)
        for h in range(2):
            pe.matmul(sums[:, h, 0:P], zeros[:], ident[:], start=True, stop=False, skip_group_check=True)
            for k in range(1, KD):
                pe.matmul(sums[:, h, k * P:(k + 1) * P], zeros[:], ident[:], start=False, stop=False, skip_group_check=True)
            pe.matmul(den[:, h, 0:1], zeros[:], ones[:], start=True, stop=False, skip_group_check=True)
        with pe.Fori(0, NC // 2) as pair:
            i = 2 * pair
            for s in range(2):
                c = i + s
                pe.wait_ge(e_set, c + 3)
                pe.wait_ge(xh_in[s], i * 8 + 16)
                for j in range(J):
                    for h in range(2):
                        pe.matmul(sums[:, h, :], e[:, s, j, h * P:(h + 1) * P], xh[:, s, j, :], start=False, stop=False, skip_group_check=True)
                        mm = pe.matmul(den[:, h, 0:1], e[:, s, j, h * P:(h + 1) * P], ones[:], start=False, stop=False, skip_group_check=True)
                mm.then_inc(summed, 1)
        pe.wait_ge(slot_set, 1)
        for k in range(KD):
            for h in range(2):
                mm = pe.transpose(turn[:, k, h * P:(h + 1) * P], slot_in[:, h, k * P:(k + 1) * P], ident[:])
        mm.then_inc(slot_turned, 1)
        pe.wait_ge(slot_t_set, 1)
        pe.wait_ge(w_in, 16 * (5 + EXPERTS))
        for x in range(EXPERTS):
            for k in range(KD):
                mm = pe.matmul(den[:, 1, x * per:(x + 1) * per], w1[:, k, x, :], slot_t[:, k, x * per:(x + 1) * per],
                               start=k == 0, stop=k == KD - 1)
        mm.then_inc(hid_ps, 1)
        pe.wait_ge(hid_set, 1)
        for x in range(EXPERTS):
            mm = pe.matmul(turn[:, 2 + x // half, :], hidden[:, x, :], w2[:, x, :], start=x % half == 0, stop=x % half == half - 1)
        mm.then_inc(out_ps, 1)


def moe_combine(nc, ctx, d, logits, slot_out):
    sb, ps, sem = makers(nc, ctx, "_c")
    ident = sb("ident", [P, P])
    x1 = sb("x1", [P, 2, J, D_MODEL])
    neg_top = sb("neg_top", [P, 2, J])
    e = sb("e", [P, 2, J, SLOTS])
    et = sb("et", [P, 2, 2, T])
    den = sb("den", [P, NC * J])
    rden = sb("rden", [P, J])
    stats = sb("stats", [P, J, 6])
    spare = sb("spare", [P, 1])
    mv = sb("mv", [P, J, 2])
    var = sb("var", [P, J])
    eps = sb("eps", [P, 1])
    sd = sb("sd", [P, J])
    mul, add = sb("mul", [P, J]), sb("add", [P, J])
    y = sb("y", [P, 2, J, D_MODEL])
    turn = ps("turn", [P, 2, T])
    mix = ps("mix", [P, J, D_MODEL])

    ident_set, eps_set = sem("ident_set"), sem("eps_set")
    x1_in = [sem(f"x1_in{s}") for s in range(2)]
    stored = [sem(f"stored{s}") for s in range(2)]
    top_set, e_set, turned, et_set, mixed, coef_set, y_set, sum_set = (
        sem(n) for n in ("top_set", "e_set", "turned", "et_set", "mixed", "coef_set", "y_set", "sum_set"))
    var_set, sd_set = sem("var_set"), sem("sd_set")
    var_step = [sem(f"var_step{hf}") for hf in range(2)]
    mul_step = [sem(f"mul_step{hf}") for hf in range(2)]
    block = ctx.enter_context(nc.Block())
    H = J // 2

    @block.gpsimd
    def _(pool):
        pool.memset(eps[:], LN_EPS).then_inc(eps_set, 1)
        build_identity(pool, ident, ident_set)
        pool.sem_inc(sum_set, 2)
        with pool.Fori(0, NC // 2) as pair:
            i = 2 * pair
            for s in range(2):
                pool.wait_ge(x1_in[s], i * 8 + 16)
                for hf in range(2):
                    js = slice(hf * H, hf * H + H)
                    pool.wait_ge(y_set, i * 2 + (2 * s + hf + 3))
                    ins = pool.tensor_tensor(y[:, s, js], y[:, s, js], x1[:, s, js], ALU.add)
                ins.then_inc(sum_set, 1)

    @block.sync
    def _(sp):
        for s in range(2):
            sp.sem_inc(stored[s], 16)
            sp.dma_start(x1[:, s], d["x1"][s]).then_inc(x1_in[s], 16)
        with sp.Fori(0, NC // 2 - 1) as pair:
            i = 2 * pair
            for s in range(2):
                sp.wait_ge(sum_set, i + (s + 3))
                sp.dma_start(d["out"][bass.ds(i + s, 1)].rearrange("a j p d -> p (a j) d"), y[:, s]).then_inc(stored[s], 16)
                sp.dma_start(x1[:, s], d["x1"][bass.ds(i + (s + 2), 1)].rearrange("a p j d -> (a p) j d")).then_inc(x1_in[s], 16)
        for s in range(2):
            sp.wait_ge(sum_set, NC + s + 1)
            sp.dma_start(d["out"][NC - 2 + s].rearrange("j p d -> p j d"), y[:, s]).then_inc(stored[s], 16)
        for s in range(2):
            sp.wait_ge(stored[s], 16 + NC * 8)

    @block.vector
    def _(dve):
        dve.sem_inc(coef_set, 2)
        dve.sem_inc(et_set, 2)
        dve.sem_inc(top_set, 2)

        def tops(c, s):
            dve.wait_ge(e_set, c + 1)
            dve.tensor_reduce(neg_top[:, s], logits[:, bass.ds(c * J, J), :], AX_X, ALU.max, negate=True).then_inc(top_set, 1)

        def variance(c, hf):
            js = slice(hf * H, hf * H + H)
            chain = Chain(dve, var_step[hf], c * 4)
            dve.wait_ge(mixed, c * 2 + (hf + 3))
            dve.wait_ge(coef_set, c * 2 + (hf + 1))
            chain.link(moments(dve, chain, stats, mv, mix, spare, range(hf * H, hf * H + H)))
            chain.link(dve.reciprocal(rden[:, js], den[:, bass.ds(c * J + hf * H, H)]))
            chain.link(dve.tensor_tensor(var[:, js], mv[:, js, 1], rden[:, js], ALU.mult))
            dve.tensor_tensor(var[:, js], var[:, js], rden[:, js], ALU.mult).then_inc(var_set, 1)

        def coefficients(c, hf):
            js = slice(hf * H, hf * H + H)
            chain = Chain(dve, mul_step[hf], c * 2)
            dve.wait_ge(sd_set, c * 2 + (hf + 1))
            chain.link(dve.reciprocal(mul[:, js], sd[:, js]))
            chain.link(dve.tensor_tensor(mul[:, js], mul[:, js], rden[:, js], ALU.mult))
            dve.scalar_tensor_tensor(add[:, js], mv[:, js, 0], -1.0, mul[:, js], ALU.mult, ALU.mult).then_inc(coef_set, 1)

        tops(0, 0)

        def step(i, s, live):
            if live[2]:
                variance(i - 2, 0)
                coefficients(i - 2, 0)
                variance(i - 2, 1)
            if live[0] and not (isinstance(i, int) and i == NC - 1):
                tops(i + 1, 1 - s)
            if live[2]:
                coefficients(i - 2, 1)
            if live[0]:
                dve.wait_ge(turned, i + 3)
                if live[2]:
                    dve.wait_ge(mixed, i * 2)
                dve.tensor_copy(et[:, s], turn[:]).then_inc(et_set, 1)

        pipelined(dve, 2, step, ahead=1)

    @block.scalar
    def _(act):
        act.sem_inc(e_set, 2)
        act.sem_inc(y_set, 2)

        act.wait_ge(eps_set, 1)

        def norm(c, s1, hf):
            js = slice(hf * H, hf * H + H)
            act.wait_ge(var_set, c * 2 + (hf + 1))
            act.activation(sd[:, js], var[:, js], ACT.Sqrt, bias=eps[:]).then_inc(sd_set, 1)
            act.wait_ge(coef_set, c * 2 + (hf + 3))
            for j in range(hf * H, hf * H + H):
                ins = act.activation(y[:, s1, j, :], mix[:, j, :], ACT.Identity, scale=mul[:, j:j + 1], bias=add[:, j:j + 1])
            ins.then_inc(y_set, 1)

        def step(i, s, live):
            if live[0]:
                act.wait_ge(top_set, i + 3)
                act.wait_ge(turned, i + 1)
                for j in range(J):
                    ins = act.activation(e[:, s, j, :], logits[:, bass.ds(i * J + j, 1), :].rearrange("p a s -> p (a s)"),
                                         ACT.Exp, bias=neg_top[:, s, j:j + 1], accum_out=den[:, bass.ds(i * J + j, 1)])
                ins.then_inc(e_set, 1)
            if live[2]:
                act.wait_ge(stored[s], (i - 2 - s) * 8 + 16)
                norm(i - 2, s, 0)
                norm(i - 2, s, 1)

        pipelined(act, 2, step)

    @block.tensor
    def _(pe):
        pe.wait_ge(ident_set, 2)
        pe.sem_inc(turned, 2)
        pe.sem_inc(mixed, 2)

        def mix_half(c, s1, hf):
            pe.wait_ge(et_set, c + 3)
            pe.wait_ge(y_set, c * 2 + (hf + 1))
            for j in range(hf * H, hf * H + H):
                for h in range(2):
                    mm = pe.matmul(mix[:, j, :], et[:, s1, h, j * P:(j + 1) * P], slot_out[:, h, :], start=h == 0, stop=h == 1)
            mm.then_inc(mixed, 1)

        def step(i, s, live):
            if live[2]:
                mix_half(i - 2, s, 0)
                mix_half(i - 2, s, 1)
            if live[0]:
                pe.wait_ge(e_set, i + 3)
                pe.wait_ge(et_set, i + 2)
                for j in range(J):
                    for h in range(2):
                        mm = pe.transpose(turn[:, h, j * P:(j + 1) * P], e[:, s, j, h * P:(h + 1) * P], ident[:])
                mm.then_inc(turned, 1)
        pipelined(pe, 2, step)


def build(nc, x, in_w, par, x_w, dt_w, out_w, mu, gamma_t, beta_t, scale, w1, b1, w2, b2, out):
    d = {"x": x.rearrange("(c j p) d -> c j p d", j=J, p=P), "out": out.rearrange("(c j p) d -> c j p d", j=J, p=P),
         "w_in": in_w, "par": par, "w_x": x_w, "w_dt": dt_w, "w_out": out_w,
         "mu": mu, "gamma_t": gamma_t, "beta_t": beta_t, "scale": scale, "w1": w1, "b1": b1, "w2": w2, "b2": b2}
    for name, shape in (("xt", [(LAYERS + 1) * NC, P, KD, T]), ("b_rows", [LAYERS * NC, STATES, T]),
                        ("x1", [NC, P, J, D_MODEL]), ("xh", [NC, P, J, D_MODEL])):
        d[name] = nc.dram_tensor(name, shape, F32, kind="Internal").ap()
    with ExitStack() as whole:
        rstd = whole.enter_context(nc.sbuf_tensor("rstd_x", [P, NC * J], F32))
        nmr = whole.enter_context(nc.sbuf_tensor("nmr_x", [P, NC * J], F32))
        with ExitStack() as ctx:
            norm_input(nc, ctx, d, rstd, nmr)
        with ExitStack() as ctx:
            mamba_stack(nc, ctx, d)
        logits = whole.enter_context(nc.sbuf_tensor("logits", [P, NC * J, SLOTS], F32))
        run_top = whole.enter_context(nc.sbuf_tensor("run_top", [P, J, SLOTS], F32))
        slot_out = whole.enter_context(nc.sbuf_tensor("slot_out", [P, 2, D_MODEL], F32))
        with ExitStack() as ctx:
            moe_logits(nc, ctx, d, rstd, nmr, logits, run_top)
        with ExitStack() as ctx:
            moe_dispatch(nc, ctx, d, logits, run_top, slot_out)
        with ExitStack() as ctx:
            moe_combine(nc, ctx, d, logits, slot_out)


def kernel(**inputs):
    import numpy as _np
    import concourse.bacc as _bacc
    from concourse import mybir as _mybir
    from concourse.bass_utils import run_bass_kernel_spmd as _run

    a = {name.split("_", 1)[1]: _np.asarray(v) for name, v in inputs.items()}

    def rows_in(m, blocks):
        return m.transpose(0, 2, 1).reshape(LAYERS, blocks, P, m.shape[1]).transpose(0, 2, 1, 3)

    def per_channel(m):
        return m.reshape(LAYERS, NB, P, -1)

    par = _np.concatenate([per_channel(a["attn_" + n]) for n in ("A_log", "conv_w", "conv_b", "dt_proj_b", "D")], axis=-1)
    arrays = {
        "x": a["attn_x"].reshape(SEQ, D_MODEL),
        "in_w": rows_in(a["attn_in_proj_w"], KD),
        "par": par.transpose(0, 2, 3, 1),
        "x_w": rows_in(a["attn_x_proj_w"], NB),
        "dt_w": a["attn_dt_proj_w"].transpose(0, 2, 1),
        "out_w": rows_in(a["attn_out_proj_w"], NB),
        "mu": a["ffn_mu"].reshape(KD, P, SLOTS).transpose(1, 0, 2),
        "gamma_t": a["ffn_ln_gamma"].reshape(KD, P).T,
        "beta_t": a["ffn_ln_beta"].reshape(KD, P).T,
        "scale": a["ffn_scale"],
        "w1": a["ffn_w1"].reshape(EXPERTS, KD, P, HID).transpose(2, 1, 0, 3),
        "b1": a["ffn_b1"].transpose(1, 0),
        "w2": a["ffn_w2"].transpose(1, 0, 2),
        "b2": a["ffn_b2"],
    }
    nc = _bacc.Bacc("TRN2", target_bir_lowering=False, num_devices=1, dynamic_dma_scratch_size=256)
    ins, args = {}, []
    for name, v in arrays.items():
        v = _np.ascontiguousarray(v)
        ins[f"in_{name}_dram"] = v
        args.append(nc.dram_tensor(f"in_{name}_dram", v.shape, _mybir.dt.from_np(v.dtype), kind="ExternalInput").ap())
    args.append(nc.dram_tensor("out_0_dram", (SEQ, D_MODEL), F32, kind="ExternalOutput").ap())
    build(nc, *args)
    r = _run(nc, [ins], core_ids=[0])
    return r.results[0]["out_0_dram"].reshape(1, SEQ, D_MODEL)
```
